# Optimizing a Trainium2 kernel written in Bass

```python
import numpy as np
import jax
import jax.numpy as jnp

def _softmax(x, axis=-1):
    return jax.nn.softmax(x, axis=axis)

def _gelu(x):
    return jax.nn.gelu(x, approximate=True)

def _silu(x):
    return jax.nn.silu(x)

def _sigmoid(x):
    return jax.nn.sigmoid(x)

def _layernorm(x, axis=-1, eps=1e-05):
    m = jnp.mean(x, axis=axis, keepdims=True)
    v = jnp.var(x, axis=axis, keepdims=True)
    return (x - m) / jnp.sqrt(v + eps)

def _scatter_add(tgt, idx, src, axis=0):
    return tgt.at[idx].add(src)

def _segment_sum(src, seg, n):
    return jax.ops.segment_sum(src, seg, n)
kernel_name = 'mk_conv_attn_hybrid_d2_conv_nchw768_r4_b6fe8a'

def setup_inputs(seed: int=0):
    np.random.seed(seed)
    _w = jnp.asarray

    def _rec_inputs():
        import jax
        import jax.numpy as jnp
        _gk = jax.random.key(seed)
        x = -0.0004039 + 1 * jax.random.normal(jax.random.fold_in(_gk, 1), (4, 192, 16, 16), jnp.float32)
        return x
    x = _rec_inputs()

    def _L0_conv_setup():
        import jax, jax.numpy as jnp
        import numpy as np
        HIDDEN_SIZE = 192
        NUM_BLOCKS = 8
        BLOCK_SIZE = HIDDEN_SIZE // NUM_BLOCKS
        HSF = 1
        SPARSITY = 0.01
        HARD_FRAC = 1.0
        SCALE = 0.02

        def softshrink(v, lam):
            return jnp.sign(v) * jnp.maximum(jnp.abs(v) - lam, 0.0)
        key = jax.random.key(seed)
        k0, k1, k2, k3, k4 = jax.random.split(key, 5)
        B, C, H, W = (4, HIDDEN_SIZE, 16, 16)
        x = jax.random.normal(k0, (B, C, H, W), dtype=jnp.float32)
        w1 = SCALE * jax.random.normal(k1, (2, NUM_BLOCKS, BLOCK_SIZE, BLOCK_SIZE * HSF), dtype=jnp.float32)
        b1 = SCALE * jax.random.normal(k2, (2, NUM_BLOCKS, BLOCK_SIZE * HSF), dtype=jnp.float32)
        w2 = SCALE * jax.random.normal(k3, (2, NUM_BLOCKS, BLOCK_SIZE * HSF, BLOCK_SIZE), dtype=jnp.float32)
        b2 = SCALE * jax.random.normal(k4, (2, NUM_BLOCKS, BLOCK_SIZE), dtype=jnp.float32)
        return {'x': x, 'w1': w1, 'b1': b1, 'w2': w2, 'b2': b2}
    _L0_conv_all = _L0_conv_setup()
    _L0_conv_in = {k: v for k, v in _L0_conv_all.items() if k in ('w1', 'b1', 'w2', 'b2')}
    del _L0_conv_all

    def _L1_attn_setup():
        import jax, jax.numpy as jnp
        import numpy as np
        B, N, D, H = (8, 256, 192, 12)
        HD = D // H
        SCALE = HD ** (-0.5)
        key = jax.random.key(seed)
        k1, k2, k3 = jax.random.split(key, 3)
        x = jax.random.normal(k1, (B, N, D), dtype=jnp.float32)
        w_qkv = jax.random.normal(k2, (D, 3 * D), dtype=jnp.float32) * D ** (-0.5)
        b_qkv = jnp.zeros((3 * D,), dtype=jnp.float32)
        w_proj = jax.random.normal(k3, (D, D), dtype=jnp.float32) * D ** (-0.5)
        b_proj = jnp.zeros((D,), dtype=jnp.float32)
        return {'x': x, 'w_qkv': w_qkv, 'b_qkv': b_qkv, 'w_proj': w_proj, 'b_proj': b_proj}
    _L1_attn_all = _L1_attn_setup()
    _L1_attn_in = {k: v for k, v in _L1_attn_all.items() if k in ('w_qkv', 'b_qkv', 'w_proj', 'b_proj')}
    del _L1_attn_all

    def _L1_ffn_setup():
        import jax, jax.numpy as jnp
        import numpy as np
        E = 16
        TOP_K = 2
        C = 192
        I = 384
        B, T = (8, 512)

        def _expert(x, wg_e, wu_e, wd_e):
            return jax.nn.silu(x @ wg_e) * (x @ wu_e) @ wd_e
        key = jax.random.key(seed)
        ks = jax.random.split(key, 9)
        s = 0.02
        return {'x': jax.random.normal(ks[0], (B, T, C), jnp.float32), 'w_gate': jax.random.normal(ks[1], (C, E), jnp.float32) * s, 'expert_bias': jnp.zeros((E,), jnp.float32), 'wg': jax.random.normal(ks[2], (E, C, I), jnp.float32) * s, 'wu': jax.random.normal(ks[3], (E, C, I), jnp.float32) * s, 'wd': jax.random.normal(ks[4], (E, I, C), jnp.float32) * s, 'swg': jax.random.normal(ks[5], (C, I), jnp.float32) * s, 'swu': jax.random.normal(ks[6], (C, I), jnp.float32) * s, 'swd': jax.random.normal(ks[7], (I, C), jnp.float32) * s}
    _L1_ffn_all = _L1_ffn_setup()
    _L1_ffn_in = {k: v for k, v in _L1_ffn_all.items() if k in ('w_gate', 'expert_bias', 'wg', 'wu', 'wd', 'swg', 'swu', 'swd')}
    del _L1_ffn_all
    return {'x': x, 'L0_conv_w1': _L0_conv_in['w1'], 'L0_conv_b1': _L0_conv_in['b1'], 'L0_conv_w2': _L0_conv_in['w2'], 'L0_conv_b2': _L0_conv_in['b2'], 'L1_attn_w_qkv': _L1_attn_in['w_qkv'], 'L1_attn_b_qkv': _L1_attn_in['b_qkv'], 'L1_attn_w_proj': _L1_attn_in['w_proj'], 'L1_attn_b_proj': _L1_attn_in['b_proj'], 'L1_ffn_w_gate': _L1_ffn_in['w_gate'], 'L1_ffn_expert_bias': _L1_ffn_in['expert_bias'], 'L1_ffn_wg': _L1_ffn_in['wg'], 'L1_ffn_wu': _L1_ffn_in['wu'], 'L1_ffn_wd': _L1_ffn_in['wd'], 'L1_ffn_swg': _L1_ffn_in['swg'], 'L1_ffn_swu': _L1_ffn_in['swu'], 'L1_ffn_swd': _L1_ffn_in['swd']}

def reference(x, L0_conv_w1, L0_conv_b1, L0_conv_w2, L0_conv_b2, L1_attn_w_qkv, L1_attn_b_qkv, L1_attn_w_proj, L1_attn_b_proj, L1_ffn_w_gate, L1_ffn_expert_bias, L1_ffn_wg, L1_ffn_wu, L1_ffn_wd, L1_ffn_swg, L1_ffn_swu, L1_ffn_swd):
    import jax
    import jax.numpy as jnp

    def _L0_conv_ref(x, w1, b1, w2, b2):
        import jax, jax.numpy as jnp
        import numpy as np
        HIDDEN_SIZE = 192
        NUM_BLOCKS = 8
        BLOCK_SIZE = HIDDEN_SIZE // NUM_BLOCKS
        HSF = 1
        SPARSITY = 0.01
        HARD_FRAC = 1.0
        SCALE = 0.02

        def softshrink(v, lam):
            return jnp.sign(v) * jnp.maximum(jnp.abs(v) - lam, 0.0)
        B, C, H, W = x.shape
        nb, bs = (w1.shape[1], w1.shape[2])
        bias = x
        xr = x.reshape(B, H, W, C)
        Xf = jnp.fft.fft2(xr, axes=(1, 2), norm='ortho')
        Xf = Xf.reshape(B, H, W, nb, bs)
        total_modes = H * W // 2 + 1
        kept = min(int(total_modes * HARD_FRAC), W)
        xk = Xf[:, :, :kept]
        xr_, xi_ = (xk.real, xk.imag)
        o1r = jax.nn.relu(jnp.einsum('bhwni,nio->bhwno', xr_, w1[0]) - jnp.einsum('bhwni,nio->bhwno', xi_, w1[1]) + b1[0])
        o1i = jax.nn.relu(jnp.einsum('bhwni,nio->bhwno', xi_, w1[0]) + jnp.einsum('bhwni,nio->bhwno', xr_, w1[1]) + b1[1])
        o2r = jnp.einsum('bhwno,noi->bhwni', o1r, w2[0]) - jnp.einsum('bhwno,noi->bhwni', o1i, w2[1]) + b2[0]
        o2i = jnp.einsum('bhwno,noi->bhwni', o1i, w2[0]) + jnp.einsum('bhwno,noi->bhwni', o1r, w2[1]) + b2[1]
        o2r = softshrink(o2r, SPARSITY)
        o2i = softshrink(o2i, SPARSITY)
        if kept < W:
            pad = [(0, 0), (0, 0), (0, W - kept), (0, 0), (0, 0)]
            o2r = jnp.pad(o2r, pad)
            o2i = jnp.pad(o2i, pad)
        y = (o2r + 1j * o2i).reshape(B, H, W, C)
        out = jnp.fft.irfft2(y, s=(H, W), axes=(1, 2), norm='ortho')
        out = out.reshape(B, C, H, W)
        return out + bias

    def _L1_attn_ref(x, w_qkv, b_qkv, w_proj, b_proj):
        import jax, jax.numpy as jnp
        import numpy as np
        B, N, D, H = (8, 256, 192, 12)
        HD = D // H
        SCALE = HD ** (-0.5)
        bsz, n, d = x.shape
        qkv = x @ w_qkv + b_qkv
        qkv = qkv.reshape(bsz, n, 3, H, HD)
        qkv = jnp.transpose(qkv, (2, 0, 3, 1, 4))
        q, k, v = (qkv[0], qkv[1], qkv[2])
        attn = jnp.einsum('bhqd,bhkd->bhqk', q, k) * SCALE
        attn = jax.nn.softmax(attn, axis=-1)
        out = jnp.einsum('bhqk,bhkd->bhqd', attn, v)
        out = jnp.transpose(out, (0, 2, 1, 3)).reshape(bsz, n, d)
        return out @ w_proj + b_proj

    def _L1_ffn_ref(x, w_gate, expert_bias, wg, wu, wd, swg, swu, swd):
        import jax, jax.numpy as jnp
        import numpy as np
        E = 16
        TOP_K = 2
        C = 192
        I = 384
        B, T = (8, 512)

        def _expert(x, wg_e, wu_e, wd_e):
            return jax.nn.silu(x @ wg_e) * (x @ wu_e) @ wd_e
        Bq, Tq, Cq = x.shape
        xf = x.reshape(-1, Cq)
        n_tok = xf.shape[0]
        shared = _expert(xf, swg, swu, swd)
        logits = xf @ w_gate + expert_bias
        probs = jax.nn.softmax(logits, axis=-1)
        topk_p, topk_i = jax.lax.top_k(probs, TOP_K)
        topk_p = topk_p / jnp.sum(topk_p, axis=-1, keepdims=True)
        comb = jnp.zeros((n_tok, E), xf.dtype).at[jnp.arange(n_tok)[:, None], topk_i].add(topk_p)
        routed = jnp.zeros_like(xf)
        for e in range(E):
            routed = routed + comb[:, e:e + 1] * _expert(xf, wg[e], wu[e], wd[e])
        return (shared + routed).reshape(Bq, Tq, Cq)

    def _gn(v, G=32, eps=1e-05):
        B_, C_, H_, W_ = v.shape
        g = v.reshape(B_, G, C_ // G, H_, W_)
        m = jnp.mean(g, axis=(2, 3, 4), keepdims=True)
        s = jnp.var(g, axis=(2, 3, 4), keepdims=True)
        return ((g - m) / jnp.sqrt(s + eps)).reshape(v.shape)

    def _ln_c(v, eps=1e-06):
        m = jnp.mean(v, axis=1, keepdims=True)
        s = jnp.var(v, axis=1, keepdims=True)
        return (v - m) / jnp.sqrt(s + eps)

    def _ln_t(v, eps=1e-05):
        m = jnp.mean(v, axis=-1, keepdims=True)
        s = jnp.var(v, axis=-1, keepdims=True)
        return (v - m) / jnp.sqrt(s + eps)

    def _to_tokens(v):
        B_, C_, H_, W_ = v.shape
        return v.reshape(B_, C_, H_ * W_).transpose(0, 2, 1)

    def _from_tokens(t, like):
        B_, C_, H_, W_ = like.shape
        return t.transpose(0, 2, 1).reshape(B_, C_, H_, W_)
    x = _L0_conv_ref(x, L0_conv_w1, L0_conv_b1, L0_conv_w2, L0_conv_b2)
    t = _to_tokens(x)
    t = t + _L1_attn_ref(_ln_t(t), L1_attn_w_qkv, L1_attn_b_qkv, L1_attn_w_proj, L1_attn_b_proj)
    t = t + _L1_ffn_ref(_ln_t(t), L1_ffn_w_gate, L1_ffn_expert_bias, L1_ffn_wg, L1_ffn_wu, L1_ffn_wd, L1_ffn_swg, L1_ffn_swu, L1_ffn_swd)
    x = _from_tokens(t, x)
    return x

_drawn_inputs = setup_inputs


def setup_inputs(seed=0):
    import zlib

    import numpy as np

    out = dict(_drawn_inputs(seed))
    spreads = {'L1_attn_b_qkv': (0.0, 0.1),
     'L1_attn_b_proj': (0.0, 0.1),
     'L1_ffn_expert_bias': (0.0, 0.8)}
    factors = {'L0_conv_w1': 7.009,
     'L0_conv_b1': 8.0,
     'L0_conv_w2': 5.831,
     'L0_conv_b2': 3.006,
     'L1_ffn_w_gate': 5.732,
     'L1_ffn_wg': 5.263,
     'L1_ffn_wu': 5.226,
     'L1_ffn_wd': 5.225,
     'L1_ffn_swg': 3.755,
     'L1_ffn_swu': 3.71,
     'L1_ffn_swd': 3.736}
    for name, (base, spread) in spreads.items():
        noise = np.random.default_rng([zlib.crc32(name.encode()), seed]).standard_normal(out[name].shape)
        drawn = base * np.exp(spread * noise) if base else spread * noise
        out[name] = jnp.asarray(drawn.astype(out[name].dtype))
    for name, factor in factors.items():
        out[name] = (out[name] * factor).astype(out[name].dtype)
    return out
```

```python
from contextlib import ExitStack

import numpy as np
import concourse.bass as bass
from concourse import mybir

F32 = mybir.dt.float32
BF16 = mybir.dt.bfloat16
F16 = mybir.dt.float16
I32 = mybir.dt.int32
U32 = mybir.dt.uint32
ALU = mybir.AluOpType
ACT = mybir.ActivationFunctionType
AX = mybir.AxisListType

B, C, H, W = 4, 192, 16, 16
N = H * W
TOK = B * N
NT = TOK // 128
CH = C // 2
WF = W // 2 + 1
MODES = H * WF
MA = 80
MB = MODES - MA
BLK = 24
BPH = CH // BLK
LAMBDA = 0.01
HEADS, HD = 12, 16
SCALE = HD ** -0.5
E, TOPK, FF = 16, 2, 384
FC = FF // 128
TILE = 128
TILES = (TOK * TOPK + E * (TILE - 1)) // TILE
SLOTS = TILES * TILE
GU = 2 * 2 * FF
DN = FC * C
EXTRA = 11300
LATE = 6
EPS = 1e-5
MEMBER_STEP = 6 + 2 * NT + 3


def constants():
    h, w = np.meshgrid(np.arange(H), np.arange(W), indexing="ij")
    k1, k2 = np.meshgrid(np.arange(H), np.arange(WF), indexing="ij")
    turn = (np.outer(h.ravel(), k1.ravel()) % H) / H + (np.outer(w.ravel(), k2.ravel()) % W) / W
    angle = 2 * np.pi * turn
    forward = np.concatenate([np.cos(angle), -np.sin(angle)], 1) / np.sqrt(N)
    twice = np.where((k2.ravel() == 0) | (k2.ravel() == W // 2), 1.0, 2.0)[:, None]
    real, imag = twice * np.cos(angle).T / np.sqrt(N), -twice * np.sin(angle).T / np.sqrt(N)
    order = np.arange(N).reshape(N // 4, 4).T.ravel()
    inverse = np.zeros((128, 3, N))
    inverse[:MA, 0], inverse[:MA, 2] = real[:MA, order], imag[:MA, order]
    inverse[:MB, 1], inverse[64:64 + MB, 1] = real[MA:, order], imag[MA:, order]
    p = np.arange(128)
    r = p % 32
    even, odd = (r < HD).astype(float), (r >= HD).astype(float)
    masks = np.stack([even * SCALE, odd * SCALE, even, odd, (r == HD) * 1.0, (r == 0) * 1.0], 1)
    f = np.concatenate([
        np.eye(128),
        np.tile(np.arange(128), (128, 1)),
        forward.reshape(2, 128, 2 * MODES).transpose(1, 0, 2).reshape(128, -1),
        inverse.reshape(128, -1),
        p[:, None] + 128 * np.repeat(np.arange(NT), TOPK)[None, :],
        masks,
        np.tile(128 * np.arange(32), (128, 1)),
    ], 1).astype(np.float32)
    before = (p[:, None] < p[None, :]) * 1.0
    upto = (p[:, None] <= p[None, :]) * 1.0
    g = np.concatenate([before, np.ones((128, 128)), upto[:, :E]], 1)
    return f, g.astype(mybir.dt.np(BF16))


F_IDENT = 0
F_IOTA = 128
F_FWD = 256
F_INV = F_FWD + 2 * 2 * MODES
F_TOKEN = F_INV + 3 * N
F_MASK = F_TOKEN + NT * TOPK
F_TILE0 = F_MASK + 6
F_ALL = F_TILE0 + 32


def program(nc, a, out):
    ctx = ExitStack()
    with ctx:
        def sb(name, shape, dt=F32):
            return ctx.enter_context(nc.sbuf_tensor(name, shape, dt))

        def sem(name):
            return ctx.enter_context(nc.semaphore(name))

        xhat_rows = nc.dram_tensor("xhat_rows", [TOK, C], F32).ap()
        slot_rows = nc.dram_tensor("slot_rows", [SLOTS, C], F32).ap()

        cf = sb("cf", [128, F_ALL])
        cb = sb("cb", [128, 256 + E], BF16)
        ident = cf[:, F_IDENT:F_IDENT + 128]
        iota = cf[:, F_IOTA:F_IOTA + 128]
        fwd = cf[:, F_FWD:F_INV].rearrange("p (k m) -> p k m", k=2)
        inv = cf[:, F_INV:F_TOKEN].rearrange("p (k n) -> p k n", k=3)
        token_id = cf[:, F_TOKEN:F_MASK]
        mask = cf[:, F_MASK:F_TILE0]
        tile_start = cf[0:E, F_TILE0:F_ALL]
        before, ones, upto = cb[:, 0:128], cb[:, 128:256], cb[0:E, 256:256 + E]

        down_all = sb("down_all", [128, E * DN])
        shared_gu = sb("shared_gu", [128, GU])
        shared_dn = sb("shared_dn", [128, DN])
        tok = sb("tok", [128, NT, C])
        tok_b = sb("tok_b", [128, NT, C])
        main = sb("main", [128, E * GU + EXTRA])
        at = [(E - LATE) * GU]

        def carve(cols, start=None):
            at[0] = (at[0] if start is None else start) + cols
            assert at[0] <= E * GU + EXTRA, at[0]
            return main[:, at[0] - cols:at[0]]

        pix = carve(B * 2 * C, (E - LATE) * GU).rearrange("p (b k c) -> p b k c", b=B, k=2)
        x_res = carve(2 * 768).rearrange("p (q f) -> p q f", q=2)
        spec = carve(4 * B * MODES).rearrange("p (g r m) -> p g r m", g=2, r=2)
        hid = carve(4 * B * MODES).rearrange("p (g r m) -> p g r m", g=2, r=2)
        y = carve(B * 3 * C).rearrange("p (b k c) -> p b k c", b=B, k=3)
        w1 = carve(6 * CH).rearrange("p (g s o) -> p g s o", g=2, s=3)
        w2 = carve(6 * CH).rearrange("p (g s o) -> p g s o", g=2, s=3)
        b1 = carve(4).rearrange("p (g r) -> p g r", g=2)
        b2 = carve(3 * C).rearrange("p (k c) -> p k c", k=3)
        img = carve(2 * 768).rearrange("p (q f) -> p q f", q=2)
        biased = carve(2 * 2 * C).rearrange("p (s b c) -> p s b c", s=2, b=2)
        clipped = carve(2 * 2 * C).rearrange("p (s b c) -> p s b c", s=2, b=2)
        spectral_end = at[0]
        wgate = sb("wgate", [128, 2, E])
        xT = carve(B * 2 * N, (E - LATE) * GU).rearrange("p (b k n) -> p b k n", b=B, k=2)
        xhat = carve(NT * C).rearrange("p (t c) -> p t c", t=NT)
        q_sb = carve(2 * 4 * N).rearrange("p (s v t n) -> p s v t n", s=2, v=2, t=2)
        k_sb = carve(2 * 4 * N).rearrange("p (s v t n) -> p s v t n", s=2, v=2, t=2)
        negmax = carve(2 * 4 * CH).rearrange("p (s f) -> p s f", s=2)
        v_sb = carve(2 * 2 * HEADS * 32).rearrange("p (s k h d) -> p s k h d", s=2, k=2, h=HEADS)
        probs = carve(2 * 8 * N).rearrange("p (s k h n) -> p s k h n", s=2, k=2, h=4)
        o_sb = carve(2 * 3 * N).rearrange("p (s j n) -> p s j n", s=2, j=3)
        recip = carve(2 * N).rearrange("p (s n) -> p s n", s=2)
        den = carve(2 * N).rearrange("p (s n) -> p s n", s=2)
        stats = carve(NT * 6).rearrange("p (t s) -> p t s", t=NT)
        meanvar = carve(NT * 2).rearrange("p (t s) -> p t s", t=NT)
        std = carve(NT)
        rstd = carve(NT)
        eps_col = sb("eps_col", [128, 1])[:, :]
        carve(0, max(at[0], spectral_end))
        wqkv = carve(2 * 3 * C).rearrange("p (k n) -> p k n", k=2)
        wproj = carve(3 * C).rearrange("p (j n) -> p j n", j=3)
        bproj = carve(C)
        x2T = carve(B * 2 * N, E * GU).rearrange("p (b k n) -> p b k n", b=B, k=2)
        xhat2 = carve(NT * C).rearrange("p (t c) -> p t c", t=NT)
        rt = carve(NT * 8)
        route0 = at[0]
        logit = carve(NT * E).rearrange("p (t e) -> p t e", t=NT)
        prob = carve(NT * E).rearrange("p (t e) -> p t e", t=NT)
        small = carve(NT * 4).rearrange("p (s t) -> p s t", s=4)
        top = carve(NT * 8).rearrange("p (t k) -> p t k", t=NT)
        top_i = carve(NT * 8).bitcast(U32).rearrange("p (t k) -> p t k", t=NT)
        top_f = carve(NT * TOPK).rearrange("p (t k) -> p t k", t=NT)
        weight = carve(NT * TOPK).rearrange("p (t k) -> p t k", t=NT)
        chosen = carve(NT * TOPK * E).rearrange("p (t k e) -> p t k e", t=NT, k=TOPK)
        member = carve(NT * E // 2).bitcast(BF16).rearrange("p (t e) -> p t e", t=NT)
        at_slot = carve(NT * TOPK * E).rearrange("p (t k e) -> p t k e", t=NT, k=TOPK)
        slot_f = carve(NT * TOPK)
        slot_i = carve(NT * TOPK).bitcast(I32)
        part_i = carve(NT * TOPK).bitcast(I32)
        tile_i = carve(NT * TOPK).bitcast(I32)
        part_f = carve(NT * TOPK)
        tile_f = carve(NT * TOPK)
        count_i = carve(128).bitcast(I32)
        padded_i = carve(128).bitcast(I32)
        padded = carve(64).bitcast(BF16)
        ended = carve(16).bitcast(BF16)
        expert_f = carve(32)
        expert_i = carve(32).bitcast(I32)
        is_part = carve(NT * TOPK * 64).bitcast(F16).rearrange("p (s q) -> p s q", s=NT * TOPK)
        is_tile = carve(NT * TOPK * 32).rearrange("p (s q) -> p s q", s=NT * TOPK)
        id_tile = carve(NT * TOPK * 16).bitcast(F16).rearrange("p (s q) -> p s q", s=NT * TOPK)
        slot_token = carve(32).bitcast(U32)
        hid_s = [carve(FC * 512).rearrange("p (f n) -> p f n", f=FC) for _ in range(2)]
        silu_s = [carve(512) for _ in range(2)]
        xg = carve(2 * C, at[0] - 2 * FC * 512 - 2 * 512).rearrange("p (s c) -> p s c", s=2)
        xgT = carve(2 * 256).rearrange("p (s k n) -> p s k n", s=2, k=2)
        silu = carve(2 * FF).rearrange("p (s f) -> p s f", s=2)
        hidden = carve(2 * FF).rearrange("p (s f) -> p s f", s=2)
        hiddenT = carve(FF)
        y_out = carve(2 * C).rearrange("p (s c) -> p s c", s=2)
        y_back = carve(NT * TOPK * C, E * GU).rearrange("p (t k c) -> p t k c", t=NT, k=TOPK)
        assert at[0] <= route0
        out_T = hid_out = carve(B * 2 * N, route0 + 4600).rearrange("p (b k n) -> p b k n", b=B, k=2)

        gu_e = lambda e: main[0:CH, bass.ds(e * GU, GU)].rearrange("p (k f) -> p k f", k=2)
        dn_e = lambda e: down_all[:, bass.ds(e * DN, DN)].rearrange("p (k c) -> p k c", k=FC)

        bank = [ctx.enter_context(nc.psum_tensor(f"bank{i}", [128, 512], F32)) for i in range(8)]

        names = """ld_const ld_pix ld_spec ld_res ld_attn ld_shared ld_experts ld_late
        zeroed w_zeroed bias_zeroed eps_set negated
        spec_done spec_act spec_dve hid_done hid_ready y_done y_biased y_clipped y_ready img_done img_ready
        tok_done tok_ready tok_b_ready stats_ready mv_ready std_ready rstd_ready xhat_ready
        xT_done xT_ready qk_done v_done q_ready k_ready v_ready smax_done smax_ready rT_done qmax_ready
        st_done exp_ready pv_done recip_ready den_ready norm_ready proj_done attn_ready
        stats2 mv2 std2 rstd2 xhat2_ready xhat2_stored x2T_done x2T_ready
        logits_done exp_logit_ready route rank_done count_done base_done end_done row_done inv_done
        padded_ready ended_ready onehot_ready expert_ready slot_token_ready
        sg_done su_done silu_s_ready hid_s_ready shared_done shared_ready
        xg_done xgT_ready gate_done up_done silu_ready hidden_ready hT_done hT_ready down_done y_out_ready
        mixed half_mixed outT_done outT_ready stored""".split()
        S = {n: sem(n) for n in names}
        gathered = [sem(f"gathered{p}") for p in range(2)]
        y_stored = [sem(f"y_stored{p}") for p in range(2)]
        back = [sem(f"back{i}") for i in range(NT)]
        block = ctx.enter_context(nc.Block())

        @block.sync
        def _(sp):
            sp.dma_start(cf[:, :], a["tables_f32"]).then_inc(S["ld_const"], 16)
            sp.dma_start(pix, a["x"].rearrange("b c h w -> b (c h w)")
                         .rearrange("b (k p c) -> p b k c", k=2, p=128)).then_inc(S["ld_pix"], 16)
            sp.dma_start(cb[:, :], a["tables_bf16"]).then_inc(S["ld_attn"], 16)
            sp.dma_start(x_res, a["x"].rearrange("b c h w -> (b c h w)")
                         .rearrange("(q p f) -> p q f", q=2, p=128)).then_inc(S["ld_res"], 16)
            sp.dma_start(wqkv[0:CH, :, :], a["w_qkv"].rearrange("(k p) n -> p k n", k=2)).then_inc(S["ld_attn"], 16)
            sp.dma_start(wqkv[CH:CH + 1, 1, :], a["b_qkv"].unsqueeze(0)).then_inc(S["ld_attn"], 16)
            sp.wait_ge(S["w_zeroed"], 1)
            for r in range(4):
                sp.dma_start(wproj[32 * r:32 * r + HD, :, :],
                             a["w_proj"].rearrange("(j r d) n -> r d j n", r=4, d=HD)[r]).then_inc(S["ld_attn"], 16)
            sp.dma_start(bproj[:, :], a["b_proj"].partition_broadcast(128)).then_inc(S["ld_attn"], 16)
            sp.dma_start(wgate[0:CH, :, :], a["w_gate"].rearrange("(k p) n -> p k n", k=2)).then_inc(S["ld_attn"], 16)
            sp.dma_start(wgate[CH:CH + 1, 1, :], a["expert_bias"].unsqueeze(0)).then_inc(S["ld_attn"], 16)
            sg = shared_gu[0:CH, :].rearrange("p (k f) -> p k f", k=2)
            sp.dma_start(sg[:, :, 0:FF], a["swg"].rearrange("(k p) f -> p k f", k=2)).then_inc(S["ld_shared"], 16)
            sp.dma_start(sg[:, :, FF:], a["swu"].rearrange("(k p) f -> p k f", k=2)).then_inc(S["ld_shared"], 16)
            sp.dma_start(shared_dn[:, :].rearrange("p (k c) -> p k c", k=FC),
                         a["swd"].rearrange("(k p) c -> p k c", k=FC)).then_inc(S["ld_shared"], 16)
            for e in range(E - LATE):
                sp.dma_start(gu_e(e)[:, :, 0:FF], a["wg"][e].rearrange("(k p) f -> p k f", k=2)).then_inc(S["ld_experts"], 16)
                sp.dma_start(gu_e(e)[:, :, FF:], a["wu"][e].rearrange("(k p) f -> p k f", k=2)).then_inc(S["ld_experts"], 16)
            for e in range(E):
                sp.dma_start(dn_e(e), a["wd"][e].rearrange("(k p) c -> p k c", k=FC)).then_inc(S["ld_experts"], 16)
            sp.wait_ge(S["proj_done"], B)
            sp.wait_ge(S["attn_ready"], B)
            sp.wait_ge(S["xhat2_ready"], NT)
            for e in range(E - LATE, E):
                sp.dma_start(gu_e(e)[:, :, 0:FF], a["wg"][e].rearrange("(k p) f -> p k f", k=2)).then_inc(S["ld_late"], 16)
                sp.dma_start(gu_e(e)[:, :, FF:], a["wu"][e].rearrange("(k p) f -> p k f", k=2)).then_inc(S["ld_late"], 16)

            def store(t, p):
                sp.wait_ge(S["y_out_ready"], t + 1)
                sp.dma_start(slot_rows[bass.ds(t * TILE, TILE), :], y_out[:, p, :]).then_inc(y_stored[p], 16)

            with sp.Fori(0, TILES // 2) as i:
                store(2 * i, 0)
                store(2 * i + 1, 1)
            store(TILES - 1, 0)
            for b in range(B):
                sp.wait_ge(S["outT_ready"], b + 1)
                sp.dma_start(out[b].rearrange("(k p) h w -> p k (h w)", k=2), out_T[0:CH, b]).then_inc(S["stored"], 16)
            sp.wait_ge(S["stored"], 16 * B)

        @block.gpsimd
        def _(pool):
            nc.gpsimd.memset(w1, 0.0).then_inc(S["zeroed"], 1)
            nc.gpsimd.memset(w2, 0.0).then_inc(S["zeroed"], 1)
            nc.gpsimd.memset(wproj[:, :, :], 0.0).then_inc(S["w_zeroed"], 1)
            pool.wait_ge(S["xhat_ready"], NT)
            pool.wait_ge(S["tok_ready"], B)
            pool.wait_ge(S["ld_attn"], 10 * 16)
            nc.gpsimd.tensor_tensor(tok_b[:, :, :], tok[:, :, :],
                                    bproj[:, :].unsqueeze(1).broadcast_to([128, NT, C]), ALU.add).then_inc(S["tok_b_ready"], 1)
            for t in range(NT):
                pool.wait_ge(S["xhat2_ready"], t + 1)
                pool.dma_start(xhat_rows[128 * t:128 * t + 128, :], xhat2[:, t, :]).then_inc(S["xhat2_stored"], 16)
            pool.wait_ge(S["xhat2_stored"], 16 * NT)
            pool.wait_ge(S["slot_token_ready"], 1)
            pool.wait_ge(S["shared_ready"], NT // 2)
            for t in range(TILES):
                if t >= 2:
                    pool.wait_ge(S["xg_done"], t - 1)
                pool.indirect_dma_start(xg[:, t % 2, :], None, xhat_rows,
                                        bass.IndirectOffsetOnAxis(ap=slot_token[:, t:t + 1], axis=0)).then_inc(gathered[t % 2], 16)
            pool.wait_ge(y_stored[0], 16 * ((TILES + 1) // 2))
            pool.wait_ge(y_stored[1], 16 * (TILES // 2))
            for t in range(NT):
                for k in range(TOPK):
                    j = t * TOPK + k
                    pool.indirect_dma_start(y_back[:, t, k, :], None, slot_rows,
                                            bass.IndirectOffsetOnAxis(ap=slot_i[:, j:j + 1].bitcast(U32), axis=0)).then_inc(back[t], 16)

        @block.scalar
        def _(act):
            act.wait_ge(S["zeroed"], 2)
            for dst, src in ((w1, a["w1"]), (w2, a["w2"])):
                for r in range(2):
                    for k in range(BPH):
                        act.dma_start(dst[BLK * k:BLK * k + BLK, :, r, BLK * k:BLK * k + BLK],
                                      src[r].rearrange("(g k) i o -> k i g o", k=BPH)[k]).then_inc(S["ld_spec"], 16)
            with nc.allow_non_contiguous_dma(reason="a bias per channel"):
                for r in range(2):
                    act.dma_start(b1[0:CH, :, r], a["b1"][r].rearrange("(g k) o -> (k o) g", g=2)).then_inc(S["ld_spec"], 16)
            for dst, r in ((b2[0:MA, 0], 0), (b2[0:MA, 2], 1), (b2[0:MB, 1], 0), (b2[64:64 + MB, 1], 1)):
                act.dma_start(dst, a["b2"][r].rearrange("n o -> (n o)").partition_broadcast(dst.shape[0])).then_inc(S["ld_spec"], 16)
            for b in range(B):
                act.wait_ge(S["spec_done"], 2 * b + 1)
                act.activation(spec[0:CH, 0, :, b * MODES:(b + 1) * MODES],
                               bank[2 * b % 4][0:CH, 0:2 * MODES].rearrange("p (r m) -> p r m", r=2), ACT.Copy).then_inc(S["spec_act"], 1)
            act.wait_ge(S["ld_spec"], 22 * 16)
            for v in range(8):
                bp, g, r = v // 4, v // 2 % 2, v % 2
                act.wait_ge(S["hid_done"], v + 1)
                act.activation(hid[0:CH, g, r, bp * 2 * MODES:(bp + 1) * 2 * MODES],
                               bank[4 + v % 4][0:CH, 0:2 * MODES], ACT.Relu, bias=b1[0:CH, g, r:r + 1]).then_inc(S["hid_ready"], 1)
            for s in range(4):
                pair, h = s // 2, s % 2
                act.wait_ge(S["tok_done"], s + 1)
                dst = tok[:, 4 * pair + h:4 * pair + h + 3:2, :].rearrange("p b (g i) -> p b g i", i=3)
                src = bank[s][:, 0:3 * 128].rearrange("p (i b g) -> p b g i", i=3, b=2)
                act.activation(dst, src, ACT.Copy).then_inc(S["tok_ready"], 1)
            act.wait_ge(S["eps_set"], 1)
            act.wait_ge(S["mv_ready"], NT)
            act.activation(std, meanvar[:, :, 1], ACT.Sqrt, bias=eps_col).then_inc(S["std_ready"], 1)
            for b in range(B):
                act.wait_ge(S["xT_done"], b + 1)
                act.activation(xT[0:CH, b, :, :], bank[4 + b][0:CH, :].rearrange("p (k n) -> p k n", k=2), ACT.Copy).then_inc(S["xT_ready"], 1)

            def values(b):
                if b == 0:
                    act.wait_ge(S["bias_zeroed"], 2)
                act.wait_ge(S["v_done"], b + 1)
                if b >= 2:
                    act.wait_ge(S["pv_done"], 3 * (b - 1))
                act.activation(v_sb[:, b % 2, :, :, 0:HD],
                               bank[5][:, 0:2 * C].rearrange("p (k h d) -> p k h d", k=2, d=HD), ACT.Copy).then_inc(S["v_ready"], 1)

            values(0)
            for b in range(B):
                if b + 1 < B:
                    values(b + 1)
                for j in range(3):
                    quad = 3 * b + j
                    if quad >= 2:
                        act.wait_ge(S["pv_done"], quad - 1)
                    for u in range(4):
                        n = 4 * quad + u
                        act.wait_ge(S["st_done"], n + 1)
                        act.activation(probs[:, quad % 2, u // 2, 2 * (u % 2):2 * (u % 2) + 2, :],
                                       bank[2 + n % 3][:, :].rearrange("p (h n) -> p h n", h=2), ACT.Exp).then_inc(S["exp_ready"], 1)
            act.wait_ge(S["mv2"], NT)
            act.activation(std, meanvar[:, :, 1], ACT.Sqrt, bias=eps_col).then_inc(S["std2"], 1)
            for b in range(B):
                act.wait_ge(S["x2T_done"], b + 1)
                act.activation(x2T[0:CH, b, :, :], bank[b][0:CH, :].rearrange("p (k n) -> p k n", k=2), ACT.Copy).then_inc(S["x2T_ready"], 1)
            act.wait_ge(S["route"], 3)
            act.activation(prob, logit, ACT.Exp).then_inc(S["exp_logit_ready"], 1)
            for u in range(2 * FC):
                act.wait_ge(S["sg_done"], u + 1)
                if u >= 2:
                    act.wait_ge(S["hid_s_ready"], u - 1)
                act.activation(silu_s[u % 2], bank[u % 2][:, :], ACT.Silu).then_inc(S["silu_s_ready"], 1)

            act.wait_ge(S["shared_ready"], NT // 2)

            def columns(t, p):
                act.wait_ge(S["xg_done"], t + 1)
                if not (isinstance(t, int) and t < 2):
                    act.wait_ge(S["up_done"], t - 1)
                act.activation(xgT[0:CH, p, :, :], bank[5][0:CH, 0:256].rearrange("p (k n) -> p k n", k=2), ACT.Copy).then_inc(S["xgT_ready"], 1)

            def gate(t, p):
                act.wait_ge(S["gate_done"], t + 1)
                if not (isinstance(t, int) and t < 2):
                    act.wait_ge(S["hidden_ready"], t - 1)
                act.activation(silu[:, p, :], bank[p][:, 0:FF], ACT.Silu).then_inc(S["silu_ready"], 1)

            def hidden_columns(t):
                act.wait_ge(S["hT_done"], t + 1)
                if not (isinstance(t, int) and t < 1):
                    act.wait_ge(S["down_done"], t)
                act.activation(hiddenT, bank[4][:, 0:FF], ACT.Copy).then_inc(S["hT_ready"], 1)

            def step(t, p):
                if not (isinstance(t, int) and t + 1 >= TILES):
                    gate(t + 1, 1 - p)
                hidden_columns(t)
                if not (isinstance(t, int) and t + 2 >= TILES):
                    columns(t + 2, p)

            columns(0, 0)
            gate(0, 0)
            columns(1, 1)
            step(0, 0)
            step(1, 1)
            with act.Fori(1, (TILES - 3) // 2) as i:
                step(2 * i, 0)
                step(2 * i + 1, 1)
            for t in range(TILES - 3, TILES):
                step(t, t % 2)
            for b in range(B):
                act.wait_ge(S["outT_done"], b + 1)
                act.activation(out_T[0:CH, b, :, :], bank[b][0:CH, :].rearrange("p (k n) -> p k n", k=2), ACT.Copy).then_inc(S["outT_ready"], 1)

        @block.vector
        def _(dve):
            vec = nc.vector
            vec.memset(eps_col, EPS).then_inc(S["eps_set"], 1)
            dve.wait_ge(S["ld_spec"], 22 * 16)
            for w in (w1, w2):
                vec.tensor_scalar(w[0:CH, :, 2, :], w[0:CH, :, 1, :], -1.0, None, ALU.mult).then_inc(S["negated"], 1)
            for b in range(B):
                dve.wait_ge(S["spec_done"], 2 * b + 2)
                vec.tensor_copy(spec[0:CH, 1, :, b * MODES:(b + 1) * MODES],
                                bank[(2 * b + 1) % 4][0:CH, 0:2 * MODES].rearrange("p (r m) -> p r m", r=2)).then_inc(S["spec_dve"], 1)
            for u in range(6):
                bp, k, s = u // 3, u % 3, u % 2
                rows = slice(0, 128 if k == 1 else MA)
                dve.wait_ge(S["y_done"], u + 1)
                vec.tensor_tensor(biased[rows, s], bank[u % 4][rows, 0:2 * C].rearrange("p (b c) -> p b c", b=2),
                                  b2[rows, k].unsqueeze(1).broadcast_to([rows.stop, 2, C]), ALU.add).then_inc(S["y_biased"], 1)
                dve.wait_ge(S["y_biased"], u + 1)
                vec.tensor_scalar(clipped[rows, s], biased[rows, s], LAMBDA, -LAMBDA, ALU.min, ALU.max).then_inc(S["y_clipped"], 1)
                dve.wait_ge(S["y_clipped"], u + 1)
                vec.tensor_tensor(y[rows, 2 * bp:2 * bp + 2, k, :], biased[rows, s], clipped[rows, s], ALU.subtract).then_inc(S["y_ready"], 1)
            dve.wait_ge(S["ld_res"], 16)
            for z in range(4):
                pair, jj = z // 2, z % 2
                dve.wait_ge(S["img_done"], z + 1)
                vec.tensor_tensor(img[:, pair, 384 * jj:384 * jj + 384], bank[4 + z][:, 0:384],
                                  x_res[:, pair, 384 * jj:384 * jj + 384], ALU.add).then_inc(S["img_ready"], 1)

            def layernorm(src, dst, sem_stats, sem_mv, sem_std, sem_rstd, sem_out, ready):
                for t in range(NT):
                    ready(t)
                    vec.bn_stats(stats[:, t, :], src[:, t, :]).then_inc(S[sem_stats], 1)
                for t in range(NT):
                    dve.wait_ge(S[sem_stats], t + 1)
                    vec.bn_aggr(meanvar[:, t, :], stats[:, t, :]).then_inc(S[sem_mv], 1)
                dve.wait_ge(S[sem_std], 1)
                vec.reciprocal(rstd, std).then_inc(S[sem_rstd], 1)
                dve.wait_ge(S[sem_rstd], 1)
                for t in range(NT):
                    vec.tensor_scalar(dst[:, t, :], src[:, t, :], meanvar[:, t, 0:1], rstd[:, t:t + 1],
                                      ALU.subtract, ALU.mult).then_inc(S[sem_out], 1)

            layernorm(tok, xhat, "stats_ready", "mv_ready", "std_ready", "rstd_ready", "xhat_ready",
                      lambda t: dve.wait_ge(S["tok_ready"], 2 * (t // 4) + t % 2 + 1))
            vec.memset(xT[CH:CH + 1, :, :, :], 1.0).then_inc(S["bias_zeroed"], 1)
            vec.memset(v_sb, 1.0).then_inc(S["bias_zeroed"], 1)
            vec.memset(negmax, 0.0).then_inc(S["bias_zeroed"], 1)
            dve.wait_ge(S["bias_zeroed"], 3)

            def queries_keys(b):
                if b >= 2:
                    dve.wait_ge(S["st_done"], 12 * (b - 1))
                dve.wait_ge(S["qk_done"], b + 1)
                for v in range(2):
                    vec.tensor_scalar(q_sb[0:CH, b % 2, v], bank[0][0:CH, :].rearrange("p (t n) -> p t n", t=2),
                                      mask[0:CH, v:v + 1], None, ALU.mult).then_inc(S["q_ready"], 1)
                    vec.tensor_scalar(k_sb[0:CH, b % 2, v], bank[1][0:CH, :].rearrange("p (t n) -> p t n", t=2),
                                      mask[0:CH, 2 + v:3 + v], mask[0:CH, 4 + v:5 + v], ALU.mult, ALU.add).then_inc(S["k_ready"], 1)

            def maxima(b, units):
                for u in units:
                    n, qh, g6 = 12 * b + u, u // 6, u % 6
                    if b >= 1:
                        dve.wait_ge(S["rT_done"], 2 * (b - 1) + qh + 1)
                    dve.wait_ge(S["smax_done"], n + 1)
                    col = CH * (g6 // 3) + 32 * (g6 % 3)
                    vec.tensor_reduce(negmax[:, qh, col + HD:col + HD + 177:176], bank[n % 2][:, :].rearrange("p (h n) -> p h n", h=2),
                                      AX.X, ALU.max, negate=True).then_inc(S["smax_ready"], 1)

            def subtract_maxima(b, qh):
                dve.wait_ge(S["rT_done"], 2 * b + qh + 1)
                dve.wait_ge(S["q_ready"], 2 * b + 2)
                dst = q_sb[0:CH, b % 2, :, :, 128 * qh:128 * qh + 128].rearrange("p v t n -> p (v t) n")
                vec.tensor_tensor(dst, dst, bank[5][0:CH, :].rearrange("p (v n) -> p v n", v=4), ALU.add).then_inc(S["qmax_ready"], 1)

            def normalise(quad):
                b, j, s = quad // 3, quad % 3, quad % 2
                dve.wait_ge(S["pv_done"], quad + 1)
                vec.reciprocal(recip[:, s], bank[6 + s][:, 0:N]).then_inc(S["recip_ready"], 1)
                dve.wait_ge(S["recip_ready"], quad + 1)
                vec.stream_shuffle(den[:, s], recip[:, s], [HD + i % HD for i in range(32)]).then_inc(S["den_ready"], 1)
                dve.wait_ge(S["den_ready"], quad + 1)
                if b >= 2 and j == 0:
                    dve.wait_ge(S["proj_done"], b - 1)
                vec.tensor_tensor(o_sb[:, b % 2, j], bank[6 + s][:, 0:N], den[:, s], ALU.mult).then_inc(S["norm_ready"], 1)

            queries_keys(0)
            maxima(0, range(12))
            for b in range(B):
                if b + 1 < B:
                    queries_keys(b + 1)
                subtract_maxima(b, 0)
                subtract_maxima(b, 1)
                for j in range(3):
                    if j:
                        normalise(3 * b + j - 1)
                    if b + 1 < B:
                        maxima(b + 1, range(4 * j, 4 * j + 4))
                normalise(3 * b + 2)
                dve.wait_ge(S["proj_done"], b + 1)
                if b == 0:
                    dve.wait_ge(S["tok_b_ready"], 1)
                vec.tensor_tensor(tok[:, 2 * b:2 * b + 2, :], tok_b[:, 2 * b:2 * b + 2, :],
                                  bank[5][:, 0:2 * C].rearrange("p (h c) -> p h c", h=2), ALU.add).then_inc(S["attn_ready"], 1)
            vec.memset(x2T[CH:CH + 1, :, :, :], 1.0).then_inc(S["bias_zeroed"], 1)
            layernorm(tok, xhat2, "stats2", "mv2", "std2", "rstd2", "xhat2_ready",
                      lambda t: dve.wait_ge(S["attn_ready"], t // 2 + 1))

            steps = [0]

            def step(instruction):
                steps[0] += 1
                instruction.then_inc(S["route"], 1)
                dve.wait_ge(S["route"], steps[0])

            def per_tile(x, n=E):
                return x.unsqueeze(2).broadcast_to([128, NT, n])

            dve.wait_ge(S["logits_done"], 1)
            lg = bank[4][:, 0:NT * E].rearrange("p (t e) -> p t e", t=NT)
            step(vec.tensor_reduce(small[:, 0, :], lg, AX.X, ALU.max))
            step(vec.tensor_tensor(logit, lg, per_tile(small[:, 0, :]), ALU.subtract))
            steps[0] += 1
            vec.tensor_copy(small[:, 3, :], small[:, 0, :]).then_inc(S["route"], 1)
            dve.wait_ge(S["exp_logit_ready"], 1)
            dve.wait_ge(S["route"], steps[0])
            step(vec.reduce_sum(small[:, 1, :], prob, AX.X))
            step(vec.reciprocal(small[:, 2, :], small[:, 1, :]))
            step(vec.tensor_tensor(prob, prob, per_tile(small[:, 2, :]), ALU.mult))
            for t in range(NT):
                step(vec.max(top[:, t, :], prob[:, t, :]))
            for t in range(NT):
                step(vec.max_index(top_i[:, t, :], top[:, t, :], prob[:, t, :]))
            step(vec.tensor_copy(top_f, top_i[:, :, 0:TOPK]))
            step(vec.tensor_tensor(chosen, iota[:, 0:E].unsqueeze(1).unsqueeze(1).broadcast_to([128, NT, TOPK, E]),
                                   top_f.unsqueeze(3).broadcast_to([128, NT, TOPK, E]), ALU.is_equal))
            step(vec.tensor_tensor(member, chosen[:, :, 0, :], chosen[:, :, 1, :], ALU.add))
            assert steps[0] == MEMBER_STEP
            step(vec.reduce_sum(small[:, 1, :], top[:, :, 0:TOPK], AX.X))
            step(vec.reciprocal(small[:, 2, :], small[:, 1, :]))
            step(vec.tensor_tensor(weight, top[:, :, 0:TOPK], per_tile(small[:, 2, :], TOPK), ALU.mult))
            dve.wait_ge(S["count_done"], 1)
            step(vec.tensor_scalar(count_i[0:E, :], bank[4][0:E, 256:384], float(TILE - 1), None, ALU.add))
            step(vec.tensor_scalar(padded_i[0:E, :], count_i[0:E, :], -TILE, None, ALU.bitwise_and))
            vec.tensor_copy(padded[0:E, :], padded_i[0:E, :]).then_inc(S["padded_ready"], 1)
            dve.wait_ge(S["end_done"], 1)
            vec.tensor_tensor(ended[0:E, :], bank[4][0:E, 384:416], tile_start, ALU.is_le).then_inc(S["ended_ready"], 1)
            dve.wait_ge(S["base_done"], 1)
            step(vec.tensor_tensor(at_slot, chosen, bank[5][:, 0:NT * E].rearrange("p (t e) -> p t e", t=NT)
                                   .unsqueeze(2).broadcast_to([128, NT, TOPK, E]), ALU.mult))
            step(vec.reduce_sum(slot_f.rearrange("p (t k) -> p t k", t=NT), at_slot, AX.X))
            step(vec.tensor_copy(slot_i, slot_f))
            step(vec.tensor_scalar(part_i, slot_i, TILE - 1, None, ALU.bitwise_and))
            step(vec.tensor_scalar(tile_i, slot_i, 7, None, ALU.logical_shift_right))
            step(vec.tensor_copy(part_f, part_i))
            step(vec.tensor_copy(tile_f, tile_i))
            pairs = NT * TOPK
            step(vec.tensor_tensor(is_part, iota.unsqueeze(1).broadcast_to([128, pairs, 128]),
                                   part_f.unsqueeze(2).broadcast_to([128, pairs, 128]), ALU.is_equal))
            step(vec.tensor_tensor(is_tile, iota[:, 0:32].unsqueeze(1).broadcast_to([128, pairs, 32]),
                                   tile_f.unsqueeze(2).broadcast_to([128, pairs, 32]), ALU.is_equal))
            vec.tensor_tensor(id_tile, is_tile, token_id.unsqueeze(2).broadcast_to([128, pairs, 32]), ALU.mult).then_inc(S["onehot_ready"], 1)
            dve.wait_ge(S["row_done"], 1)
            vec.tensor_scalar(expert_i[0:1, :], bank[4][0:1, 448:480], float(E - 1), None, ALU.min).then_inc(S["expert_ready"], 1)
            dve.wait_ge(S["inv_done"], 1)
            vec.tensor_copy(slot_token, bank[5][:, 128:160]).then_inc(S["slot_token_ready"], 1)

            def shared_rows(u):
                dve.wait_ge(S["shared_done"], u + 1)
                vec.tensor_tensor(tok_b[:, 2 * u:2 * u + 2, :], tok[:, 2 * u:2 * u + 2, :],
                                  bank[6 + u % 2][:, 0:2 * C].rearrange("p (h c) -> p h c", h=2), ALU.add).then_inc(S["shared_ready"], 1)

            for u in range(2 * FC):
                dve.wait_ge(S["silu_s_ready"], u + 1)
                dve.wait_ge(S["su_done"], u + 1)
                vec.tensor_tensor(hid_s[u // FC][:, u % FC, :], silu_s[u % 2], bank[2 + u % 2][:, :], ALU.mult).then_inc(S["hid_s_ready"], 1)
            for u in range(NT // 2):
                shared_rows(u)

            def hidden_rows(t, p):
                dve.wait_ge(S["silu_ready"], t + 1)
                dve.wait_ge(S["up_done"], t + 1)
                if not (isinstance(t, int) and t < 2):
                    dve.wait_ge(S["hT_done"], t - 1)
                vec.tensor_tensor(hidden[:, p, :], silu[:, p, :], bank[2 + p][:, 0:FF], ALU.mult).then_inc(S["hidden_ready"], 1)

            def down_rows(t, p, half):
                dve.wait_ge(S["down_done"], t + 1)
                if not (isinstance(t, int) and t < 2):
                    dve.wait_ge(y_stored[p], 16 * half)
                vec.tensor_copy(y_out[:, p, :], bank[6][:, 0:C]).then_inc(S["y_out_ready"], 1)

            def expert_step(t, p, half):
                if not (isinstance(t, int) and t + 1 >= TILES):
                    hidden_rows(t + 1, 1 - p)
                down_rows(t, p, half)

            hidden_rows(0, 0)
            expert_step(0, 0, 0)
            expert_step(1, 1, 0)
            with dve.Fori(1, (TILES - 3) // 2) as i:
                expert_step(2 * i, 0, i)
                expert_step(2 * i + 1, 1, i)
            for t in range(TILES - 3, TILES):
                expert_step(t, t % 2, t // 2)

            for t in range(NT):
                dve.wait_ge(back[t], 16 * TOPK)
                vec.scalar_tensor_tensor(tok[:, t, :], y_back[:, t, 0, :], weight[:, t, 0:1], tok_b[:, t, :], ALU.mult, ALU.add).then_inc(S["half_mixed"], 1)
                dve.wait_ge(S["half_mixed"], t + 1)
                vec.scalar_tensor_tensor(tok_b[:, t, :], y_back[:, t, 1, :], weight[:, t, 1:2], tok[:, t, :], ALU.mult, ALU.add).then_inc(S["mixed"], 1)

        @block.tensor
        def _(pe):
            mm, tr = nc.tensor.matmul, nc.tensor.transpose
            pe.wait_ge(S["ld_const"], 16)
            pe.wait_ge(S["ld_pix"], 16)
            for u in range(8):
                b, g = u // 2, u % 2
                if u >= 4:
                    pe.wait_ge(S["spec_dve" if g else "spec_act"], (u - 4) // 2 + 1)
                for k in range(2):
                    last = mm(bank[u % 4][0:CH, 0:2 * MODES], pix[:, b, k, g * CH:(g + 1) * CH], fwd[:, k, :], start=(k == 0), stop=(k == 1))
                last.then_inc(S["spec_done"], 1)
            pe.wait_ge(S["negated"], 2)
            for v in range(8):
                bp, g, r = v // 4, v // 2 % 2, v % 2
                pe.wait_ge(S["spec_act"], 2 * (bp + 1))
                pe.wait_ge(S["spec_dve"], 2 * (bp + 1))
                if v >= 4:
                    pe.wait_ge(S["hid_ready"], v - 3)
                cols = slice(bp * 2 * MODES, (bp + 1) * 2 * MODES)
                dst = bank[4 + v % 4][0:CH, 0:2 * MODES]
                mm(dst, w1[0:CH, g, 0, :], spec[0:CH, g, r, cols], start=True, stop=False)
                mm(dst, w1[0:CH, g, 1 if r else 2, :], spec[0:CH, g, 1 - r, cols], start=False, stop=True).then_inc(S["hid_done"], 1)
            for u in range(6):
                bp, k = u // 3, u % 3
                pe.wait_ge(S["hid_ready"], 4 * (bp + 1))
                if u == 0:
                    pe.wait_ge(S["spec_act"], 4)
                    pe.wait_ge(S["spec_dve"], 4)
                if u >= 4:
                    pe.wait_ge(S["y_biased"], u - 3)
                parts = {0: [(0, 0, 0, MA)], 1: [(0, 0, MA, MODES), (64, 1, MA, MODES)], 2: [(0, 1, 0, MA)]}[k]
                for bb in range(2):
                    for g in range(2):
                        for c in range(2):
                            for row, r, m0, m1 in parts:
                                src = hid[0:CH, g, c, (2 * bp + bb) * MODES + m0:(2 * bp + bb) * MODES + m1]
                                sign = 0 if r == c else (1 if r else 2)
                                last = mm(bank[u % 4][row:row + m1 - m0, bb * C + g * CH:bb * C + (g + 1) * CH], src,
                                          w2[0:CH, g, sign, :], start=(c == 0), stop=(c == 1))
                last.then_inc(S["y_done"], 1)
            for z in range(4):
                pair, jj = z // 2, z % 2
                pe.wait_ge(S["y_ready"], 3 * (pair + 1))
                if z == 0:
                    pe.wait_ge(S["hid_ready"], 8)
                for j in range(2):
                    for k in range(3):
                        rows = slice(0, 128 if k == 1 else MA)
                        for bb in range(2):
                            last = mm(bank[4 + z][64 * bb:64 * bb + 64, j * C:(j + 1) * C], inv[rows, k, (2 * jj + j) * 64:(2 * jj + j) * 64 + 64],
                                      y[rows, 2 * pair + bb, k, :], start=(k == 0), stop=(k == 2))
                last.then_inc(S["img_done"], 1)
            for s in range(4):
                pair, h = s // 2, s % 2
                pe.wait_ge(S["img_ready"], 2 * (pair + 1))
                if s == 0:
                    pe.wait_ge(S["y_biased"], 6)
                for i in range(3):
                    last = tr(bank[s][:, 128 * i:128 * i + 128], img[:, pair, 256 * i + 128 * h:256 * i + 128 * h + 128], ident)
                last.then_inc(S["tok_done"], 1)
            pe.wait_ge(S["img_ready"], 4)
            for b in range(B):
                pe.wait_ge(S["xhat_ready"], 2 * b + 2)
                for k in range(2):
                    for h in range(2):
                        last = tr(bank[4 + b][0:CH, 256 * k + 128 * h:256 * k + 128 * h + 128], xhat[:, 2 * b + h, k * CH:(k + 1) * CH], ident)
                last.then_inc(S["xT_done"], 1)

            rows = (slice(0, CH), slice(0, CH + 1))

            def project_qkv(b):
                if b == 0:
                    pe.wait_ge(S["tok_ready"], 4)
                    pe.wait_ge(S["xT_ready"], 4)
                    pe.wait_ge(S["bias_zeroed"], 1)
                    pe.wait_ge(S["ld_attn"], 10 * 16)
                else:
                    pe.wait_ge(S["smax_ready"], 12 * b)
                for m in range(2):
                    for t in range(2):
                        for k in range(2):
                            last = mm(bank[m][0:CH, t * N:(t + 1) * N], wqkv[rows[k], k, m * C + t * CH:m * C + (t + 1) * CH],
                                      xT[rows[k], b, k, :], start=(k == 0), stop=(k == 1))
                last.then_inc(S["qk_done"], 1)
                if b == 1:
                    pe.wait_ge(S["v_ready"], 1)
                if b >= 2:
                    pe.wait_ge(S["attn_ready"], b - 1)
                for h in range(2):
                    for k in range(2):
                        last = mm(bank[5][:, h * C:(h + 1) * C], xT[rows[k], b, k, 128 * h:128 * h + 128],
                                  wqkv[rows[k], k, 2 * C:3 * C], start=(k == 0), stop=(k == 1))
                last.then_inc(S["v_done"], 1)

            def scores_for_max(b, units):
                for u in units:
                    n, qh, g6 = 12 * b + u, u // 6, u % 6
                    if u == 0:
                        pe.wait_ge(S["q_ready"], 2 * (b + 1))
                        pe.wait_ge(S["k_ready"], 2 * (b + 1))
                    if n >= 2:
                        pe.wait_ge(S["smax_ready"], n - 1)
                    t, r = g6 // 3, slice(32 * (g6 % 3), 32 * (g6 % 3) + 32)
                    for v in range(2):
                        last = mm(bank[n % 2][:, v * N:(v + 1) * N], q_sb[r, b % 2, v, t, 128 * qh:128 * qh + 128],
                                  k_sb[r, b % 2, v, t, :], start=True, stop=True)
                    last.then_inc(S["smax_done"], 1)

            def maxima_rows(b, qh):
                pe.wait_ge(S["smax_ready"], 12 * b + 6 * qh + 6)
                if qh == 0:
                    pe.wait_ge(S["v_ready"], min(b + 2, B))
                    pe.wait_ge(S["bias_zeroed"], 3)
                    if b:
                        pe.wait_ge(S["attn_ready"], b)
                else:
                    pe.wait_ge(S["qmax_ready"], 2 * b + 1)
                for v in range(4):
                    last = tr(bank[5][0:CH, 128 * v:128 * v + 128], negmax[:, qh, v * CH:(v + 1) * CH], ident)
                last.then_inc(S["rT_done"], 1)

            def scores(b, j):
                for u in range(4):
                    n, kh, g6 = 12 * b + 4 * j + u, u // 2, 2 * j + u % 2
                    if n >= 3:
                        pe.wait_ge(S["exp_ready"], n - 2)
                    t, r = g6 // 3, slice(32 * (g6 % 3), 32 * (g6 % 3) + 32)
                    for v in range(2):
                        last = mm(bank[2 + n % 3][:, v * N:(v + 1) * N], k_sb[r, b % 2, v, t, 128 * kh:128 * kh + 128],
                                  q_sb[r, b % 2, v, t, :], start=True, stop=True)
                    last.then_inc(S["st_done"], 1)

            def attend(quad):
                b, j, s = quad // 3, quad % 3, quad % 2
                pe.wait_ge(S["exp_ready"], 4 * quad + 4)
                if quad >= 2:
                    pe.wait_ge(S["norm_ready"], quad - 1)
                for kh in range(2):
                    for h in range(4):
                        last = mm(bank[6 + s][32 * h:32 * h + 32, 0:N], v_sb[:, b % 2, kh, 4 * j + h, :], probs[:, s, kh, h, :],
                                  start=(kh == 0), stop=(kh == 1))
                last.then_inc(S["pv_done"], 1)

            def project_out(b):
                pe.wait_ge(S["norm_ready"], 3 * b + 3)
                pe.wait_ge(S["qmax_ready"], 2 * b + 2)
                for h in range(2):
                    for j in range(3):
                        last = mm(bank[5][:, h * C:(h + 1) * C], o_sb[:, b % 2, j, 128 * h:128 * h + 128], wproj[:, j, :],
                                  start=(j == 0), stop=(j == 2))
                last.then_inc(S["proj_done"], 1)

            project_qkv(0)
            scores_for_max(0, range(12))
            for b in range(B):
                if b + 1 < B:
                    project_qkv(b + 1)
                maxima_rows(b, 0)
                maxima_rows(b, 1)
                pe.wait_ge(S["qmax_ready"], 2 * b + 2)
                for j in range(3):
                    scores(b, j)
                    if j:
                        attend(3 * b + j - 1)
                    if b + 1 < B:
                        scores_for_max(b + 1, range(4 * j, 4 * j + 4))
                attend(3 * b + 2)
                project_out(b)

            pe.wait_ge(S["exp_ready"], 48)
            for b in range(B):
                pe.wait_ge(S["xhat2_ready"], 2 * b + 2)
                for k in range(2):
                    for h in range(2):
                        last = tr(bank[b][0:CH, 256 * k + 128 * h:256 * k + 128 * h + 128], xhat2[:, 2 * b + h, k * CH:(k + 1) * CH], ident)
                last.then_inc(S["x2T_done"], 1)
            pe.wait_ge(S["bias_zeroed"], 4)
            for t in range(NT):
                pe.wait_ge(S["x2T_ready"], t // 2 + 1)
                for k in range(2):
                    last = mm(bank[4][:, t * E:(t + 1) * E], x2T[rows[k], t // 2, k, 128 * (t % 2):128 * (t % 2) + 128],
                              wgate[rows[k], k, :], start=(k == 0), stop=(k == 1))
            last.then_inc(S["logits_done"], 1)

            def shared_gate_up(u):
                half, f = u // FC, u % FC
                for m, free in ((0, "silu_s_ready"), (1, "hid_s_ready")):
                    if u >= 2:
                        pe.wait_ge(S[free], u - 1)
                    for b in range(2):
                        for k in range(2):
                            last = mm(bank[2 * m + u % 2][:, b * N:(b + 1) * N],
                                      shared_gu[0:CH, k * 2 * FF + m * FF + 128 * f:k * 2 * FF + m * FF + 128 * f + 128],
                                      x2T[0:CH, 2 * half + b, k, :], start=(k == 0), stop=(k == 1))
                    last.then_inc(S["su_done" if m else "sg_done"], 1)

            def shared_down(u):
                if u >= 2:
                    pe.wait_ge(S["shared_ready"], u - 1)
                for h in range(2):
                    t = 2 * u + h
                    for f in range(FC):
                        last = mm(bank[6 + u % 2][:, h * C:(h + 1) * C], hid_s[t // 4][:, f, 128 * (t % 4):128 * (t % 4) + 128],
                                  shared_dn[:, f * C:(f + 1) * C], start=(f == 0), stop=(f == FC - 1))
                last.then_inc(S["shared_done"], 1)

            def rank_and_count():
                pe.wait_ge(S["route"], MEMBER_STEP)
                rank = bank[5][:, 0:NT * E].rearrange("p (t e) -> p t e", t=NT)
                mm(rank, before, member, start=True, stop=False, skip_group_check=True)
                for t in range(NT - 1):
                    mm(rank[:, t + 1:, :], ones, member[:, t:t + 1, :].broadcast_to([128, NT - 1 - t, E]),
                       start=False, stop=False, skip_group_check=True)
                for t in range(NT):
                    last = mm(bank[4][0:E, 256:384], member[:, t, :], ones, start=(t == 0), stop=(t == NT - 1))
                last.then_inc(S["count_done"], 1)

            def base_and_end():
                pe.wait_ge(S["padded_ready"], 1)
                rank = bank[5][:, 0:NT * E].rearrange("p (t e) -> p t e", t=NT)
                mm(rank, padded[0:E, :], before[0:E, 0:E].unsqueeze(1).broadcast_to([E, NT, E]), start=False, stop=True,
                   skip_group_check=True).then_inc(S["base_done"], 1)
                mm(bank[4][0:E, 384:416], upto, padded[0:E, 0:32], start=True, stop=True).then_inc(S["end_done"], 1)
                pe.wait_ge(S["ended_ready"], 1)
                mm(bank[4][0:1, 448:480], ones[0:E, 0:1], ended[0:E, :], start=True, stop=True).then_inc(S["row_done"], 1)

            def slot_tokens():
                pe.wait_ge(S["onehot_ready"], 1)
                for s in range(NT * TOPK):
                    last = mm(bank[5][:, 128:160], is_part[:, s, :], id_tile[:, s, :], start=(s == 0), stop=(s == NT * TOPK - 1))
                last.then_inc(S["inv_done"], 1)

            pe.wait_ge(S["ld_shared"], 3 * 16)
            pe.wait_ge(S["attn_ready"], B)
            pe.wait_ge(S["norm_ready"], 12)
            rank_and_count()
            base_and_end()
            slot_tokens()
            for u in range(2 * FC):
                shared_gate_up(u)
            pe.wait_ge(S["hid_s_ready"], 2 * FC)
            for u in range(NT // 2):
                shared_down(u)

            pe.wait_ge(S["ld_experts"], 16 * (2 * (E - LATE) + E))
            pe.wait_ge(S["ld_late"], 16 * 2 * LATE)
            pe.wait_ge(S["expert_ready"], 1)
            pe.wait_ge(S["slot_token_ready"], 1)

            def tokens_T(t, p, half):
                pe.wait_ge(gathered[p], 16 * half + 16)
                if not (isinstance(t, int) and t < 1):
                    pe.wait_ge(S["xgT_ready"], t)
                for k in range(2):
                    last = tr(bank[5][0:CH, 128 * k:128 * k + 128], xg[:, p, k * CH:(k + 1) * CH], ident)
                last.then_inc(S["xg_done"], 1)

            def gate_up(t, p, m, e):
                if m == 0:
                    pe.wait_ge(S["xgT_ready"], t + 1)
                if not (isinstance(t, int) and t < 2):
                    pe.wait_ge(S["hidden_ready" if m else "silu_ready"], t - 1)
                for k in range(2):
                    last = mm(bank[2 * m + p][:, 0:FF], xgT[0:CH, p, k, :], main[0:CH, bass.ds(e * GU + k * 2 * FF + m * FF, FF)],
                              start=(k == 0), stop=(k == 1))
                last.then_inc(S["up_done" if m else "gate_done"], 1)

            def hidden_T(t, p):
                pe.wait_ge(S["hidden_ready"], t + 1)
                if not (isinstance(t, int) and t < 1):
                    pe.wait_ge(S["hT_ready"], t)
                for f in range(FC):
                    last = tr(bank[4][:, 128 * f:128 * f + 128], hidden[:, p, 128 * f:128 * f + 128], ident)
                last.then_inc(S["hT_done"], 1)

            def down(t, e):
                pe.wait_ge(S["hT_ready"], t + 1)
                if not (isinstance(t, int) and t < 1):
                    pe.wait_ge(S["y_out_ready"], t)
                for f in range(FC):
                    last = mm(bank[6][:, 0:C], hiddenT[:, 128 * f:128 * f + 128], down_all[:, bass.ds(e * DN + f * C, C)],
                              start=(f == 0), stop=(f == FC - 1))
                last.then_inc(S["down_done"], 1)

            def expert(t):
                return pe.value_load(expert_i[0:1, bass.ds(t, 1)], min_val=0, max_val=E - 1)

            def step(t, p, half):
                more = not (isinstance(t, int) and t + 1 >= TILES)
                if more:
                    e = expert(t + 1)
                    gate_up(t + 1, 1 - p, 0, e)
                hidden_T(t, p)
                if more:
                    gate_up(t + 1, 1 - p, 1, e)
                if not (isinstance(t, int) and t + 2 >= TILES):
                    tokens_T(t + 2, p, half + 1)
                down(t, expert(t))

            tokens_T(0, 0, 0)
            e0 = expert(0)
            gate_up(0, 0, 0, e0)
            gate_up(0, 0, 1, e0)
            tokens_T(1, 1, 0)
            step(0, 0, 0)
            step(1, 1, 0)
            with pe.Fori(1, (TILES - 3) // 2) as i:
                step(2 * i, 0, i)
                step(2 * i + 1, 1, i)
            for t in range(TILES - 3, TILES):
                step(t, t % 2, t // 2)

            for b in range(B):
                pe.wait_ge(S["mixed"], 2 * b + 2)
                for k in range(2):
                    for h in range(2):
                        last = tr(bank[b][0:CH, 256 * k + 128 * h:256 * k + 128 * h + 128], tok_b[:, 2 * b + h, k * CH:(k + 1) * CH], ident)
                last.then_inc(S["outT_done"], 1)


_NAMES = {"x": "x", "w1": "L0_conv_w1", "b1": "L0_conv_b1", "w2": "L0_conv_w2", "b2": "L0_conv_b2",
          "w_qkv": "L1_attn_w_qkv", "b_qkv": "L1_attn_b_qkv", "w_proj": "L1_attn_w_proj", "b_proj": "L1_attn_b_proj",
          "w_gate": "L1_ffn_w_gate", "expert_bias": "L1_ffn_expert_bias", "wg": "L1_ffn_wg", "wu": "L1_ffn_wu",
          "wd": "L1_ffn_wd", "swg": "L1_ffn_swg", "swu": "L1_ffn_swu", "swd": "L1_ffn_swd"}


def kernel(**inputs):
    import concourse.bacc as bacc
    from concourse.bass_utils import run_bass_kernel_spmd

    nc = bacc.Bacc("TRN2", target_bir_lowering=False, num_devices=1)
    tables = constants()
    arrays = {k: np.ascontiguousarray(inputs[v]) for k, v in _NAMES.items()}
    arrays.update(tables_f32=tables[0], tables_bf16=tables[1])
    aps = {k: nc.dram_tensor(k, v.shape, mybir.dt.from_np(v.dtype), kind="ExternalInput").ap() for k, v in arrays.items()}
    out = nc.dram_tensor("out", [B, C, H, W], F32, kind="ExternalOutput").ap()
    program(nc, aps, out)
    return run_bass_kernel_spmd(nc, [arrays], core_ids=[0]).results[0]["out"]
```

```python
from contextlib import ExitStack

import numpy as np
import concourse.bass as bass
from concourse import mybir

F32 = mybir.dt.float32
BF16 = mybir.dt.bfloat16
F16 = mybir.dt.float16
F32R = mybir.dt.float32r
I32 = mybir.dt.int32
U32 = mybir.dt.uint32
ALU = mybir.AluOpType
ACT = mybir.ActivationFunctionType
AX = mybir.AxisListType

B, C, H, W = 4, 192, 16, 16
N = H * W
TOK = B * N
NT = TOK // 128
CH = C // 2
WF = W // 2 + 1
MODES = H * WF
MA = 80
MB = MODES - MA
BLK = 24
BPH = CH // BLK
LAMBDA = 0.01
HEADS, HD = 12, 16
HPT = HEADS // 2
SCALE = HD ** -0.5
E, TOPK, FF = 16, 2, 384
FC = FF // 128
TILE = 128
TILES = (TOK * TOPK + E * (TILE - 1)) // TILE
SLOTS = TILES * TILE
GU = 2 * 2 * FF
DN = FC * C
EXTRA = 11300
LATE = 14
EPS = 1e-5
NORM_PARTS = (range(0, NT - 2), range(NT - 2, NT))
WQ = 4 * 128 + C
BIAS_SET = 5
MEMBER_STEP = 5 + 2 * NT + 3


def constants():
    h, w = np.meshgrid(np.arange(H), np.arange(W), indexing="ij")
    k1, k2 = np.meshgrid(np.arange(H), np.arange(WF), indexing="ij")
    turn = (np.outer(h.ravel(), k1.ravel()) % H) / H + (np.outer(w.ravel(), k2.ravel()) % W) / W
    angle = 2 * np.pi * turn
    forward = np.concatenate([np.cos(angle), -np.sin(angle)], 1) / np.sqrt(N)
    twice = np.where((k2.ravel() == 0) | (k2.ravel() == W // 2), 1.0, 2.0)[:, None]
    real, imag = twice * np.cos(angle).T / np.sqrt(N), -twice * np.sin(angle).T / np.sqrt(N)
    order = np.arange(N).reshape(N // 4, 4).T.ravel()
    inverse = np.zeros((128, 3, N))
    inverse[:MA, 0], inverse[:MA, 2] = real[:MA, order], imag[:MA, order]
    inverse[:MB, 1], inverse[64:64 + MB, 1] = real[MA:, order], imag[MA:, order]
    p = np.arange(128)
    masks = np.stack([(p // HD == h) | (p == CH + h) for h in range(HPT)], 1) * 1.0
    f = np.concatenate([
        np.eye(128),
        np.tile(np.arange(128), (128, 1)),
        forward.reshape(2, 128, 2 * MODES).transpose(1, 0, 2).reshape(128, -1),
        inverse.reshape(128, -1),
        p[:, None] + 128 * np.repeat(np.arange(NT), TOPK)[None, :],
        masks,
        np.tile(128 * np.arange(32), (128, 1)),
    ], 1).astype(np.float32)
    before = (p[:, None] < p[None, :]) * 1.0
    upto = (p[:, None] <= p[None, :]) * 1.0
    g = np.concatenate([before, np.ones((128, 128)), upto[:, :E]], 1)
    return f, g.astype(mybir.dt.np(BF16))


F_IDENT = 0
F_IOTA = 128
F_FWD = 256
F_INV = F_FWD + 2 * 2 * MODES
F_TOKEN = F_INV + 3 * N
F_MASK = F_TOKEN + NT * TOPK
F_TILE0 = F_MASK + HPT
F_ALL = F_TILE0 + 32


def program(nc, a, out):
    ctx = ExitStack()
    with ctx:
        def sb(name, shape, dt=F32):
            return ctx.enter_context(nc.sbuf_tensor(name, shape, dt))

        def sem(name):
            return ctx.enter_context(nc.semaphore(name))

        xhat_rows = nc.dram_tensor("xhat_rows", [TOK, C], F32).ap()
        slot_rows = nc.dram_tensor("slot_rows", [SLOTS, C], F32).ap()

        cf = sb("cf", [128, F_ALL])
        cb = sb("cb", [128, 256 + E], BF16)
        ident = cf[:, F_IDENT:F_IDENT + 128]
        iota = cf[:, F_IOTA:F_IOTA + 128]
        fwd = cf[:, F_FWD:F_INV].rearrange("p (k m) -> p k m", k=2)
        inv = cf[:, F_INV:F_TOKEN].rearrange("p (k n) -> p k n", k=3)
        token_id = cf[:, F_TOKEN:F_MASK]
        mask = cf[:, F_MASK:F_TILE0]
        tile_start = cf[0:E, F_TILE0:F_ALL]
        before, ones, upto = cb[:, 0:128], cb[:, 128:256], cb[0:E, 256:256 + E]

        down_all = sb("down_all", [128, E * DN])
        shared_gu = sb("shared_gu", [128, GU])
        shared_dn = sb("shared_dn", [128, DN])
        tok = sb("tok", [128, NT, C])
        tok_b = sb("tok_b", [128, NT, C])
        with nc.sbuf_tensor("rounded", [128, E * GU + EXTRA], F32R) as rounded:
            pass
        main = sb("main", [128, E * GU + EXTRA])
        at = [(E - LATE) * GU]

        def carve(cols, start=None):
            at[0] = (at[0] if start is None else start) + cols
            assert at[0] <= E * GU + EXTRA, at[0]
            return main[:, at[0] - cols:at[0]]

        def carve_r(cols):
            carve(cols)
            return rounded[:, at[0] - cols:at[0]]

        pix = carve(B * 2 * C, (E - LATE) * GU).rearrange("p (b k c) -> p b k c", b=B, k=2)
        x_res = carve(2 * 768).rearrange("p (q f) -> p q f", q=2)
        spec = carve(4 * B * MODES).rearrange("p (g r m) -> p g r m", g=2, r=2)
        hid = carve(4 * B * MODES).rearrange("p (g r m) -> p g r m", g=2, r=2)
        y = carve(B * 3 * C).rearrange("p (b k c) -> p b k c", b=B, k=3)
        w1 = carve(6 * CH).rearrange("p (g s o) -> p g s o", g=2, s=3)
        w2 = carve(6 * CH).rearrange("p (g s o) -> p g s o", g=2, s=3)
        b1 = carve(4).rearrange("p (g r) -> p g r", g=2)
        b2 = carve(3 * C).rearrange("p (k c) -> p k c", k=3)
        img = carve(2 * 768).rearrange("p (q f) -> p q f", q=2)
        biased = carve(2 * 2 * C).rearrange("p (s b c) -> p s b c", s=2, b=2)
        clipped = carve(2 * 2 * C).rearrange("p (s b c) -> p s b c", s=2, b=2)
        wgate = sb("wgate", [128, 2, E])
        carve(0, E * GU)
        xT = [carve_r(B * 2 * N).rearrange("p (b k n) -> p b k n", b=B, k=2) for _ in range(2)]
        after_xT = at[0]
        carve(0, (E - LATE) * GU)
        q_sb = [carve_r(2 * 2 * N).rearrange("p (s t n) -> p s t n", s=2, t=2) for _ in range(2)]
        k_all = [carve_r(2 * N).rearrange("p (t n) -> p t n", t=2) for _ in range(2)]
        k_sb = [carve_r(2 * HEADS * N).rearrange("p (s t h n) -> p s t h n", s=2, t=2, h=HPT) for _ in range(2)]
        negmax = carve(2 * 2 * (CH + HPT)).rearrange("p (t q f) -> p t q f", t=2, q=2)
        v_sb = carve(2 * 2 * HEADS * 32).rearrange("p (s k h d) -> p s k h d", s=2, k=2, h=HEADS)
        probs_flat = carve(2 * 8 * N)
        assert at[0] <= E * GU
        carve(0, after_xT)
        probs = probs_flat.rearrange("p (s k h n) -> p s k h n", s=2, k=2, h=4)
        o_sb = carve(2 * 3 * N).rearrange("p (s j n) -> p s j n", s=2, j=3)
        xhat = probs_flat[:, 0:NT * C].rearrange("p (t c) -> p t c", t=NT)
        recip = carve(2 * N).rearrange("p (s n) -> p s n", s=2)
        den = recip
        stats = carve(NT * 6).rearrange("p (t s) -> p t s", t=NT)
        meanvar = carve(NT * 2).rearrange("p (t s) -> p t s", t=NT)
        std = carve(NT)
        rstd = carve(NT)
        eps_col = sb("eps_col", [128, 1])[:, :]
        warm = sb("warm", [128, 1])[:, :]
        wqkv_raw = carve(2 * WQ).rearrange("p (k n) -> p k n", k=2)
        wqkv = [carve_r(2 * WQ).rearrange("p (k n) -> p k n", k=2) for _ in range(2)]
        wproj = carve(3 * C).rearrange("p (j n) -> p j n", j=3)
        bproj = carve(C)
        x2T = carve(B * 2 * N, E * GU).rearrange("p (b k n) -> p b k n", b=B, k=2)
        xhat2 = carve(NT * C).rearrange("p (t c) -> p t c", t=NT)
        assert at[0] <= after_xT
        carve(0, after_xT)
        hid_s = carve(FC * 512).rearrange("p (f n) -> p f n", f=FC)
        silu_s = [carve(512) for _ in range(2)]
        weight = carve(NT * TOPK).rearrange("p (t k) -> p t k", t=NT)
        slot_i = carve(NT * TOPK).bitcast(I32)
        slot_token = carve(32).bitcast(U32)
        expert_i = carve(32).bitcast(I32)
        temporary = at[0]
        logit = carve(NT * E).rearrange("p (t e) -> p t e", t=NT)
        prob = carve(NT * E).rearrange("p (t e) -> p t e", t=NT)
        small = carve(NT * 4).rearrange("p (s t) -> p s t", s=4)
        top = carve(NT * 8).rearrange("p (t k) -> p t k", t=NT)
        top_i = carve(NT * 8).bitcast(U32).rearrange("p (t k) -> p t k", t=NT)
        top_f = carve(NT * TOPK).rearrange("p (t k) -> p t k", t=NT)
        chosen = carve(NT * TOPK * E).rearrange("p (t k e) -> p t k e", t=NT, k=TOPK)
        member = carve(NT * E // 2).bitcast(BF16).rearrange("p (t e) -> p t e", t=NT)
        at_slot = carve(NT * TOPK * E).rearrange("p (t k e) -> p t k e", t=NT, k=TOPK)
        slot_f = carve(NT * TOPK)
        part_i = carve(NT * TOPK).bitcast(I32)
        tile_i = carve(NT * TOPK).bitcast(I32)
        part_f = carve(NT * TOPK)
        tile_f = carve(NT * TOPK)
        count_i = carve(128).bitcast(I32)
        padded_i = carve(128).bitcast(I32)
        padded = carve(64).bitcast(BF16)
        ended = carve(16).bitcast(BF16)
        is_part = carve(NT * TOPK * 64).bitcast(F16).rearrange("p (s q) -> p s q", s=NT * TOPK)
        is_tile = carve(NT * TOPK * 32).rearrange("p (s q) -> p s q", s=NT * TOPK)
        id_tile = carve(NT * TOPK * 16).bitcast(F16).rearrange("p (s q) -> p s q", s=NT * TOPK)
        xg = carve(2 * C, E * GU + B * 2 * N).rearrange("p (s c) -> p s c", s=2)
        xgT = carve(2 * 256).rearrange("p (s k n) -> p s k n", s=2, k=2)
        silu = carve(2 * FF).rearrange("p (s f) -> p s f", s=2)
        assert at[0] <= after_xT
        hidden = carve(2 * FF, temporary).rearrange("p (s f) -> p s f", s=2)
        hiddenT = carve(FF)
        y_out = carve(2 * C).rearrange("p (s c) -> p s c", s=2)
        y_back = carve(NT * TOPK * C, 0).rearrange("p (t k c) -> p t k c", t=NT, k=TOPK)
        out_T = carve(B * 2 * N).rearrange("p (b k n) -> p b k n", b=B, k=2)

        gu_e = lambda e: main[0:CH, bass.ds(e * GU, GU)].rearrange("p (k f) -> p k f", k=2)
        dn_e = lambda e: down_all[:, bass.ds(e * DN, DN)].rearrange("p (k c) -> p k c", k=FC)

        bank = [ctx.enter_context(nc.psum_tensor(f"bank{i}", [128, 512], F32)) for i in range(8)]

        names = """ld_const ld_pix ld_spec ld_res ld_attn ld_qkv ld_shared ld_experts ld_late
        zeroed w_zeroed padded_rows w_split bias_zeroed eps_set negated
        spec_done spec_act spec_dve hid_done hid_ready y_done y_biased y_clipped y_ready img_done img_ready
        tok_done tok_ready tok_b_ready stats_ready mv_ready std_ready rstd_ready xhat_ready
        xT_done xT_high xT_low qk_done v_done q_high q_low k_high k_low k_masked_pool k_masked_dve v_ready smax_done smax_ready rT_done qmax_ready
        st_done exp_ready pv_done recip_ready den_ready norm_ready proj_done attn_ready
        stats2 mv2 std2 rstd2 xhat2_ready xhat2_stored x2T_done x2T_ready
        logits_done exp_logit_ready route rank_done count_done base_done end_done row_done inv_done
        padded_ready ended_ready onehot_ready expert_ready slot_token_ready
        sg_done su_done silu_s_ready hid_s_ready shared_done shared_ready
        xg_done xgT_ready gate_done up_done silu_ready hidden_ready hT_done hT_ready down_done y_out_ready
        mixed half_mixed outT_done outT_ready stored""".split()
        S = {n: sem(n) for n in names}
        gathered = [sem(f"gathered{p}") for p in range(2)]
        y_stored = [sem(f"y_stored{p}") for p in range(2)]
        back = [sem(f"back{i}") for i in range(NT)]
        block = ctx.enter_context(nc.Block())

        def one_head_keys(engine, b, part, t):
            return engine.tensor_tensor(k_sb[part][:, b % 2, t], k_all[part][:, t, :].bitcast(F32).unsqueeze(1).broadcast_to([128, HPT, N]),
                                        mask.unsqueeze(2).broadcast_to([128, HPT, N]), ALU.mult)

        def max_units(b, u):
            upto = lambda v: max(0, min(12, -(-12 * (v - 3) // 8)))
            return range(upto(u), upto(u + 1)) if b + 1 < B else range(0)

        @block.sync
        def _(sp):
            sp.dma_start(cf[:, :], a["tables_f32"]).then_inc(S["ld_const"], 16)
            sp.dma_start(pix, a["x"].rearrange("b c h w -> b (c h w)")
                         .rearrange("b (k p c) -> p b k c", k=2, p=128)).then_inc(S["ld_pix"], 16)
            sp.dma_start(cb[:, :], a["tables_bf16"]).then_inc(S["ld_attn"], 16)
            sp.dma_start(x_res, a["x"].rearrange("b c h w -> (b c h w)")
                         .rearrange("(q p f) -> p q f", q=2, p=128)).then_inc(S["ld_res"], 16)
            sp.wait_ge(S["w_zeroed"], 3)
            for m in range(2):
                for k in range(2):
                    sp.dma_start(wqkv_raw[0:CH, k, 256 * m:256 * m + 256].rearrange("p (t n) -> p t n", t=2)[:, :, 0:CH],
                                 a["w_qkv"][k * CH:(k + 1) * CH, m * C:(m + 1) * C].rearrange("p (t n) -> p t n", t=2)).then_inc(S["ld_qkv"], 16)
                sp.dma_start(wqkv_raw[CH:CH + 1, 1, 256 * m:256 * m + 256].rearrange("p (t n) -> p t n", t=2)[:, :, 0:CH],
                             a["b_qkv"][m * C:(m + 1) * C].rearrange("(t n) -> t n", t=2).unsqueeze(0)).then_inc(S["ld_qkv"], 16)
            sp.dma_start(wqkv_raw[0:CH, :, 512:WQ], a["w_qkv"][:, 2 * C:3 * C].rearrange("(k p) n -> p k n", k=2)).then_inc(S["ld_qkv"], 16)
            sp.dma_start(wqkv_raw[CH:CH + 1, 1, 512:WQ], a["b_qkv"][2 * C:3 * C].unsqueeze(0)).then_inc(S["ld_qkv"], 16)
            for r in range(4):
                sp.dma_start(wproj[32 * r:32 * r + HD, :, :],
                             a["w_proj"].rearrange("(j r d) n -> r d j n", r=4, d=HD)[r]).then_inc(S["ld_attn"], 16)
            sp.dma_start(bproj[:, :], a["b_proj"].partition_broadcast(128)).then_inc(S["ld_attn"], 16)
            sp.dma_start(wgate[0:CH, :, :], a["w_gate"].rearrange("(k p) n -> p k n", k=2)).then_inc(S["ld_attn"], 16)
            sp.dma_start(wgate[CH:CH + 1, 1, :], a["expert_bias"].unsqueeze(0)).then_inc(S["ld_attn"], 16)
            sg = shared_gu[0:CH, :].rearrange("p (k f) -> p k f", k=2)
            sp.dma_start(sg[:, :, 0:FF], a["swg"].rearrange("(k p) f -> p k f", k=2)).then_inc(S["ld_shared"], 16)
            sp.dma_start(sg[:, :, FF:], a["swu"].rearrange("(k p) f -> p k f", k=2)).then_inc(S["ld_shared"], 16)
            sp.dma_start(shared_dn[:, :].rearrange("p (k c) -> p k c", k=FC),
                         a["swd"].rearrange("(k p) c -> p k c", k=FC)).then_inc(S["ld_shared"], 16)
            for e in range(E - LATE):
                sp.dma_start(gu_e(e)[:, :, 0:FF], a["wg"][e].rearrange("(k p) f -> p k f", k=2)).then_inc(S["ld_experts"], 16)
                sp.dma_start(gu_e(e)[:, :, FF:], a["wu"][e].rearrange("(k p) f -> p k f", k=2)).then_inc(S["ld_experts"], 16)
            for e in range(E):
                sp.dma_start(dn_e(e), a["wd"][e].rearrange("(k p) c -> p k c", k=FC)).then_inc(S["ld_experts"], 16)
            sp.wait_ge(S["attn_ready"], B)
            sp.wait_ge(S["xhat2_ready"], NT)
            for e in range(E - LATE, E):
                sp.dma_start(gu_e(e)[:, :, 0:FF], a["wg"][e].rearrange("(k p) f -> p k f", k=2)).then_inc(S["ld_late"], 16)
                sp.dma_start(gu_e(e)[:, :, FF:], a["wu"][e].rearrange("(k p) f -> p k f", k=2)).then_inc(S["ld_late"], 16)

            def store(t, p):
                sp.wait_ge(S["y_out_ready"], t + 1)
                sp.dma_start(slot_rows[bass.ds(t * TILE, TILE), :], y_out[:, p, :]).then_inc(y_stored[p], 16)

            with sp.Fori(0, TILES // 2) as i:
                store(2 * i, 0)
                store(2 * i + 1, 1)
            store(TILES - 1, 0)
            for b in range(B):
                sp.wait_ge(S["outT_ready"], b + 1)
                sp.dma_start(out[b].rearrange("(k p) h w -> p k (h w)", k=2), out_T[0:CH, b]).then_inc(S["stored"], 16)
            sp.wait_ge(S["stored"], 16 * B)

        @block.gpsimd
        def _(pool):
            nc.gpsimd.memset(w1, 0.0).then_inc(S["zeroed"], 1)
            nc.gpsimd.memset(w2, 0.0).then_inc(S["zeroed"], 1)
            nc.gpsimd.memset(wqkv_raw, 0.0).then_inc(S["w_zeroed"], 1)
            nc.gpsimd.memset(wproj, 0.0).then_inc(S["w_zeroed"], 1)
            pool.wait_ge(S["zeroed"], 2)
            pool.wait_ge(S["w_zeroed"], 2)
            nc.gpsimd.memset(spec[CH:, :, :, :], 0.0).then_inc(S["padded_rows"], 1)
            nc.gpsimd.memset(hid[CH:, :, :, :], 0.0).then_inc(S["padded_rows"], 1)
            pool.wait_ge(S["padded_rows"], 2)
            nc.gpsimd.memset(y, 0.0).then_inc(S["padded_rows"], 1)
            pool.wait_ge(S["padded_rows"], 3)
            nc.gpsimd.memset(wqkv_raw[CH:CH + 1, 1, 256:512].rearrange("p (t n) -> p t n", t=2)[:, :, CH:CH + HPT], 1.0).then_inc(S["w_zeroed"], 1)
            pool.wait_ge(S["img_ready"], 4)
            pool.wait_ge(S["tok_done"], 4)
            for i, (part, value) in enumerate(((xT[0][CH:, :, :, :], 0.0), (xT[0][CH:CH + 1, :, 1, :], 1.0), (xT[1][CH:, :, :, :], 0.0),
                                               (v_sb, 1.0), (negmax, 0.0))):
                nc.gpsimd.memset(part.bitcast(F32), value).then_inc(S["bias_zeroed"], 1)
                pool.wait_ge(S["bias_zeroed"], i + 1)
            pool.wait_ge(S["tok_ready"], B)
            pool.wait_ge(S["ld_attn"], 8 * 16)
            nc.gpsimd.tensor_tensor(tok_b[:, :, :], tok[:, :, :],
                                    bproj[:, :].unsqueeze(1).broadcast_to([128, NT, C]), ALU.add).then_inc(S["tok_b_ready"], 1)
            for b in range(B):
                if b >= 2:
                    pool.wait_ge(S["st_done"], 12 * (b - 1))
                for part, t in ((0, 0), (1, 0), (1, 1)):
                    pool.wait_ge(S["k_high"] if part == 0 else S["k_low"], b + 1)
                    one_head_keys(nc.gpsimd, b, part, t).then_inc(S["k_masked_pool"], 1)
            pool.wait_ge(S["v_done"], B)
            pool.wait_ge(S["k_masked_pool"], 3 * B)
            nc.gpsimd.memset(x2T[CH:CH + 1, :, :, :], 1.0).then_inc(S["bias_zeroed"], 1)
            for t in range(NT):
                pool.wait_ge(S["xhat2_ready"], t + 1)
                pool.dma_start(xhat_rows[128 * t:128 * t + 128, :], xhat2[:, t, :]).then_inc(S["xhat2_stored"], 16)
            pool.wait_ge(S["xhat2_stored"], 16 * NT)
            pool.wait_ge(S["slot_token_ready"], 1)
            for t in range(TILES):
                if t >= 2:
                    pool.wait_ge(S["xg_done"], t - 1)
                pool.indirect_dma_start(xg[:, t % 2, :], None, xhat_rows,
                                        bass.IndirectOffsetOnAxis(ap=slot_token[:, t:t + 1], axis=0)).then_inc(gathered[t % 2], 16)
            pool.wait_ge(y_stored[0], 16 * ((TILES + 1) // 2))
            pool.wait_ge(y_stored[1], 16 * (TILES // 2))
            for t in range(NT):
                for k in range(TOPK):
                    j = t * TOPK + k
                    pool.indirect_dma_start(y_back[:, t, k, :], None, slot_rows,
                                            bass.IndirectOffsetOnAxis(ap=slot_i[:, j:j + 1].bitcast(U32), axis=0)).then_inc(back[t], 16)

        @block.scalar
        def _(act):
            act.wait_ge(S["zeroed"], 2)
            for dst, src in ((w1, a["w1"]), (w2, a["w2"])):
                for r in range(2):
                    for k in range(BPH):
                        act.dma_start(dst[BLK * k:BLK * k + BLK, :, r, BLK * k:BLK * k + BLK],
                                      src[r].rearrange("(g k) i o -> k i g o", k=BPH)[k]).then_inc(S["ld_spec"], 16)
            with nc.allow_non_contiguous_dma(reason="a bias per channel"):
                for r in range(2):
                    act.dma_start(b1[0:CH, :, r], a["b1"][r].rearrange("(g k) o -> (k o) g", g=2)).then_inc(S["ld_spec"], 16)
            for dst, r in ((b2[0:MA, 0], 0), (b2[0:MA, 2], 1), (b2[0:MB, 1], 0), (b2[64:64 + MB, 1], 1)):
                act.dma_start(dst, a["b2"][r].rearrange("n o -> (n o)").partition_broadcast(dst.shape[0])).then_inc(S["ld_spec"], 16)
            for b in range(B):
                act.wait_ge(S["spec_done"], 2 * b + 1)
                act.activation(spec[0:CH, 0, :, b * MODES:(b + 1) * MODES],
                               bank[2 * b % 4][0:CH, 0:2 * MODES].rearrange("p (r m) -> p r m", r=2), ACT.Copy).then_inc(S["spec_act"], 1)
            act.wait_ge(S["ld_spec"], 22 * 16)
            for v in range(8):
                bp, g, r = v // 4, v // 2 % 2, v % 2
                act.wait_ge(S["hid_done"], v + 1)
                act.activation(hid[0:CH, g, r, bp * 2 * MODES:(bp + 1) * 2 * MODES],
                               bank[4 + v % 4][0:CH, 0:2 * MODES], ACT.Relu, bias=b1[0:CH, g, r:r + 1]).then_inc(S["hid_ready"], 1)
            for s in range(4):
                pair, h = s // 2, s % 2
                act.wait_ge(S["tok_done"], s + 1)
                dst = tok[:, 4 * pair + h:4 * pair + h + 3:2, :].rearrange("p b (g i) -> p b g i", i=3)
                src = bank[s][:, 0:3 * 128].rearrange("p (i b g) -> p b g i", i=3, b=2)
                act.activation(dst, src, ACT.Copy).then_inc(S["tok_ready"], 1)
            act.wait_ge(S["eps_set"], 1)
            act.activation(warm, eps_col, ACT.Sqrt)
            act.wait_ge(S["mv_ready"], NT)
            act.activation(std, meanvar[:, :, 1], ACT.Sqrt, bias=eps_col).then_inc(S["std_ready"], 1)
            for b in range(B):
                act.wait_ge(S["xT_done"], b + 1)
                act.activation(xT[0][0:CH, b, :, :], bank[4 + b][0:CH, :].rearrange("p (k n) -> p k n", k=2), ACT.Copy).then_inc(S["xT_high"], 1)

            def high_parts(b):
                act.wait_ge(S["qk_done"], b + 1)
                if b >= 1:
                    act.wait_ge(S["k_masked_pool"], 3 * b)
                    act.wait_ge(S["k_masked_dve"], b)
                act.activation(k_all[0], bank[1][:, :].rearrange("p (t n) -> p t n", t=2), ACT.Copy).then_inc(S["k_high"], 1)
                if b >= 2:
                    act.wait_ge(S["st_done"], 12 * (b - 1))
                act.activation(q_sb[0][:, b % 2], bank[0][:, :].rearrange("p (t n) -> p t n", t=2), ACT.Copy).then_inc(S["q_high"], 1)

            def values(b):
                if b == 0:
                    act.wait_ge(S["bias_zeroed"], BIAS_SET)
                act.wait_ge(S["v_done"], b + 1)
                if b >= 2:
                    act.wait_ge(S["pv_done"], 3 * (b - 1))
                act.activation(v_sb[:, b % 2, :, :, 0:HD],
                               bank[5][:, 0:2 * C].rearrange("p (k h d) -> p k h d", k=2, d=HD), ACT.Copy).then_inc(S["v_ready"], 1)

            def second_norm(part, tiles):
                act.wait_ge(S["mv2"], tiles.stop)
                act.activation(std[:, tiles.start:tiles.stop], meanvar[:, tiles.start:tiles.stop, 1], ACT.Sqrt, bias=eps_col).then_inc(S["std2"], 1)

            def tokens_for_experts(b):
                act.wait_ge(S["x2T_done"], b + 1)
                act.activation(x2T[0:CH, b, :, :], bank[b % 2][0:CH, :].rearrange("p (k n) -> p k n", k=2), ACT.Copy).then_inc(S["x2T_ready"], 1)

            def shared_silu(u):
                act.wait_ge(S["sg_done"], u + 1)
                if u >= 2:
                    act.wait_ge(S["hid_s_ready"], u - 1)
                act.activation(silu_s[u % 2], bank[u % 2][:, :], ACT.Silu).then_inc(S["silu_s_ready"], 1)

            high_parts(0)
            values(0)
            for b in range(B):
                if b + 1 < B:
                    high_parts(b + 1)
                    values(b + 1)
                for j in range(3):
                    quad = 3 * b + j
                    if quad >= 2:
                        act.wait_ge(S["pv_done"], quad - 1)
                    for u in range(4):
                        n = 4 * quad + u
                        act.wait_ge(S["st_done"], n + 1)
                        act.activation(probs[:, quad % 2, u // 2, 2 * (u % 2):2 * (u % 2) + 2, :],
                                       bank[2 + n % 3][:, :].rearrange("p (h n) -> p h n", h=2), ACT.Exp).then_inc(S["exp_ready"], 1)
                    if quad == 3 * B - 2:
                        second_norm(0, NORM_PARTS[0])
            act.activation(warm, eps_col, ACT.Sqrt)
            for b in range(B - 1):
                tokens_for_experts(b)
            second_norm(1, NORM_PARTS[1])
            act.activation(warm, eps_col, ACT.Exp)
            tokens_for_experts(B - 1)
            act.wait_ge(S["route"], 2)
            act.activation(prob, logit, ACT.Exp).then_inc(S["exp_logit_ready"], 1)
            for u in range(FC):
                shared_silu(u)


            def columns(t, p):
                act.wait_ge(S["xg_done"], t + 1)
                if not (isinstance(t, int) and t < 2):
                    act.wait_ge(S["up_done"], t - 1)
                act.activation(xgT[0:CH, p, :, :], bank[5][0:CH, 0:256].rearrange("p (k n) -> p k n", k=2), ACT.Copy).then_inc(S["xgT_ready"], 1)

            def gate(t, p):
                act.wait_ge(S["gate_done"], t + 1)
                if not (isinstance(t, int) and t < 2):
                    act.wait_ge(S["hidden_ready"], t - 1)
                act.activation(silu[:, p, :], bank[p][:, 0:FF], ACT.Silu).then_inc(S["silu_ready"], 1)

            def hidden_columns(t):
                act.wait_ge(S["hT_done"], t + 1)
                if not (isinstance(t, int) and t < 1):
                    act.wait_ge(S["down_done"], t)
                act.activation(hiddenT, bank[4][:, 0:FF], ACT.Copy).then_inc(S["hT_ready"], 1)

            def step(t, p):
                if not (isinstance(t, int) and t + 1 >= TILES):
                    gate(t + 1, 1 - p)
                hidden_columns(t)
                if not (isinstance(t, int) and t + 2 >= TILES):
                    columns(t + 2, p)

            columns(0, 0)
            gate(0, 0)
            columns(1, 1)
            step(0, 0)
            step(1, 1)
            with act.Fori(1, (TILES - 3) // 2) as i:
                step(2 * i, 0)
                step(2 * i + 1, 1)
            for t in range(TILES - 3, TILES):
                step(t, t % 2)
            for u in range(FC, 2 * FC):
                shared_silu(u)
            for b in range(B):
                act.wait_ge(S["outT_done"], b + 1)
                act.activation(out_T[0:CH, b, :, :], bank[b][0:CH, :].rearrange("p (k n) -> p k n", k=2), ACT.Copy).then_inc(S["outT_ready"], 1)

        @block.vector
        def _(dve):
            vec = nc.vector
            vec.memset(eps_col, EPS).then_inc(S["eps_set"], 1)
            dve.wait_ge(S["ld_spec"], 22 * 16)
            for w in (w1, w2):
                vec.tensor_scalar(w[0:CH, :, 2, :], w[0:CH, :, 1, :], -1.0, None, ALU.mult).then_inc(S["negated"], 1)
            dve.wait_ge(S["ld_qkv"], 8 * 16)
            for cols, scale in ((slice(0, 256), SCALE), (slice(256, WQ), 1.0)):
                vec.tensor_scalar(wqkv[0][:, :, cols], wqkv_raw[:, :, cols], scale, None, ALU.mult).then_inc(S["w_split"], 1)
            dve.wait_ge(S["w_split"], 2)
            for cols, scale in ((slice(0, 256), SCALE), (slice(256, WQ), 1.0)):
                vec.scalar_tensor_tensor(wqkv[1][:, :, cols], wqkv_raw[:, :, cols], scale, wqkv[0][:, :, cols].bitcast(F32),
                                         ALU.mult, ALU.subtract).then_inc(S["w_split"], 1)
            for b in range(B):
                dve.wait_ge(S["spec_done"], 2 * b + 2)
                vec.tensor_copy(spec[0:CH, 1, :, b * MODES:(b + 1) * MODES],
                                bank[(2 * b + 1) % 4][0:CH, 0:2 * MODES].rearrange("p (r m) -> p r m", r=2)).then_inc(S["spec_dve"], 1)
            for u in range(6):
                bp, k, s = u // 3, u % 3, u % 2
                rows = slice(0, 128 if k == 1 else MA)
                dve.wait_ge(S["y_done"], u + 1)
                vec.tensor_tensor(biased[rows, s], bank[u % 4][rows, 0:2 * C].rearrange("p (b c) -> p b c", b=2),
                                  b2[rows, k].unsqueeze(1).broadcast_to([rows.stop, 2, C]), ALU.add).then_inc(S["y_biased"], 1)
                dve.wait_ge(S["y_biased"], u + 1)
                vec.tensor_scalar(clipped[rows, s], biased[rows, s], LAMBDA, -LAMBDA, ALU.min, ALU.max).then_inc(S["y_clipped"], 1)
                dve.wait_ge(S["y_clipped"], u + 1)
                vec.tensor_tensor(y[rows, 2 * bp:2 * bp + 2, k, :], biased[rows, s], clipped[rows, s], ALU.subtract).then_inc(S["y_ready"], 1)
            dve.wait_ge(S["ld_res"], 16)
            for z in range(4):
                pair, jj = z // 2, z % 2
                dve.wait_ge(S["img_done"], z + 1)
                vec.tensor_tensor(img[:, pair, 384 * jj:384 * jj + 384], bank[4 + z][:, 0:384],
                                  x_res[:, pair, 384 * jj:384 * jj + 384], ALU.add).then_inc(S["img_ready"], 1)

            def statistics(tiles, sem_stats, sem_mv, ready):
                for t in tiles:
                    ready(t)
                    vec.bn_stats(stats[:, t, :], tok[:, t, :]).then_inc(S[sem_stats], 1)
                for t in tiles:
                    dve.wait_ge(S[sem_stats], t + 1)
                    vec.bn_aggr(meanvar[:, t, :], stats[:, t, :]).then_inc(S[sem_mv], 1)

            def normal(tiles, dst, part, sem_std, sem_rstd, sem_out):
                dve.wait_ge(S[sem_std], part + 1)
                vec.reciprocal(rstd[:, tiles.start:tiles.stop], std[:, tiles.start:tiles.stop]).then_inc(S[sem_rstd], 1)
                dve.wait_ge(S[sem_rstd], part + 1)
                for t in tiles:
                    vec.tensor_scalar(dst[:, t, :], tok[:, t, :], meanvar[:, t, 0:1], rstd[:, t:t + 1],
                                      ALU.subtract, ALU.mult).then_inc(S[sem_out], 1)

            statistics(range(NT), "stats_ready", "mv_ready", lambda t: dve.wait_ge(S["tok_ready"], 2 * (t // 4) + t % 2 + 1))
            normal(range(NT), xhat, 0, "std_ready", "rstd_ready", "xhat_ready")
            for b in range(B):
                dve.wait_ge(S["xT_high"], b + 1)
                vec.tensor_tensor(xT[1][0:CH, b, :, :], bank[4 + b][0:CH, :].rearrange("p (k n) -> p k n", k=2),
                                  xT[0][0:CH, b, :, :].bitcast(F32), ALU.subtract).then_inc(S["xT_low"], 1)

            def low_parts(b):
                dve.wait_ge(S["k_high"], b + 1)
                if b >= 1:
                    dve.wait_ge(S["k_masked_pool"], 3 * b)
                vec.tensor_tensor(k_all[1], bank[1][:, :].rearrange("p (t n) -> p t n", t=2), k_all[0].bitcast(F32), ALU.subtract).then_inc(S["k_low"], 1)
                if b >= 2:
                    dve.wait_ge(S["st_done"], 12 * (b - 1))
                dve.wait_ge(S["q_high"], b + 1)
                vec.tensor_tensor(q_sb[1][:, b % 2], bank[0][:, :].rearrange("p (t n) -> p t n", t=2), q_sb[0][:, b % 2].bitcast(F32),
                                  ALU.subtract).then_inc(S["q_low"], 1)
                one_head_keys(vec, b, 0, 1).then_inc(S["k_masked_dve"], 1)

            def maxima(b, units):
                for u in units:
                    n, qh, g6 = 12 * b + u, u // 6, u % 6
                    if b >= 1 and u == 0:
                        dve.wait_ge(S["rT_done"], b)
                    dve.wait_ge(S["smax_done"], n + 1)
                    col = CH + 2 * g6 % HPT
                    vec.tensor_reduce(negmax[:, g6 // 3, qh, col:col + 2], bank[n % 2][:, :].rearrange("p (h n) -> p h n", h=2),
                                      AX.X, ALU.max, negate=True).then_inc(S["smax_ready"], 1)

            def maxima_to_queries(b):
                dve.wait_ge(S["rT_done"], b + 1)
                dve.wait_ge(S["q_high"], b + 1)
                vec.tensor_copy(q_sb[0][CH:CH + HPT, b % 2], bank[5][CH:CH + HPT, :].rearrange("p (t n) -> p t n", t=2)).then_inc(S["qmax_ready"], 1)

            def normalise(quad):
                b, j, s = quad // 3, quad % 3, quad % 2
                dve.wait_ge(S["pv_done"], quad + 1)
                vec.reciprocal(recip[:, s], bank[6 + s][:, 0:N]).then_inc(S["recip_ready"], 1)
                dve.wait_ge(S["recip_ready"], quad + 1)
                vec.stream_shuffle(den[:, s], recip[:, s], [HD + i % HD for i in range(32)]).then_inc(S["den_ready"], 1)
                dve.wait_ge(S["den_ready"], quad + 1)
                if b >= 2 and j == 0:
                    dve.wait_ge(S["proj_done"], b - 1)
                vec.tensor_tensor(o_sb[:, b % 2, j], bank[6 + s][:, 0:N], den[:, s], ALU.mult).then_inc(S["norm_ready"], 1)

            def add_attention(b):
                dve.wait_ge(S["proj_done"], b + 1)
                if b == 0:
                    dve.wait_ge(S["tok_b_ready"], 1)
                vec.tensor_tensor(tok[:, 2 * b:2 * b + 2, :], tok_b[:, 2 * b:2 * b + 2, :],
                                  bank[5][:, 0:2 * C].rearrange("p (h c) -> p h c", h=2), ALU.add).then_inc(S["attn_ready"], 1)

            low_parts(0)
            maxima(0, range(12))
            for b in range(B):
                maxima_to_queries(b)
                if b + 1 < B:
                    low_parts(b + 1)
                if b:
                    normalise(3 * b - 1)
                for u in range(12):
                    maxima(b + 1, max_units(b, u))
                    if b and u == 1:
                        add_attention(b - 1)
                        if b == B - 1:
                            statistics(NORM_PARTS[0], "stats2", "mv2", lambda t: dve.wait_ge(S["attn_ready"], t // 2 + 1))
                    if u in (7, 11):
                        normalise(3 * b + u // 4 - 1)
            normal(NORM_PARTS[0], xhat2, 0, "std2", "rstd2", "xhat2_ready")
            normalise(3 * B - 1)
            add_attention(B - 1)
            statistics(NORM_PARTS[1], "stats2", "mv2", lambda t: dve.wait_ge(S["attn_ready"], t // 2 + 1))
            normal(NORM_PARTS[1], xhat2, 1, "std2", "rstd2", "xhat2_ready")

            def shared_hidden(u):
                dve.wait_ge(S["silu_s_ready"], u + 1)
                dve.wait_ge(S["su_done"], u + 1)
                if u == FC:
                    dve.wait_ge(S["shared_done"], 2)
                vec.tensor_tensor(hid_s[:, u % FC, :], silu_s[u % 2], bank[2 + u % 2][:, :], ALU.mult).then_inc(S["hid_s_ready"], 1)

            def shared_rows(u):
                dve.wait_ge(S["shared_done"], u + 1)
                vec.tensor_tensor(tok_b[:, 2 * u:2 * u + 2, :], tok[:, 2 * u:2 * u + 2, :],
                                  bank[6 + u % 2][:, 0:2 * C].rearrange("p (h c) -> p h c", h=2), ALU.add).then_inc(S["shared_ready"], 1)

            steps = [0]

            def step(instruction):
                steps[0] += 1
                instruction.then_inc(S["route"], 1)
                dve.wait_ge(S["route"], steps[0])

            def per_tile(x, n=E):
                return x.unsqueeze(2).broadcast_to([128, NT, n])

            def put(instruction):
                steps[0] += 1
                instruction.then_inc(S["route"], 1)

            dve.wait_ge(S["logits_done"], 1)
            lg = bank[4][:, 0:NT * E].rearrange("p (t e) -> p t e", t=NT)
            step(vec.tensor_reduce(small[:, 0, :], lg, AX.X, ALU.max))
            step(vec.tensor_tensor(logit, lg, per_tile(small[:, 0, :]), ALU.subtract))
            dve.wait_ge(S["exp_logit_ready"], 1)
            step(vec.reduce_sum(small[:, 1, :], prob, AX.X))
            step(vec.reciprocal(small[:, 2, :], small[:, 1, :]))
            step(vec.tensor_tensor(prob, prob, per_tile(small[:, 2, :]), ALU.mult))
            for t in range(NT):
                put(vec.max(top[:, t, :], prob[:, t, :]))
            for t in range(NT):
                dve.wait_ge(S["route"], steps[0] - NT + 1)
                put(vec.max_index(top_i[:, t, :], top[:, t, :], prob[:, t, :]))
            dve.wait_ge(S["route"], steps[0])
            step(vec.tensor_copy(top_f, top_i[:, :, 0:TOPK]))
            step(vec.tensor_tensor(chosen, iota[:, 0:E].unsqueeze(1).unsqueeze(1).broadcast_to([128, NT, TOPK, E]),
                                   top_f.unsqueeze(3).broadcast_to([128, NT, TOPK, E]), ALU.is_equal))
            step(vec.tensor_tensor(member, chosen[:, :, 0, :], chosen[:, :, 1, :], ALU.add))
            assert steps[0] == MEMBER_STEP
            step(vec.reduce_sum(small[:, 1, :], top[:, :, 0:TOPK], AX.X))
            step(vec.reciprocal(small[:, 2, :], small[:, 1, :]))
            put(vec.tensor_tensor(weight, top[:, :, 0:TOPK], per_tile(small[:, 2, :], TOPK), ALU.mult))
            shared_hidden(0)
            dve.wait_ge(S["count_done"], 1)
            step(vec.tensor_scalar(count_i[0:E, :], bank[4][0:E, 256:384], float(TILE - 1), None, ALU.add))
            step(vec.tensor_scalar(padded_i[0:E, :], count_i[0:E, :], -TILE, None, ALU.bitwise_and))
            vec.tensor_copy(padded[0:E, :], padded_i[0:E, :]).then_inc(S["padded_ready"], 1)
            dve.wait_ge(S["base_done"], 1)
            step(vec.tensor_tensor(at_slot, chosen, bank[5][:, 0:NT * E].rearrange("p (t e) -> p t e", t=NT)
                                   .unsqueeze(2).broadcast_to([128, NT, TOPK, E]), ALU.mult))
            step(vec.reduce_sum(slot_f.rearrange("p (t k) -> p t k", t=NT), at_slot, AX.X))
            step(vec.tensor_copy(slot_i, slot_f))
            step(vec.tensor_scalar(part_i, slot_i, TILE - 1, None, ALU.bitwise_and))
            step(vec.tensor_scalar(tile_i, slot_i, 7, None, ALU.logical_shift_right))
            step(vec.tensor_copy(part_f, part_i))
            step(vec.tensor_copy(tile_f, tile_i))
            pairs = NT * TOPK
            put(vec.tensor_tensor(is_part, iota.unsqueeze(1).broadcast_to([128, pairs, 128]),
                                  part_f.unsqueeze(2).broadcast_to([128, pairs, 128]), ALU.is_equal))
            step(vec.tensor_tensor(is_tile, iota[:, 0:32].unsqueeze(1).broadcast_to([128, pairs, 32]),
                                   tile_f.unsqueeze(2).broadcast_to([128, pairs, 32]), ALU.is_equal))
            vec.tensor_tensor(id_tile, is_tile, token_id.unsqueeze(2).broadcast_to([128, pairs, 32]), ALU.mult).then_inc(S["onehot_ready"], 1)
            dve.wait_ge(S["end_done"], 1)
            vec.tensor_tensor(ended[0:E, :], bank[4][0:E, 384:416], tile_start, ALU.is_le).then_inc(S["ended_ready"], 1)
            dve.wait_ge(S["inv_done"], 1)
            vec.tensor_copy(slot_token, bank[5][:, 128:160]).then_inc(S["slot_token_ready"], 1)
            dve.wait_ge(S["row_done"], 1)
            vec.tensor_scalar(expert_i[0:1, :], bank[4][0:1, 448:480], float(E - 1), None, ALU.min).then_inc(S["expert_ready"], 1)
            shared_hidden(1)
            shared_hidden(2)
            shared_rows(0)
            shared_rows(1)

            def hidden_rows(t, p):
                dve.wait_ge(S["silu_ready"], t + 1)
                dve.wait_ge(S["up_done"], t + 1)
                if not (isinstance(t, int) and t < 2):
                    dve.wait_ge(S["hT_done"], t - 1)
                vec.tensor_tensor(hidden[:, p, :], silu[:, p, :], bank[2 + p][:, 0:FF], ALU.mult).then_inc(S["hidden_ready"], 1)

            def down_rows(t, p, half):
                dve.wait_ge(S["down_done"], t + 1)
                if not (isinstance(t, int) and t < 2):
                    dve.wait_ge(y_stored[p], 16 * half)
                vec.tensor_copy(y_out[:, p, :], bank[6][:, 0:C]).then_inc(S["y_out_ready"], 1)

            def expert_step(t, p, half):
                if not (isinstance(t, int) and t + 1 >= TILES):
                    hidden_rows(t + 1, 1 - p)
                down_rows(t, p, half)

            hidden_rows(0, 0)
            expert_step(0, 0, 0)
            expert_step(1, 1, 0)
            with dve.Fori(1, (TILES - 3) // 2) as i:
                expert_step(2 * i, 0, i)
                expert_step(2 * i + 1, 1, i)
            for t in range(TILES - 3, TILES):
                expert_step(t, t % 2, t // 2)

            def mix(t):
                dve.wait_ge(back[t], 16 * TOPK)
                vec.scalar_tensor_tensor(tok[:, t, :], y_back[:, t, 0, :], weight[:, t, 0:1], tok_b[:, t, :], ALU.mult, ALU.add).then_inc(S["half_mixed"], 1)
                dve.wait_ge(S["half_mixed"], t + 1)
                vec.scalar_tensor_tensor(tok_b[:, t, :], y_back[:, t, 1, :], weight[:, t, 1:2], tok[:, t, :], ALU.mult, ALU.add).then_inc(S["mixed"], 1)

            for u in range(FC, 2 * FC):
                shared_hidden(u)
            for t in range(NT // 2):
                mix(t)
            for u in range(NT // 4, NT // 2):
                shared_rows(u)
                dve.wait_ge(S["shared_ready"], u + 1)
                mix(2 * u)
                mix(2 * u + 1)

        @block.tensor
        def _(pe):
            mm, tr = nc.tensor.matmul, nc.tensor.transpose
            pe.wait_ge(S["ld_const"], 16)
            pe.wait_ge(S["ld_pix"], 16)
            for u in range(8):
                b, g = u // 2, u % 2
                if u >= 4:
                    pe.wait_ge(S["spec_dve" if g else "spec_act"], (u - 4) // 2 + 1)
                for k in range(2):
                    last = mm(bank[u % 4][0:CH, 0:2 * MODES], pix[:, b, k, g * CH:(g + 1) * CH], fwd[:, k, :], start=(k == 0), stop=(k == 1))
                last.then_inc(S["spec_done"], 1)
            pe.wait_ge(S["negated"], 2)
            pe.wait_ge(S["padded_rows"], 3)
            for v in range(8):
                bp, g, r = v // 4, v // 2 % 2, v % 2
                pe.wait_ge(S["spec_act"], 2 * (bp + 1))
                pe.wait_ge(S["spec_dve"], 2 * (bp + 1))
                if v >= 4:
                    pe.wait_ge(S["hid_ready"], v - 3)
                cols = slice(bp * 2 * MODES, (bp + 1) * 2 * MODES)
                dst = bank[4 + v % 4][0:CH, 0:2 * MODES]
                mm(dst, w1[:, g, 0, :], spec[:, g, r, cols], start=True, stop=False)
                mm(dst, w1[:, g, 1 if r else 2, :], spec[:, g, 1 - r, cols], start=False, stop=True).then_inc(S["hid_done"], 1)
            for u in range(6):
                bp, k = u // 3, u % 3
                pe.wait_ge(S["hid_ready"], 4 * (bp + 1))
                if u == 0:
                    pe.wait_ge(S["spec_act"], 4)
                    pe.wait_ge(S["spec_dve"], 4)
                if u >= 4:
                    pe.wait_ge(S["y_biased"], u - 3)
                parts = {0: [(0, 0, 0, MA)], 1: [(0, 0, MA, MODES), (64, 1, MA, MODES)], 2: [(0, 1, 0, MA)]}[k]
                for bb in range(2):
                    for g in range(2):
                        for c in range(2):
                            for row, r, m0, m1 in parts:
                                src = hid[:, g, c, (2 * bp + bb) * MODES + m0:(2 * bp + bb) * MODES + m1]
                                sign = 0 if r == c else (1 if r else 2)
                                last = mm(bank[u % 4][row:row + m1 - m0, bb * C + g * CH:bb * C + (g + 1) * CH], src,
                                          w2[:, g, sign, :], start=(c == 0), stop=(c == 1))
                last.then_inc(S["y_done"], 1)
            for z in range(4):
                pair, jj = z // 2, z % 2
                pe.wait_ge(S["y_ready"], 3 * (pair + 1))
                if z == 0:
                    pe.wait_ge(S["hid_ready"], 8)
                for j in range(2):
                    for k in range(3):
                        for bb in range(2):
                            last = mm(bank[4 + z][64 * bb:64 * bb + 64, j * C:(j + 1) * C], inv[:, k, (2 * jj + j) * 64:(2 * jj + j) * 64 + 64],
                                      y[:, 2 * pair + bb, k, :], start=(k == 0), stop=(k == 2))
                last.then_inc(S["img_done"], 1)
            for s in range(4):
                pair, h = s // 2, s % 2
                pe.wait_ge(S["img_ready"], 2 * (pair + 1))
                if s == 0:
                    pe.wait_ge(S["y_biased"], 6)
                for i in range(3):
                    last = tr(bank[s][:, 128 * i:128 * i + 128], img[:, pair, 256 * i + 128 * h:256 * i + 128 * h + 128], ident)
                last.then_inc(S["tok_done"], 1)
            pe.wait_ge(S["img_ready"], 4)
            for b in range(B):
                pe.wait_ge(S["xhat_ready"], 2 * b + 2)
                for k in range(2):
                    for h in range(2):
                        last = tr(bank[4 + b][0:CH, 256 * k + 128 * h:256 * k + 128 * h + 128], xhat[:, 2 * b + h, k * CH:(k + 1) * CH], ident)
                last.then_inc(S["xT_done"], 1)

            rows = (slice(0, CH), slice(0, CH + 1))

            def mm3(dst, w, x, first=True, last=True):
                mm(dst, w(0), x(0), start=first, stop=False)
                mm(dst, w(0), x(1), start=False, stop=False)
                return mm(dst, w(1), x(0), start=False, stop=last)

            def project_qk(b):
                if b == 0:
                    pe.wait_ge(S["tok_ready"], 4)
                    pe.wait_ge(S["xT_low"], 4)
                    pe.wait_ge(S["bias_zeroed"], BIAS_SET)
                    pe.wait_ge(S["w_split"], 4)
                else:
                    pe.wait_ge(S["smax_ready"], 12 * b)
                for m in (1, 0):
                    for t in range(2):
                        for k in range(2):
                            last = mm3(bank[m][:, t * N:(t + 1) * N], lambda i: wqkv[i][:, k, m * 256 + t * 128:m * 256 + t * 128 + 128],
                                       lambda i: xT[i][:, b, k, :], k == 0, k == 1)
                last.then_inc(S["qk_done"], 1)

            def project_v(b):
                if b:
                    pe.wait_ge(S["qmax_ready"], b)
                for h in range(2):
                    for k in range(2):
                        last = mm3(bank[5][:, h * C:(h + 1) * C], lambda i: xT[i][:, b, k, 128 * h:128 * h + 128],
                                   lambda i: wqkv[i][:, k, 512:WQ], k == 0, k == 1)
                last.then_inc(S["v_done"], 1)

            def scores_for_max(b, units):
                for u in units:
                    n, qh, g6 = 12 * b + u, u // 6, u % 6
                    if u == 0:
                        pe.wait_ge(S["q_low"], b + 1)
                        pe.wait_ge(S["k_low"], b + 1)
                        pe.wait_ge(S["k_masked_pool"], 3 * b + 1)
                    if u == 3:
                        pe.wait_ge(S["k_masked_dve"], b + 1)
                    if n >= 2:
                        pe.wait_ge(S["smax_ready"], n - 1)
                    t, h = g6 // 3, 2 * g6 % HPT
                    last = mm(bank[n % 2][:, :], q_sb[0][:, b % 2, t, 128 * qh:128 * qh + 128],
                              k_sb[0][:, b % 2, t, h:h + 2, :], start=True, stop=True)
                    last.then_inc(S["smax_done"], 1)

            def maxima_rows(b):
                pe.wait_ge(S["smax_ready"], 12 * b + 12)
                if b < 2:
                    pe.wait_ge(S["v_ready"], b + 1)
                else:
                    pe.wait_ge(S["attn_ready"], b - 1)
                for t in range(2):
                    for qh in range(2):
                        last = tr(bank[5][0:CH + HPT, t * N + 128 * qh:t * N + 128 * qh + 128], negmax[:, t, qh, :], ident)
                last.then_inc(S["rT_done"], 1)

            def scores(b, u):
                n, kh, g6 = 12 * b + u, u // 2 % 2, 2 * (u // 4) + u % 2
                if u == 0:
                    pe.wait_ge(S["k_masked_pool"], 3 * b + 3)
                if n >= 3:
                    pe.wait_ge(S["exp_ready"], n - 2)
                for v in range(2):
                    t, h = g6 // 3, (2 * g6 + v) % HPT
                    last = mm3(bank[2 + n % 3][:, v * N:(v + 1) * N], lambda i: k_sb[i][:, b % 2, t, h, 128 * kh:128 * kh + 128],
                               lambda i: q_sb[i][:, b % 2, t, :])
                last.then_inc(S["st_done"], 1)

            def attend(quad):
                b, j, s = quad // 3, quad % 3, quad % 2
                pe.wait_ge(S["exp_ready"], 4 * quad + 4)
                if quad >= 2:
                    pe.wait_ge(S["norm_ready"], quad - 1)
                for kh in range(2):
                    for h in range(4):
                        last = mm(bank[6 + s][32 * h:32 * h + 32, 0:N], v_sb[:, b % 2, kh, 4 * j + h, :], probs[:, s, kh, h, :],
                                  start=(kh == 0), stop=(kh == 1))
                last.then_inc(S["pv_done"], 1)

            def project_out(b):
                pe.wait_ge(S["norm_ready"], 3 * b + 3)
                if b + 2 < B:
                    pe.wait_ge(S["v_ready"], b + 3)
                else:
                    pe.wait_ge(S["qmax_ready"], B)
                if b == B - 1:
                    pe.wait_ge(S["attn_ready"], b)
                for h in range(2):
                    for j in range(3):
                        last = mm(bank[5][:, h * C:(h + 1) * C], o_sb[:, b % 2, j, 128 * h:128 * h + 128], wproj[:, j, :],
                                  start=(j == 0), stop=(j == 2))
                last.then_inc(S["proj_done"], 1)

            project_qk(0)
            project_v(0)
            scores_for_max(0, range(12))
            for b in range(B):
                if b:
                    attend(3 * b - 1)
                maxima_rows(b)
                if b + 1 < B:
                    project_qk(b + 1)
                    project_v(b + 1)
                pe.wait_ge(S["qmax_ready"], b + 1)
                for u in range(12):
                    if b and u == 1:
                        project_out(b - 1)
                    scores(b, u)
                    scores_for_max(b + 1, max_units(b, u))
                    if u in (7, 11):
                        attend(3 * b + u // 4 - 1)
            def shared_gate_up(u):
                half, f = u // FC, u % FC
                for m, free in ((0, "silu_s_ready"), (1, "hid_s_ready")):
                    if u >= 2:
                        pe.wait_ge(S[free], u - 1)
                    for b in range(2):
                        for k in range(2):
                            last = mm(bank[2 * m + u % 2][:, b * N:(b + 1) * N],
                                      shared_gu[0:CH, k * 2 * FF + m * FF + 128 * f:k * 2 * FF + m * FF + 128 * f + 128],
                                      x2T[0:CH, 2 * half + b, k, :], start=(k == 0), stop=(k == 1))
                    last.then_inc(S["su_done" if m else "sg_done"], 1)

            def shared_down(u):
                if u >= 2:
                    pe.wait_ge(S["shared_ready"], u - 1)
                for h in range(2):
                    t = 2 * u + h
                    for f in range(FC):
                        last = mm(bank[6 + u % 2][:, h * C:(h + 1) * C], hid_s[:, f, 128 * (t % 4):128 * (t % 4) + 128],
                                  shared_dn[:, f * C:(f + 1) * C], start=(f == 0), stop=(f == FC - 1))
                last.then_inc(S["shared_done"], 1)

            def rank_and_count():
                pe.wait_ge(S["route"], MEMBER_STEP)
                rank = bank[5][:, 0:NT * E].rearrange("p (t e) -> p t e", t=NT)
                mm(rank, before, member, start=True, stop=False, skip_group_check=True)
                for t in range(NT - 1):
                    mm(rank[:, t + 1:, :], ones, member[:, t:t + 1, :].broadcast_to([128, NT - 1 - t, E]),
                       start=False, stop=False, skip_group_check=True)
                for t in range(NT):
                    last = mm(bank[4][0:E, 256:384], member[:, t, :], ones, start=(t == 0), stop=(t == NT - 1))
                last.then_inc(S["count_done"], 1)

            def base():
                pe.wait_ge(S["padded_ready"], 1)
                rank = bank[5][:, 0:NT * E].rearrange("p (t e) -> p t e", t=NT)
                mm(rank, padded[0:E, :], before[0:E, 0:E].unsqueeze(1).broadcast_to([E, NT, E]), start=False, stop=True,
                   skip_group_check=True).then_inc(S["base_done"], 1)

            def tile_experts():
                mm(bank[4][0:E, 384:416], upto, padded[0:E, 0:32], start=True, stop=True).then_inc(S["end_done"], 1)
                pe.wait_ge(S["ended_ready"], 1)
                mm(bank[4][0:1, 448:480], ones[0:E, 0:1], ended[0:E, :], start=True, stop=True).then_inc(S["row_done"], 1)

            def slot_tokens():
                pe.wait_ge(S["onehot_ready"], 1)
                for s in range(NT * TOPK):
                    last = mm(bank[5][:, 128:160], is_part[:, s, :], id_tile[:, s, :], start=(s == 0), stop=(s == NT * TOPK - 1))
                last.then_inc(S["inv_done"], 1)

            def tokens_for_experts(b):
                pe.wait_ge(S["xhat2_ready"], 2 * b + 2)
                if b >= 2:
                    pe.wait_ge(S["x2T_ready"], b - 1)
                for k in range(2):
                    for h in range(2):
                        last = tr(bank[b % 2][0:CH, 256 * k + 128 * h:256 * k + 128 * h + 128], xhat2[:, 2 * b + h, k * CH:(k + 1) * CH], ident)
                last.then_inc(S["x2T_done"], 1)

            def gate_logits():
                for t in range(NT):
                    for k in range(2):
                        last = mm(bank[4][:, t * E:(t + 1) * E], x2T[rows[k], t // 2, k, 128 * (t % 2):128 * (t % 2) + 128],
                                  wgate[rows[k], k, :], start=(k == 0), stop=(k == 1))
                last.then_inc(S["logits_done"], 1)

            pe.wait_ge(S["ld_shared"], 3 * 16)
            pe.wait_ge(S["ld_attn"], 8 * 16)
            attend(3 * B - 1)
            for b in range(B - 1):
                tokens_for_experts(b)
            project_out(B - 1)
            pe.wait_ge(S["exp_ready"], 48)
            pe.wait_ge(S["x2T_ready"], B - 1)
            shared_gate_up(0)
            tokens_for_experts(B - 1)
            pe.wait_ge(S["x2T_ready"], B)
            pe.wait_ge(S["bias_zeroed"], BIAS_SET + 1)
            gate_logits()
            shared_gate_up(1)
            pe.wait_ge(S["attn_ready"], B)
            pe.wait_ge(S["norm_ready"], 12)
            rank_and_count()
            base()
            shared_gate_up(2)
            slot_tokens()
            tile_experts()
            pe.wait_ge(S["hid_s_ready"], FC)
            shared_down(0)
            shared_down(1)

            pe.wait_ge(S["ld_experts"], 16 * (2 * (E - LATE) + E))
            pe.wait_ge(S["ld_late"], 16 * 2 * LATE)
            pe.wait_ge(S["expert_ready"], 1)
            pe.wait_ge(S["slot_token_ready"], 1)

            def tokens_T(t, p, half):
                pe.wait_ge(gathered[p], 16 * half + 16)
                if not (isinstance(t, int) and t < 1):
                    pe.wait_ge(S["xgT_ready"], t)
                for k in range(2):
                    last = tr(bank[5][0:CH, 128 * k:128 * k + 128], xg[:, p, k * CH:(k + 1) * CH], ident)
                last.then_inc(S["xg_done"], 1)

            def gate_up(t, p, m, e):
                if m == 0:
                    pe.wait_ge(S["xgT_ready"], t + 1)
                if not (isinstance(t, int) and t < 2):
                    pe.wait_ge(S["hidden_ready" if m else "silu_ready"], t - 1)
                for k in range(2):
                    last = mm(bank[2 * m + p][:, 0:FF], xgT[0:CH, p, k, :], main[0:CH, bass.ds(e * GU + k * 2 * FF + m * FF, FF)],
                              start=(k == 0), stop=(k == 1))
                last.then_inc(S["up_done" if m else "gate_done"], 1)

            def hidden_T(t, p):
                pe.wait_ge(S["hidden_ready"], t + 1)
                if not (isinstance(t, int) and t < 1):
                    pe.wait_ge(S["hT_ready"], t)
                for f in range(FC):
                    last = tr(bank[4][:, 128 * f:128 * f + 128], hidden[:, p, 128 * f:128 * f + 128], ident)
                last.then_inc(S["hT_done"], 1)

            def down(t, e):
                pe.wait_ge(S["hT_ready"], t + 1)
                if not (isinstance(t, int) and t < 1):
                    pe.wait_ge(S["y_out_ready"], t)
                for f in range(FC):
                    last = mm(bank[6][:, 0:C], hiddenT[:, 128 * f:128 * f + 128], down_all[:, bass.ds(e * DN + f * C, C)],
                              start=(f == 0), stop=(f == FC - 1))
                last.then_inc(S["down_done"], 1)

            def expert(t):
                return pe.value_load(expert_i[0:1, bass.ds(t, 1)], min_val=0, max_val=E - 1)

            def step(t, p, half):
                more = not (isinstance(t, int) and t + 1 >= TILES)
                if more:
                    e = expert(t + 1)
                    gate_up(t + 1, 1 - p, 0, e)
                hidden_T(t, p)
                if more:
                    gate_up(t + 1, 1 - p, 1, e)
                if not (isinstance(t, int) and t + 2 >= TILES):
                    tokens_T(t + 2, p, half + 1)
                down(t, expert(t))

            tokens_T(0, 0, 0)
            e0 = expert(0)
            gate_up(0, 0, 0, e0)
            gate_up(0, 0, 1, e0)
            tokens_T(1, 1, 0)
            step(0, 0, 0)
            step(1, 1, 0)
            with pe.Fori(1, (TILES - 3) // 2) as i:
                step(2 * i, 0, i)
                step(2 * i + 1, 1, i)
            for t in range(TILES - 3, TILES):
                step(t, t % 2, t // 2)

            pe.wait_ge(S["silu_ready"], TILES)
            pe.wait_ge(S["hidden_ready"], TILES)
            pe.wait_ge(S["y_out_ready"], TILES)
            for u in range(FC, 2 * FC):
                shared_gate_up(u)
            pe.wait_ge(S["hid_s_ready"], 2 * FC)
            shared_down(2)
            shared_down(3)
            for b in range(B):
                pe.wait_ge(S["mixed"], 2 * b + 2)
                for k in range(2):
                    for h in range(2):
                        last = tr(bank[b][0:CH, 256 * k + 128 * h:256 * k + 128 * h + 128], tok_b[:, 2 * b + h, k * CH:(k + 1) * CH], ident)
                last.then_inc(S["outT_done"], 1)


_NAMES = {"x": "x", "w1": "L0_conv_w1", "b1": "L0_conv_b1", "w2": "L0_conv_w2", "b2": "L0_conv_b2",
          "w_qkv": "L1_attn_w_qkv", "b_qkv": "L1_attn_b_qkv", "w_proj": "L1_attn_w_proj", "b_proj": "L1_attn_b_proj",
          "w_gate": "L1_ffn_w_gate", "expert_bias": "L1_ffn_expert_bias", "wg": "L1_ffn_wg", "wu": "L1_ffn_wu",
          "wd": "L1_ffn_wd", "swg": "L1_ffn_swg", "swu": "L1_ffn_swu", "swd": "L1_ffn_swd"}


def kernel(**inputs):
    import concourse.bacc as bacc
    from concourse.bass_utils import run_bass_kernel_spmd

    nc = bacc.Bacc("TRN2", target_bir_lowering=False, num_devices=1)
    tables = constants()
    arrays = {k: np.ascontiguousarray(inputs[v]) for k, v in _NAMES.items()}
    arrays.update(tables_f32=tables[0], tables_bf16=tables[1])
    aps = {k: nc.dram_tensor(k, v.shape, mybir.dt.from_np(v.dtype), kind="ExternalInput").ap() for k, v in arrays.items()}
    out = nc.dram_tensor("out", [B, C, H, W], F32, kind="ExternalOutput").ap()
    program(nc, aps, out)
    return run_bass_kernel_spmd(nc, [arrays], core_ids=[0]).results[0]["out"]
```

```python
from contextlib import ExitStack

import numpy as np
import concourse.bass as bass
from concourse import mybir

F32 = mybir.dt.float32
BF16 = mybir.dt.bfloat16
F16 = mybir.dt.float16
F32R = mybir.dt.float32r
I32 = mybir.dt.int32
U32 = mybir.dt.uint32
ALU = mybir.AluOpType
ACT = mybir.ActivationFunctionType
AX = mybir.AxisListType

B, C, H, W = 4, 192, 16, 16
N = H * W
TOK = B * N
NT = TOK // 128
CH = C // 2
WF = W // 2 + 1
MODES = H * WF
MA = 80
MB = MODES - MA
BLK = 24
GC = 2 * BLK
GROUPS = C // GC
IM = 64
LAMBDA = 0.01
HEADS, HD = 12, 16
HPT = HEADS // 2
SCALE = HD ** -0.5
E, TOPK, FF = 16, 2, 384
FC = FF // 128
TILE = 128
TILES = (TOK * TOPK + E * (TILE - 1)) // TILE
SURE = TOK * TOPK // TILE
PAIRS = (TILES - 1) // 2
assert SURE % 2 == 0 and TILES % 2 == 1
GU = 2 * 2 * FF
DN = FC * C
EXTRA = 13240
SPLIT = 2 * 2 * 2 * TILE + 3 * 2 * 2 * FF
LATE = 14
EPS = 1e-5
HALVES = (range(0, NT // 2), range(NT // 2, NT))
NORM_PARTS = (range(0, NT - 2), range(NT - 2, NT))
WQ = 4 * 128 + C
BIAS_SET = 5
MEMBER_STEP = 5 + 2 * NT + 3


def constants():
    h, w = np.meshgrid(np.arange(H), np.arange(W), indexing="ij")
    k1, k2 = np.meshgrid(np.arange(H), np.arange(WF), indexing="ij")
    turn = (np.outer(h.ravel(), k1.ravel()) % H) / H + (np.outer(w.ravel(), k2.ravel()) % W) / W
    angle = 2 * np.pi * turn
    forward = np.concatenate([np.cos(angle), -np.sin(angle)], 1) / np.sqrt(N)
    twice = np.where((k2.ravel() == 0) | (k2.ravel() == W // 2), 1.0, 2.0)[:, None]
    real, imag = twice * np.cos(angle).T / np.sqrt(N), -twice * np.sin(angle).T / np.sqrt(N)
    order = np.arange(N).reshape(N // 4, 4).T.ravel()
    inverse = np.zeros((128, 3, N))
    inverse[:MA, 0], inverse[:MA, 2] = real[:MA, order], imag[:MA, order]
    inverse[:MB, 1], inverse[64:64 + MB, 1] = real[MA:, order], imag[MA:, order]
    p = np.arange(128)
    masks = np.stack([(p // HD == h) | (p == CH + h) for h in range(HPT)], 1) * 1.0
    f = np.concatenate([
        forward.reshape(2, 128, 2 * MODES).transpose(1, 0, 2).reshape(128, -1),
        inverse.reshape(128, -1),
        np.eye(128),
        np.tile(np.arange(128), (128, 1)),
        TOPK * (p[:, None] + 128 * np.repeat(np.arange(NT), TOPK)[None, :]) + np.arange(NT * TOPK)[None, :] % TOPK + 1,
        masks,
        np.tile(128 * np.arange(32), (128, 1)),
        TOK * TOPK + 1 + p[:, None],
    ], 1).astype(np.float32)
    before = (p[:, None] < p[None, :]) * 1.0
    upto = (p[:, None] <= p[None, :]) * 1.0
    g = np.concatenate([before, np.ones((128, 128)), upto[:, :E]], 1)
    return f, g.astype(mybir.dt.np(BF16))


F_FWD = 0
F_INV = F_FWD + 2 * 2 * MODES
F_IDENT = F_INV + 3 * N
F_IOTA = F_IDENT + 128
F_PAIR = F_IOTA + 128
F_MASK = F_PAIR + NT * TOPK
F_TILE0 = F_MASK + HPT
F_SPARE = F_TILE0 + 32
F_ALL = F_SPARE + 1


def program(nc, a, out):
    ctx = ExitStack()
    with ctx:
        def sb(name, shape, dt=F32):
            return ctx.enter_context(nc.sbuf_tensor(name, shape, dt))

        def sem(name):
            return ctx.enter_context(nc.semaphore(name))

        xhat_rows = nc.dram_tensor("xhat_rows", [TOK, C], F32).ap()
        pair_rows = nc.dram_tensor("pair_rows", [TOK * TOPK + TILE, C], F32).ap()

        cf = sb("cf", [128, F_ALL - F_IDENT])
        cb = sb("cb", [128, 256 + E], BF16)
        table = lambda start, end: cf[:, start - F_IDENT:end - F_IDENT]
        ident = table(F_IDENT, F_IOTA)
        iota = table(F_IOTA, F_PAIR)
        pair_id = table(F_PAIR, F_MASK)
        mask = table(F_MASK, F_TILE0)
        tile_start = table(F_TILE0, F_SPARE)[0:E, :]
        spare_row = table(F_SPARE, F_ALL)
        before, ones, upto = cb[:, 0:128], cb[:, 128:256], cb[0:E, 256:256 + E]

        down_all = sb("down_all", [128, E * DN])
        shared_gu = sb("shared_gu", [128, GU])
        shared_dn = sb("shared_dn", [128, DN])
        tok = sb("tok", [128, NT, C])
        tok_b = sb("tok_b", [128, NT, C])
        with nc.sbuf_tensor("rounded", [128, E * GU + EXTRA], F32R) as rounded:
            pass
        with nc.sbuf_tensor("before_split", [128, E * GU + EXTRA - SPLIT], F32), nc.sbuf_tensor("split", [128, SPLIT], F32R) as split:
            pass
        main = sb("main", [128, E * GU + EXTRA])
        at = [(E - LATE) * GU]

        def carve(cols, start=None):
            at[0] = (at[0] if start is None else start) + cols
            assert at[0] <= E * GU + EXTRA, at[0]
            return main[:, at[0] - cols:at[0]]

        def carve_r(cols):
            carve(cols)
            return rounded[:, at[0] - cols:at[0]]

        pix = carve(B * (2 * C + IM - GC), (E - LATE) * GU).rearrange("p (b c) -> p b c", b=B)
        spec = carve(GROUPS * B * MODES).rearrange("p (q m) -> p q m", q=GROUPS)
        hid = carve(GROUPS * B * MODES).rearrange("p (q m) -> p q m", q=GROUPS)
        y_low = carve(B * 2 * C).rearrange("p (b q r c) -> p b q r c", b=B, q=GROUPS, r=2)
        y_high = carve(B * C).rearrange("p (b c) -> p b c", b=B)
        w1 = carve(GROUPS * 128).rearrange("p (q r o) -> p q r o", q=GROUPS, r=2)
        w2 = carve(GROUPS * 2 * GC).rearrange("p (q r o) -> p q r o", q=GROUPS, r=2)
        b1 = carve(GROUPS)
        fwd = carve(2 * 2 * MODES).rearrange("p (k m) -> p k m", k=2)
        inv = carve(3 * N).rearrange("p (k n) -> p k n", k=3)
        x_res = carve(2 * 768).rearrange("p (q f) -> p q f", q=2)
        img = carve(2 * 768).rearrange("p (q f) -> p q f", q=2)
        clipped = carve(2 * 2 * C).rearrange("p (s c) -> p s c", s=2)
        spectral_end = at[0]
        wgate = sb("wgate", [128, 2, E])
        carve(0, E * GU)
        xT = [carve_r(B * 2 * N).rearrange("p (b k n) -> p b k n", b=B, k=2) for _ in range(2)]
        after_xT = at[0]
        carve(0, (E - LATE) * GU)
        q_sb = [carve_r(2 * 2 * N).rearrange("p (s t n) -> p s t n", s=2, t=2) for _ in range(2)]
        k_all = [carve_r(2 * N).rearrange("p (t n) -> p t n", t=2) for _ in range(2)]
        k_sb = [carve_r(2 * HEADS * N).rearrange("p (s t h n) -> p s t h n", s=2, t=2, h=HPT) for _ in range(2)]
        assert at[0] >= spectral_end
        negmax = carve(2 * 2 * (CH + HPT)).rearrange("p (t q f) -> p t q f", t=2, q=2)
        v_sb = carve(2 * 2 * HEADS * 32).rearrange("p (s k h d) -> p s k h d", s=2, k=2, h=HEADS)
        probs_flat = carve(2 * 8 * N)
        assert at[0] <= E * GU
        carve(0, after_xT)
        probs = probs_flat.rearrange("p (s k h n) -> p s k h n", s=2, k=2, h=4)
        o_sb = carve(2 * 3 * N).rearrange("p (s j n) -> p s j n", s=2, j=3)
        xhat = probs_flat[:, 0:NT * C].rearrange("p (t c) -> p t c", t=NT)
        recip = carve(2 * N).rearrange("p (s n) -> p s n", s=2)
        den = recip
        stats = carve(NT * 6).rearrange("p (t s) -> p t s", t=NT)
        meanvar = carve(NT * 2).rearrange("p (t s) -> p t s", t=NT)
        std = carve(NT)
        rstd = carve(NT)
        eps_col = sb("eps_col", [128, 1])[:, :]
        warm = sb("warm", [128, 1])[:, :]
        ended_act = sb("ended_act", [128, 1])[:, :]
        ended_dve = sb("ended_dve", [128, 1])[:, :]
        wqkv_raw = carve(2 * WQ).rearrange("p (k n) -> p k n", k=2)
        wqkv = [carve_r(2 * WQ).rearrange("p (k n) -> p k n", k=2) for _ in range(2)]
        wproj = carve(3 * C).rearrange("p (j n) -> p j n", j=3)
        bproj = carve(C)
        x2T = carve(B * 2 * N, E * GU).rearrange("p (b k n) -> p b k n", b=B, k=2)
        xhat2 = carve(NT * C).rearrange("p (t c) -> p t c", t=NT)
        assert at[0] <= after_xT
        carve(0, after_xT)
        hid_s = carve(FC * 512).rearrange("p (f n) -> p f n", f=FC)
        silu_s = [carve(512) for _ in range(2)]
        weight = carve(NT * TOPK).rearrange("p (t k) -> p t k", t=NT)
        slot_token = carve(32).bitcast(I32)
        slot_pair = carve(32).bitcast(U32)
        expert_i = carve(32).bitcast(I32)
        used_i = carve(2).bitcast(I32)
        tile_used = carve(32)
        temporary = at[0]
        logit = carve(NT * E).rearrange("p (t e) -> p t e", t=NT)
        prob = carve(NT * E).rearrange("p (t e) -> p t e", t=NT)
        small = carve(NT * 4).rearrange("p (s t) -> p s t", s=4)
        top = carve(NT * 8).rearrange("p (t k) -> p t k", t=NT)
        top_i = carve(NT * 8).bitcast(U32).rearrange("p (t k) -> p t k", t=NT)
        top_f = carve(NT * TOPK).rearrange("p (t k) -> p t k", t=NT)
        chosen = carve(NT * TOPK * E).rearrange("p (t k e) -> p t k e", t=NT, k=TOPK)
        member = carve(NT * E // 2).bitcast(BF16).rearrange("p (t e) -> p t e", t=NT)
        at_slot = carve(NT * TOPK * E).rearrange("p (t k e) -> p t k e", t=NT, k=TOPK)
        slot_f = carve(NT * TOPK)
        slot_i = carve(NT * TOPK).bitcast(I32)
        pair_i = carve(32).bitcast(I32)
        spare = carve(32)
        part_i = carve(NT * TOPK).bitcast(I32)
        tile_i = carve(NT * TOPK).bitcast(I32)
        part_f = carve(NT * TOPK)
        tile_f = carve(NT * TOPK)
        count_i = carve(128).bitcast(I32)
        padded_i = carve(128).bitcast(I32)
        padded = carve(64).bitcast(BF16)
        ended = carve(16).bitcast(BF16)
        is_part = carve(NT * TOPK * 64).bitcast(F16).rearrange("p (s q) -> p s q", s=NT * TOPK)
        is_tile = carve(NT * TOPK * 32).rearrange("p (s q) -> p s q", s=NT * TOPK)
        id_tile = carve(NT * TOPK * 16).bitcast(F16).rearrange("p (s q) -> p s q", s=NT * TOPK)
        xg = carve(2 * C, E * GU + B * 2 * N).rearrange("p (s c) -> p s c", s=2)
        silu = carve(2 * FF).rearrange("p (s f) -> p s f", s=2)
        hiddenT = carve(FF)
        y_out = carve(2 * C).rearrange("p (s c) -> p s c", s=2)
        assert at[0] <= after_xT
        hidden = carve(2 * FF, temporary).rearrange("p (s f) -> p s f", s=2)
        assert at[0] <= E * GU + EXTRA - SPLIT
        xgT = [split[:, i * 512:(i + 1) * 512].rearrange("p (s k n) -> p s k n", s=2, k=2) for i in range(2)]
        w_gate = [split[:, 1024 + i * 4 * FF:1024 + (i + 1) * 4 * FF].rearrange("p (s k f) -> p s k f", s=2, k=2) for i in range(2)]
        w_up = [split[:, 1024 + (8 + 2 * i) * FF:1024 + (10 + 2 * i) * FF].rearrange("p (k f) -> p k f", k=2) for i in range(2)]
        y_back = carve(NT * TOPK * C, 0).rearrange("p (t k c) -> p t k c", t=NT, k=TOPK)
        out_T = carve(B * 2 * N).rearrange("p (b k n) -> p b k n", b=B, k=2)

        gu_e = lambda e: main[0:CH, bass.ds(e * GU, GU)].rearrange("p (k f) -> p k f", k=2)
        gate_or_up_e = lambda e, m: gu_e(e)[:, :, m * FF:(m + 1) * FF]
        dn_e = lambda e: down_all[:, bass.ds(e * DN, DN)].rearrange("p (k c) -> p k c", k=FC)

        bank = [ctx.enter_context(nc.psum_tensor(f"bank{i}", [128, 512], F32)) for i in range(8)]

        names = """ld_fwd ld_const ld_w1 ld_w2 ld_res ld_attn ld_qkv ld_shared ld_experts ld_late
        zeroed w_zeroed w_split bias_zeroed eps_set negated
        spec_done spec_act spec_dve hid_done hid_ready y_done y_clipped y_ready img_done img_ready
        tok_done tok_ready tok_b_ready stats_ready mv_ready std_ready rstd_ready xhat_ready
        xT_done xT_high xT_low qk_done v_done q_high q_low k_high k_low k_masked_pool k_masked_dve v_ready smax_done smax_ready rT_done qmax_ready
        st_done exp_ready pv_done recip_ready den_ready norm_ready proj_done attn_ready
        stats2 mv2 std2 rstd2 xhat2_ready xhat2_stored x2T_done x2T_ready
        logits_done exp_logit_ready route rank_done count_done base_done end_done inv_done
        padded_ready ended_ready is_part_ready is_tile_ready id_tile_ready expert_ready used_ready loop_act loop_dve pair_ready slot_pair_ready scattered slot_token_ready
        sg_done su_done silu_s_ready hid_s_ready shared_done shared_ready
        xg_done xgT_high xgT_low w_gate_high w_gate_low w_up_high w_up_low gate_done up_done silu_ready hidden_ready hT_done hT_ready down_done y_out_ready
        mixed half_mixed outT_done outT_ready stored""".split()
        S = {n: sem(n) for n in names}
        ld_pix = [sem(f"ld_pix{b}") for b in range(B)]
        gathered = [sem(f"gathered{p}") for p in range(2)]
        y_stored = [sem(f"y_stored{p}") for p in range(2)]
        back = [sem(f"back{i}") for i in range(NT)]
        block = ctx.enter_context(nc.Block())

        def one_head_keys(engine, b, part, t):
            return engine.tensor_tensor(k_sb[part][:, b % 2, t], k_all[part][:, t, :].bitcast(F32).unsqueeze(1).broadcast_to([128, HPT, N]),
                                        mask.unsqueeze(2).broadcast_to([128, HPT, N]), ALU.mult)

        def loop_pairs(engine, step):
            with engine.Fori(1, SURE // 2) as i:
                step(2 * i, 0, i)
                step(2 * i + 1, 1, i)
            used = engine.value_load(used_i[0:1, 0:1], min_val=SURE, max_val=TILES)
            with engine.Fori(SURE // 2, PAIRS - 1) as i:
                with engine.If(used > 2 * i):
                    step(2 * i, 0, i)
                    step(2 * i + 1, 1, i)
            with engine.If(used > 2 * (PAIRS - 1)):
                for t in range(2 * (PAIRS - 1), TILES):
                    step(t, t % 2, t // 2)

        def shared_banks(u):
            return ((1, 3), (0, 2), (6, 7), (1, 3), (1, 3), (0, 2))[u]

        def x2T_bank(b):
            return bank[b == 1]

        def max_bank(n):
            return bank[2 + n % 3 if n < 12 else n % 2][:, :]

        def max_units(b, u):
            upto = lambda v: max(0, min(12, -(-12 * (v - 3) // 7)))
            return range(upto(u), upto(u + 1)) if b + 1 < B else range(0)

        def spectrum_units():
            for pair in range(2):
                for b in range(2 * pair, 2 * pair + 2):
                    yield bank[(3 * pair + b % 2) % 4][0:MA, 0:2 * C], y_low[0:MA, b].rearrange("p q r c -> p (q r c)")
                yield bank[(3 * pair + 2) % 4][:, 0:2 * C], y_high[:, 2 * pair:2 * pair + 2, :].rearrange("p b c -> p (b c)")

        def load_pixels(queue, b):
            queue.dma_start(pix[:, b, 0:2 * C].rearrange("p (k c) -> p k c", k=2),
                            a["x"][b].rearrange("c h w -> (c h w)").rearrange("(k p c) -> p k c", k=2, p=128)).then_inc(ld_pix[b], 16)

        def load_blocks(queue, dst, src, sem):
            for k in range(2):
                i, o = slice(BLK * k, BLK * k + BLK), slice(BLK * k, BLK * k + BLK)
                im = slice(IM + BLK * k, IM + BLK * k + BLK)
                block_k = src.rearrange("r (q k) i o -> k r i q o", k=2)[k]
                for r in range(2):
                    queue.dma_start(dst[i, :, r, o], block_k[r]).then_inc(sem, 16)
                    queue.dma_start(dst[im, :, 1 - r, o], block_k[r]).then_inc(sem, 16)

        @block.sync
        def _(sp):
            sp.dma_start(fwd, a["tables_f32"][:, F_FWD:F_INV].rearrange("p (k m) -> p k m", k=2)).then_inc(S["ld_fwd"], 16)
            for b in (1, 3):
                load_pixels(sp, b)
            sp.wait_ge(S["zeroed"], 3)
            load_blocks(sp, w2, a["w2"], S["ld_w2"])
            sp.dma_start(w2[GC:GC + 1, :, :, :], a["b2"].rearrange("r n o -> r (n o)").rearrange("r (q c) -> q r c", c=GC).unsqueeze(0)).then_inc(S["ld_w2"], 16)
            sp.dma_start(inv, a["tables_f32"][:, F_INV:F_IDENT].rearrange("p (k n) -> p k n", k=3)).then_inc(S["ld_const"], 16)
            sp.dma_start(cf[:, :], a["tables_f32"][:, F_IDENT:]).then_inc(S["ld_const"], 16)
            sp.dma_start(cb[:, :], a["tables_bf16"]).then_inc(S["ld_attn"], 16)
            sp.dma_start(x_res, a["x"].rearrange("b c h w -> (b c h w)")
                         .rearrange("(q p f) -> p q f", q=2, p=128)).then_inc(S["ld_res"], 16)
            sp.wait_ge(S["w_zeroed"], 4)
            for m in range(2):
                for k in range(2):
                    sp.dma_start(wqkv_raw[0:CH, k, 256 * m:256 * m + 256].rearrange("p (t n) -> p t n", t=2)[:, :, 0:CH],
                                 a["w_qkv"][k * CH:(k + 1) * CH, m * C:(m + 1) * C].rearrange("p (t n) -> p t n", t=2)).then_inc(S["ld_qkv"], 16)
                sp.dma_start(wqkv_raw[CH:CH + 1, 1, 256 * m:256 * m + 256].rearrange("p (t n) -> p t n", t=2)[:, :, 0:CH],
                             a["b_qkv"][m * C:(m + 1) * C].rearrange("(t n) -> t n", t=2).unsqueeze(0)).then_inc(S["ld_qkv"], 16)
            sp.dma_start(wqkv_raw[0:CH, :, 512:WQ], a["w_qkv"][:, 2 * C:3 * C].rearrange("(k p) n -> p k n", k=2)).then_inc(S["ld_qkv"], 16)
            sp.dma_start(wqkv_raw[CH:CH + 1, 1, 512:WQ], a["b_qkv"][2 * C:3 * C].unsqueeze(0)).then_inc(S["ld_qkv"], 16)
            for r in range(4):
                sp.dma_start(wproj[32 * r:32 * r + HD, :, :],
                             a["w_proj"].rearrange("(j r d) n -> r d j n", r=4, d=HD)[r]).then_inc(S["ld_attn"], 16)
            sp.dma_start(bproj[:, :], a["b_proj"].partition_broadcast(128)).then_inc(S["ld_attn"], 16)
            sp.dma_start(wgate[0:CH, :, :], a["w_gate"].rearrange("(k p) n -> p k n", k=2)).then_inc(S["ld_attn"], 16)
            sp.dma_start(wgate[CH:CH + 1, 1, :], a["expert_bias"].unsqueeze(0)).then_inc(S["ld_attn"], 16)
            sg = shared_gu[0:CH, :].rearrange("p (k f) -> p k f", k=2)
            sp.dma_start(sg[:, :, 0:FF], a["swg"].rearrange("(k p) f -> p k f", k=2)).then_inc(S["ld_shared"], 16)
            sp.dma_start(sg[:, :, FF:], a["swu"].rearrange("(k p) f -> p k f", k=2)).then_inc(S["ld_shared"], 16)
            sp.dma_start(shared_dn[:, :].rearrange("p (k c) -> p k c", k=FC),
                         a["swd"].rearrange("(k p) c -> p k c", k=FC)).then_inc(S["ld_shared"], 16)
            for e in range(E - LATE):
                sp.dma_start(gu_e(e)[:, :, 0:FF], a["wg"][e].rearrange("(k p) f -> p k f", k=2)).then_inc(S["ld_experts"], 16)
                sp.dma_start(gu_e(e)[:, :, FF:], a["wu"][e].rearrange("(k p) f -> p k f", k=2)).then_inc(S["ld_experts"], 16)
            for e in range(E):
                sp.dma_start(dn_e(e), a["wd"][e].rearrange("(k p) c -> p k c", k=FC)).then_inc(S["ld_experts"], 16)
            first = E - LATE
            keys = [first + 2 + 4 * part + 2 * slot + e for slot in range(2) for part in range(2) for e in range(2)]
            for wait, count, experts in (("st_done", 12 * (B - 1), keys[:4]), ("st_done", 12 * B, keys[4:] + [first, first + 1]),
                                         ("pv_done", 3 * B, range(first + 10, E))):
                sp.wait_ge(S[wait], count)
                for e in experts:
                    sp.dma_start(gu_e(e)[:, :, 0:FF], a["wg"][e].rearrange("(k p) f -> p k f", k=2)).then_inc(S["ld_late"], 16)
                    sp.dma_start(gu_e(e)[:, :, FF:], a["wu"][e].rearrange("(k p) f -> p k f", k=2)).then_inc(S["ld_late"], 16)

            sp.wait_ge(S["scattered"], 1)
            for t in range(NT):
                sp.dma_start(y_back[:, t].rearrange("p k c -> p (k c)"),
                             pair_rows[TOPK * TILE * t:TOPK * TILE * (t + 1), :].rearrange("(p k) c -> p (k c)", k=TOPK)).then_inc(back[t], 16)
            for b in range(B):
                sp.wait_ge(S["outT_ready"], b + 1)
                sp.dma_start(out[b].rearrange("(k p) h w -> p k (h w)", k=2), out_T[0:CH, b]).then_inc(S["stored"], 16)
            sp.wait_ge(S["stored"], 16 * B)

        @block.gpsimd
        def _(pool):
            nc.gpsimd.memset(w1, 0.0).then_inc(S["zeroed"], 1)
            nc.gpsimd.memset(b1, 0.0).then_inc(S["zeroed"], 1)
            nc.gpsimd.memset(w2, 0.0).then_inc(S["zeroed"], 1)
            nc.gpsimd.memset(pix[:, :, 2 * C:], 0.0).then_inc(S["zeroed"], 1)
            pool.wait_ge(S["zeroed"], 4)
            nc.gpsimd.memset(b1[32:IM, :], 1.0).then_inc(S["zeroed"], 1)
            pool.wait_ge(S["zeroed"], 5)
            nc.gpsimd.memset(wqkv_raw, 0.0).then_inc(S["w_zeroed"], 1)
            nc.gpsimd.memset(wproj, 0.0).then_inc(S["w_zeroed"], 1)
            nc.gpsimd.memset(wgate[:, :, :], 0.0).then_inc(S["w_zeroed"], 1)
            pool.wait_ge(S["w_zeroed"], 3)
            nc.gpsimd.memset(wqkv_raw[CH:CH + 1, 1, 256:512].rearrange("p (t n) -> p t n", t=2)[:, :, CH:CH + HPT], 1.0).then_inc(S["w_zeroed"], 1)
            pool.wait_ge(S["w_zeroed"], 4)
            nc.gpsimd.memset(shared_gu[CH:, :], 0.0).then_inc(S["w_zeroed"], 1)
            pool.wait_ge(S["w_zeroed"], 5)
            for i, (part, value) in enumerate(((xT[0][CH:, :, :, :], 0.0), (xT[0][CH:CH + 1, :, 1, :], 1.0), (xT[1][CH:, :, :, :], 0.0),
                                               (v_sb, 1.0), (negmax, 0.0))):
                nc.gpsimd.memset(part.bitcast(F32), value).then_inc(S["bias_zeroed"], 1)
                pool.wait_ge(S["bias_zeroed"], i + 1)
            pool.wait_ge(S["tok_ready"], B)
            pool.wait_ge(S["ld_attn"], 8 * 16)
            nc.gpsimd.tensor_tensor(tok_b[:, :, :], tok[:, :, :],
                                    bproj[:, :].unsqueeze(1).broadcast_to([128, NT, C]), ALU.add).then_inc(S["tok_b_ready"], 1)
            for b in range(B):
                if b >= 2:
                    pool.wait_ge(S["st_done"], 12 * (b - 1))
                for part, t in ((0, 0), (1, 0), (1, 1)):
                    pool.wait_ge(S["k_high"] if part == 0 else S["k_low"], b + 1)
                    one_head_keys(nc.gpsimd, b, part, t).then_inc(S["k_masked_pool"], 1)
            pool.wait_ge(S["v_done"], B)
            pool.wait_ge(S["k_masked_pool"], 3 * B)
            nc.gpsimd.memset(x2T[CH:, :, :, :], 0.0).then_inc(S["bias_zeroed"], 1)
            pool.wait_ge(S["bias_zeroed"], BIAS_SET + 1)
            nc.gpsimd.memset(x2T[CH:CH + 1, :, 1, :], 1.0).then_inc(S["bias_zeroed"], 1)
            for t in range(NT):
                pool.wait_ge(S["xhat2_ready"], t + 1)
                pool.dma_start(xhat_rows[128 * t:128 * t + 128, :], xhat2[:, t, :]).then_inc(S["xhat2_stored"], 16)
            pool.wait_ge(S["is_tile_ready"], 1)
            nc.gpsimd.tensor_tensor(id_tile, is_tile, pair_id.unsqueeze(2).broadcast_to([128, NT * TOPK, 32]), ALU.mult).then_inc(S["id_tile_ready"], 1)
            pool.wait_ge(S["xhat2_stored"], 16 * NT)
            pool.wait_ge(S["slot_token_ready"], 1)

            def gather(t):
                if t >= 2:
                    pool.wait_ge(S["xg_done"], t - 1)
                pool.indirect_dma_start(xg[:, t % 2, :], None, xhat_rows,
                                        bass.IndirectOffsetOnAxis(ap=slot_token[:, t:t + 1].bitcast(U32), axis=0)).then_inc(gathered[t % 2], 16)

            def scatter(t):
                pool.wait_ge(S["y_out_ready"], t + 1)
                if t:
                    pool.wait_ge(y_stored[(t - 1) % 2], 16 * ((t - 1) // 2 + 1))
                pool.indirect_dma_start(pair_rows, bass.IndirectOffsetOnAxis(ap=slot_pair[:, t:t + 1], axis=0),
                                        y_out[:, t % 2, :], None).then_inc(y_stored[t % 2], 16)

            for t in range(4):
                gather(t)
            pool.wait_ge(S["slot_pair_ready"], 1)
            for t in range(0, SURE - 2, 2):
                for tt in (t, t + 1):
                    gather(tt + 4)
                    scatter(tt)
            pool.wait_ge(S["expert_ready"], 2)
            used = pool.value_load(used_i[0:1, 0:1], min_val=SURE, max_val=TILES)

            def last_pair(tiles):
                for t in tiles:
                    scatter(t)
                pool.wait_ge(y_stored[t % 2], 16 * (t // 2 + 1))

            for t in range(SURE - 2, 2 * (PAIRS - 1), 2):
                with pool.If(used > t + 2):
                    for tt in (t, t + 1):
                        if tt + 4 < TILES:
                            gather(tt + 4)
                        scatter(tt)
                with pool.Else():
                    if t < SURE:
                        last_pair((t, t + 1))
                    else:
                        with pool.If(used > t):
                            last_pair((t, t + 1))
            with pool.If(used > 2 * (PAIRS - 1)):
                last_pair(range(2 * (PAIRS - 1), TILES))
            pool.sem_inc(S["scattered"], 1)

        @block.scalar
        def _(act):
            for b in (0, 2):
                load_pixels(act, b)
            act.wait_ge(S["zeroed"], 5)
            load_blocks(act, w1, a["w1"], S["ld_w1"])
            with nc.allow_non_contiguous_dma(reason="a bias per channel"):
                for r in range(2):
                    act.dma_start(b1[IM * r:IM * r + GC, :], a["b1"][r].rearrange("n o -> (n o)").rearrange("(q p) -> p q", p=GC)).then_inc(S["ld_w1"], 16)
            for b in range(B):
                act.wait_ge(S["spec_done"], 2 * b + 1)
                act.activation(spec[:, 0:2, b * MODES:(b + 1) * MODES],
                               bank[2 * b][:, 0:2 * MODES].rearrange("p (q m) -> p q m", q=2), ACT.Copy).then_inc(S["spec_act"], 1)
            act.wait_ge(S["ld_w1"], 10 * 16)
            for v in range(2 * GROUPS):
                bp, q = v // GROUPS, v % GROUPS
                act.wait_ge(S["hid_done"], v + 1)
                act.activation(hid[:, q, bp * 2 * MODES:(bp + 1) * 2 * MODES],
                               bank[4 + v % 4][:, 0:2 * MODES], ACT.Relu, bias=b1[:, q:q + 1]).then_inc(S["hid_ready"], 1)
            act.wait_ge(S["eps_set"], 1)
            act.activation(warm, eps_col, ACT.Sqrt)

            def token_major(s):
                pair, h = s // 2, s % 2
                act.wait_ge(S["tok_done"], s + 1)
                dst = tok[:, 4 * pair + h:4 * pair + h + 3:2, :].rearrange("p b (g i) -> p b g i", i=3)
                src = bank[s][:, 0:3 * 128].rearrange("p (i b g) -> p b g i", i=3, b=2)
                act.activation(dst, src, ACT.Copy).then_inc(S["tok_ready"], 1)

            def deviations(tiles, mv, std_sem):
                act.wait_ge(S[mv], tiles.stop)
                act.activation(std[:, tiles.start:tiles.stop], meanvar[:, tiles.start:tiles.stop, 1], ACT.Sqrt, bias=eps_col).then_inc(S[std_sem], 1)

            def xT_high(b):
                act.wait_ge(S["xT_done"], b + 1)
                act.activation(xT[0][0:CH, b, :, :], bank[4 + b][0:CH, :].rearrange("p (k n) -> p k n", k=2), ACT.Copy).then_inc(S["xT_high"], 1)

            def high_parts(b):
                act.wait_ge(S["qk_done"], b + 1)
                if b >= 1:
                    act.wait_ge(S["k_masked_pool"], 3 * b)
                    act.wait_ge(S["k_masked_dve"], b)
                act.activation(k_all[0], bank[1][:, :].rearrange("p (t n) -> p t n", t=2), ACT.Copy).then_inc(S["k_high"], 1)
                if b >= 2:
                    act.wait_ge(S["st_done"], 12 * (b - 1))
                act.activation(q_sb[0][:, b % 2], bank[0][:, :].rearrange("p (t n) -> p t n", t=2), ACT.Copy).then_inc(S["q_high"], 1)

            def values(b):
                if b == 0:
                    act.wait_ge(S["bias_zeroed"], BIAS_SET)
                act.wait_ge(S["v_done"], b + 1)
                if b >= 2:
                    act.wait_ge(S["pv_done"], 3 * (b - 1))
                act.activation(v_sb[:, b % 2, :, :, 0:HD],
                               bank[5][:, 0:2 * C].rearrange("p (k h d) -> p k h d", k=2, d=HD), ACT.Copy).then_inc(S["v_ready"], 1)

            def tokens_for_experts(b):
                act.wait_ge(S["x2T_done"], b + 1)
                act.activation(x2T[0:CH, b, :, :], x2T_bank(b)[0:CH, :].rearrange("p (k n) -> p k n", k=2), ACT.Copy).then_inc(S["x2T_ready"], 1)

            def shared_silu(u):
                act.wait_ge(S["sg_done"], u + 1)
                if u >= 2:
                    act.wait_ge(S["hid_s_ready"], u - 1)
                act.activation(silu_s[u % 2], bank[shared_banks(u)[0]][:, :], ACT.Silu).then_inc(S["silu_s_ready"], 1)

            for s in range(2):
                token_major(s)
            deviations(HALVES[0], "mv_ready", "std_ready")
            for b in range(2):
                xT_high(b)
            for s in range(2, 4):
                token_major(s)
            deviations(HALVES[1], "mv_ready", "std_ready")
            high_parts(0)
            values(0)
            for b in range(2, B):
                xT_high(b)
            act.activation(warm, eps_col, ACT.Exp)
            for b in range(B):
                if b + 1 < B:
                    high_parts(b + 1)
                    values(b + 1)
                for j in range(3):
                    quad = 3 * b + j
                    if quad >= 2:
                        act.wait_ge(S["pv_done"], quad - 1)
                    for u in range(4):
                        n = 4 * quad + u
                        act.wait_ge(S["st_done"], n + 1)
                        act.activation(probs[:, quad % 2, u // 2, 2 * (u % 2):2 * (u % 2) + 2, :],
                                       bank[2 + n % 3][:, :].rearrange("p (h n) -> p h n", h=2), ACT.Exp).then_inc(S["exp_ready"], 1)
            deviations(NORM_PARTS[0], "mv2", "std2")
            for b in range(B - 1):
                tokens_for_experts(b)
            deviations(NORM_PARTS[1], "mv2", "std2")
            act.activation(warm, eps_col, ACT.Exp)
            tokens_for_experts(B - 1)
            act.wait_ge(S["route"], 2)
            act.activation(prob, logit, ACT.Exp).then_inc(S["exp_logit_ready"], 1)
            for u in range(FC):
                shared_silu(u)


            def columns_high(t, p):
                act.wait_ge(S["xg_done"], t + 1)
                if not (isinstance(t, int) and t < 2):
                    act.wait_ge(S["up_done"], t - 1)
                act.activation(xgT[0][0:CH, p], bank[5][0:CH, 0:256].rearrange("p (k n) -> p k n", k=2), ACT.Copy).then_inc(S["xgT_high"], 1)

            def expert(t):
                return act.value_load(expert_i[0:1, bass.ds(t, 1)], min_val=0, max_val=E - 1)

            def gate_weights_high(t, p, e):
                if not (isinstance(t, int) and t < 2):
                    act.wait_ge(S["gate_done"], t - 1)
                act.activation(w_gate[0][0:CH, p], gate_or_up_e(e, 0), ACT.Copy).then_inc(S["w_gate_high"], 1)

            def up_weights_high(t, e):
                if not (isinstance(t, int) and t < 1):
                    act.wait_ge(S["up_done"], t)
                act.activation(w_up[0][0:CH], gate_or_up_e(e, 1), ACT.Copy).then_inc(S["w_up_high"], 1)

            def gate(t, p):
                act.wait_ge(S["gate_done"], t + 1)
                if not (isinstance(t, int) and t < 2):
                    act.wait_ge(S["hidden_ready"], t - 1)
                act.activation(silu[:, p, :], bank[p][:, 0:FF], ACT.Silu).then_inc(S["silu_ready"], 1)

            def hidden_columns(t):
                act.wait_ge(S["hT_done"], t + 1)
                if not (isinstance(t, int) and t < 1):
                    act.wait_ge(S["down_done"], t)
                act.activation(hiddenT, bank[4][:, 0:FF], ACT.Copy).then_inc(S["hT_ready"], 1)

            def step(t, p):
                ahead = not (isinstance(t, int) and t + 2 >= TILES)
                if ahead:
                    e = expert(t + 2)
                    gate_weights_high(t + 2, p, e)
                if not (isinstance(t, int) and t + 1 >= TILES):
                    gate(t + 1, 1 - p)
                hidden_columns(t)
                if ahead:
                    columns_high(t + 2, p)
                    up_weights_high(t + 2, e)

            act.wait_ge(S["ld_experts"], 16 * (2 * (E - LATE) + E))
            act.wait_ge(S["ld_late"], 16 * 2 * LATE)
            act.wait_ge(S["expert_ready"], 1)
            e0, e1 = expert(0), expert(1)
            gate_weights_high(0, 0, e0)
            up_weights_high(0, e0)
            shared_silu(FC)
            columns_high(0, 0)
            gate_weights_high(1, 1, e1)
            columns_high(1, 1)
            gate(0, 0)
            up_weights_high(1, e1)
            step(0, 0)
            step(1, 1)
            act.wait_ge(S["expert_ready"], 2)
            loop_pairs(act, lambda t, p, half: step(t, p))
            act.activation(ended_act, eps_col, ACT.Copy).then_inc(S["loop_act"], 1)
            for u in range(FC + 1, 2 * FC):
                shared_silu(u)
            for b in range(B):
                act.wait_ge(S["outT_done"], b + 1)
                act.activation(out_T[0:CH, b, :, :], bank[b][0:CH, :].rearrange("p (k n) -> p k n", k=2), ACT.Copy).then_inc(S["outT_ready"], 1)

        @block.vector
        def _(dve):
            vec = nc.vector
            vec.memset(eps_col, EPS).then_inc(S["eps_set"], 1)
            for b in range(B):
                dve.wait_ge(S["spec_done"], 2 * b + 2)
                vec.tensor_copy(spec[:, 2:4, b * MODES:(b + 1) * MODES],
                                bank[2 * b + 1][:, 0:2 * MODES].rearrange("p (q m) -> p q m", q=2)).then_inc(S["spec_dve"], 1)
                if b == 1:
                    for w, loaded, count in ((w1, "ld_w1", 10), (w2, "ld_w2", 9)):
                        dve.wait_ge(S[loaded], 16 * count)
                        vec.tensor_scalar(w[IM:, :, 0, :], w[IM:, :, 0, :], -1.0, None, ALU.mult).then_inc(S["negated"], 1)
            dve.wait_ge(S["ld_qkv"], 8 * 16)
            for cols, scale in ((slice(0, 256), SCALE), (slice(256, WQ), 1.0)):
                vec.tensor_scalar(wqkv[0][:, :, cols], wqkv_raw[:, :, cols], scale, None, ALU.mult).then_inc(S["w_split"], 1)
            dve.wait_ge(S["w_split"], 2)
            for cols, scale in ((slice(0, 256), SCALE), (slice(256, WQ), 1.0)):
                vec.scalar_tensor_tensor(wqkv[1][:, :, cols], wqkv_raw[:, :, cols], scale, wqkv[0][:, :, cols].bitcast(F32),
                                         ALU.mult, ALU.subtract).then_inc(S["w_split"], 1)
            for u, (v, dst) in enumerate(spectrum_units()):
                dve.wait_ge(S["y_done"], u + 1)
                c = clipped[0:v.shape[0], u % 2]
                vec.tensor_scalar(c, v, LAMBDA, -LAMBDA, ALU.min, ALU.max).then_inc(S["y_clipped"], 1)
                dve.wait_ge(S["y_clipped"], u + 1)
                vec.tensor_tensor(dst, v, c, ALU.subtract).then_inc(S["y_ready"], 1)
            dve.wait_ge(S["ld_res"], 16)

            def add_input(z):
                pair, jj = z // 2, z % 2
                dve.wait_ge(S["img_done"], z + 1)
                vec.tensor_tensor(img[:, pair, 384 * jj:384 * jj + 384], bank[4 + z][:, 0:384],
                                  x_res[:, pair, 384 * jj:384 * jj + 384], ALU.add).then_inc(S["img_ready"], 1)

            def statistics(tiles, sem_stats, sem_mv, ready):
                for t in tiles:
                    ready(t)
                    vec.bn_stats(stats[:, t, :], tok[:, t, :]).then_inc(S[sem_stats], 1)
                for t in tiles:
                    dve.wait_ge(S[sem_stats], t + 1)
                    vec.bn_aggr(meanvar[:, t, :], stats[:, t, :]).then_inc(S[sem_mv], 1)

            def normal(tiles, dst, part, sem_std, sem_rstd, sem_out):
                dve.wait_ge(S[sem_std], part + 1)
                vec.reciprocal(rstd[:, tiles.start:tiles.stop], std[:, tiles.start:tiles.stop]).then_inc(S[sem_rstd], 1)
                dve.wait_ge(S[sem_rstd], part + 1)
                for t in tiles:
                    vec.tensor_scalar(dst[:, t, :], tok[:, t, :], meanvar[:, t, 0:1], rstd[:, t:t + 1],
                                      ALU.subtract, ALU.mult).then_inc(S[sem_out], 1)

            def xT_low(b):
                dve.wait_ge(S["xT_high"], b + 1)
                vec.tensor_tensor(xT[1][0:CH, b, :, :], bank[4 + b][0:CH, :].rearrange("p (k n) -> p k n", k=2),
                                  xT[0][0:CH, b, :, :].bitcast(F32), ALU.subtract).then_inc(S["xT_low"], 1)

            def low_parts(b):
                dve.wait_ge(S["k_high"], b + 1)
                if b >= 1:
                    dve.wait_ge(S["k_masked_pool"], 3 * b)
                vec.tensor_tensor(k_all[1], bank[1][:, :].rearrange("p (t n) -> p t n", t=2), k_all[0].bitcast(F32), ALU.subtract).then_inc(S["k_low"], 1)
                if b >= 2:
                    dve.wait_ge(S["st_done"], 12 * (b - 1))
                one_head_keys(vec, b, 0, 1).then_inc(S["k_masked_dve"], 1)
                dve.wait_ge(S["q_high"], b + 1)
                vec.tensor_tensor(q_sb[1][:, b % 2], bank[0][:, :].rearrange("p (t n) -> p t n", t=2), q_sb[0][:, b % 2].bitcast(F32),
                                  ALU.subtract).then_inc(S["q_low"], 1)

            def maxima(b, units):
                for u in units:
                    n, qh, g6 = 12 * b + u, u // 6, u % 6
                    if b >= 1 and u == 0:
                        dve.wait_ge(S["rT_done"], b)
                    dve.wait_ge(S["smax_done"], n + 1)
                    col = CH + 2 * g6 % HPT
                    vec.tensor_reduce(negmax[:, g6 // 3, qh, col:col + 2], max_bank(n).rearrange("p (h n) -> p h n", h=2),
                                      AX.X, ALU.max, negate=True).then_inc(S["smax_ready"], 1)

            def maxima_to_queries(b):
                dve.wait_ge(S["rT_done"], b + 1)
                dve.wait_ge(S["q_high"], b + 1)
                vec.tensor_copy(q_sb[0][CH:CH + HPT, b % 2], bank[5][CH:CH + HPT, :].rearrange("p (t n) -> p t n", t=2)).then_inc(S["qmax_ready"], 1)

            def normalise(quad):
                b, j, s = quad // 3, quad % 3, quad % 2
                dve.wait_ge(S["pv_done"], quad + 1)
                vec.reciprocal(recip[:, s], bank[6 + s][:, 0:N]).then_inc(S["recip_ready"], 1)
                dve.wait_ge(S["recip_ready"], quad + 1)
                vec.stream_shuffle(den[:, s], recip[:, s], [HD + i % HD for i in range(32)]).then_inc(S["den_ready"], 1)
                dve.wait_ge(S["den_ready"], quad + 1)
                if b >= 2 and j == 0:
                    dve.wait_ge(S["proj_done"], b - 1)
                vec.tensor_tensor(o_sb[:, b % 2, j], bank[6 + s][:, 0:N], den[:, s], ALU.mult).then_inc(S["norm_ready"], 1)

            def add_attention(b):
                dve.wait_ge(S["proj_done"], b + 1)
                if b == 0:
                    dve.wait_ge(S["tok_b_ready"], 1)
                vec.tensor_tensor(tok[:, 2 * b:2 * b + 2, :], tok_b[:, 2 * b:2 * b + 2, :],
                                  bank[5][:, 0:2 * C].rearrange("p (h c) -> p h c", h=2), ALU.add).then_inc(S["attn_ready"], 1)

            for z in range(3):
                add_input(z)
            for half in range(2):
                statistics(HALVES[half], "stats_ready", "mv_ready", lambda t: dve.wait_ge(S["tok_ready"], 2 * (t // 4) + t % 2 + 1))
                normal(HALVES[half], xhat, half, "std_ready", "rstd_ready", "xhat_ready")
                if half == 0:
                    add_input(3)
                    for b in range(2):
                        xT_low(b)
            low_parts(0)
            for b in range(2, B):
                xT_low(b)
            maxima(0, range(12))
            for b in range(B):
                maxima_to_queries(b)
                if b:
                    normalise(3 * b - 1)
                if b + 1 < B:
                    low_parts(b + 1)
                for u in range(12):
                    maxima(b + 1, max_units(b, u))
                    if b and u == 2:
                        add_attention(b - 1)
                        if b == B - 1:
                            statistics(NORM_PARTS[0], "stats2", "mv2", lambda t: dve.wait_ge(S["attn_ready"], t // 2 + 1))
                    if u == 11 and b == B - 1:
                        normal(NORM_PARTS[0], xhat2, 0, "std2", "rstd2", "xhat2_ready")
                    if u in (8, 11):
                        normalise(3 * b + (u == 11))
            normalise(3 * B - 1)
            add_attention(B - 1)
            statistics(NORM_PARTS[1], "stats2", "mv2", lambda t: dve.wait_ge(S["attn_ready"], t // 2 + 1))
            normal(NORM_PARTS[1], xhat2, 1, "std2", "rstd2", "xhat2_ready")

            def shared_hidden(u):
                dve.wait_ge(S["silu_s_ready"], u + 1)
                dve.wait_ge(S["su_done"], u + 1)
                if u == FC:
                    dve.wait_ge(S["shared_done"], 2)
                vec.tensor_tensor(hid_s[:, u % FC, :], silu_s[u % 2], bank[shared_banks(u)[1]][:, :], ALU.mult).then_inc(S["hid_s_ready"], 1)

            def shared_rows(u):
                dve.wait_ge(S["shared_done"], u + 1)
                vec.tensor_tensor(tok_b[:, 2 * u:2 * u + 2, :], tok[:, 2 * u:2 * u + 2, :],
                                  bank[7 - u % 2][:, 0:2 * C].rearrange("p (h c) -> p h c", h=2), ALU.add).then_inc(S["shared_ready"], 1)

            steps = [0]

            def step(instruction):
                steps[0] += 1
                instruction.then_inc(S["route"], 1)
                dve.wait_ge(S["route"], steps[0])

            def per_tile(x, n=E):
                return x.unsqueeze(2).broadcast_to([128, NT, n])

            def put(instruction):
                steps[0] += 1
                instruction.then_inc(S["route"], 1)

            dve.wait_ge(S["logits_done"], 2)
            lg = bank[4][:, 0:NT * E].rearrange("p (t e) -> p t e", t=NT)
            step(vec.tensor_reduce(small[:, 0, :], lg, AX.X, ALU.max))
            step(vec.tensor_tensor(logit, lg, per_tile(small[:, 0, :]), ALU.subtract))
            dve.wait_ge(S["exp_logit_ready"], 1)
            step(vec.reduce_sum(small[:, 1, :], prob, AX.X))
            step(vec.reciprocal(small[:, 2, :], small[:, 1, :]))
            step(vec.tensor_tensor(prob, prob, per_tile(small[:, 2, :]), ALU.mult))
            for t in range(NT):
                put(vec.max(top[:, t, :], prob[:, t, :]))
            for t in range(NT):
                dve.wait_ge(S["route"], steps[0] - NT + 1)
                put(vec.max_index(top_i[:, t, :], top[:, t, :], prob[:, t, :]))
            dve.wait_ge(S["route"], steps[0])
            step(vec.tensor_copy(top_f, top_i[:, :, 0:TOPK]))
            step(vec.tensor_tensor(chosen, iota[:, 0:E].unsqueeze(1).unsqueeze(1).broadcast_to([128, NT, TOPK, E]),
                                   top_f.unsqueeze(3).broadcast_to([128, NT, TOPK, E]), ALU.is_equal))
            step(vec.tensor_tensor(member, chosen[:, :, 0, :], chosen[:, :, 1, :], ALU.add))
            assert steps[0] == MEMBER_STEP
            step(vec.reduce_sum(small[:, 1, :], top[:, :, 0:TOPK], AX.X))
            step(vec.reciprocal(small[:, 2, :], small[:, 1, :]))
            put(vec.tensor_tensor(weight, top[:, :, 0:TOPK], per_tile(small[:, 2, :], TOPK), ALU.mult))
            shared_hidden(0)
            dve.wait_ge(S["count_done"], 1)
            step(vec.tensor_scalar(count_i[0:E, :], bank[4][0:E, 256:384], float(TILE - 1), None, ALU.add))
            step(vec.tensor_scalar(padded_i[0:E, :], count_i[0:E, :], -TILE, None, ALU.bitwise_and))
            vec.tensor_copy(padded[0:E, :], padded_i[0:E, :]).then_inc(S["padded_ready"], 1)
            dve.wait_ge(S["base_done"], 1)
            step(vec.tensor_tensor(at_slot, chosen, bank[5][:, 0:NT * E].rearrange("p (t e) -> p t e", t=NT)
                                   .unsqueeze(2).broadcast_to([128, NT, TOPK, E]), ALU.mult))
            step(vec.reduce_sum(slot_f.rearrange("p (t k) -> p t k", t=NT), at_slot, AX.X))
            step(vec.tensor_copy(slot_i, slot_f))
            step(vec.tensor_scalar(part_i, slot_i, TILE - 1, None, ALU.bitwise_and))
            step(vec.tensor_scalar(tile_i, slot_i, 7, None, ALU.logical_shift_right))
            step(vec.tensor_copy(part_f, part_i))
            step(vec.tensor_copy(tile_f, tile_i))
            dve.wait_ge(S["end_done"], 1)
            vec.tensor_tensor(ended[0:E, :], bank[4][0:E, 384:416], tile_start, ALU.is_le).then_inc(S["ended_ready"], 1)
            pairs = NT * TOPK
            vec.tensor_tensor(is_tile, iota[:, 0:32].unsqueeze(1).broadcast_to([128, pairs, 32]),
                              tile_f.unsqueeze(2).broadcast_to([128, pairs, 32]), ALU.is_equal).then_inc(S["is_tile_ready"], 1)
            vec.tensor_tensor(is_part, iota.unsqueeze(1).broadcast_to([128, pairs, 128]),
                              part_f.unsqueeze(2).broadcast_to([128, pairs, 128]), ALU.is_equal).then_inc(S["is_part_ready"], 1)
            shared_hidden(1)
            dve.wait_ge(S["inv_done"], 1)
            numbers = bank[5][:, 128:160]
            vec.tensor_scalar(pair_i, numbers, 1.0, -1.0, ALU.max, ALU.add).then_inc(S["pair_ready"], 1)
            dve.wait_ge(S["pair_ready"], 1)
            vec.tensor_scalar(slot_token, pair_i, 1, None, ALU.logical_shift_right).then_inc(S["slot_token_ready"], 1)
            vec.tensor_scalar(expert_i[0:1, :], bank[4][0:1, 448:480], float(E - 1), None, ALU.min).then_inc(S["expert_ready"], 1)
            shared_hidden(2)
            vec.tensor_scalar(spare, numbers, 0.0, spare_row, ALU.is_equal, ALU.mult).then_inc(S["pair_ready"], 1)
            dve.wait_ge(S["pair_ready"], 2)
            vec.scalar_tensor_tensor(slot_pair, numbers, -1.0, spare, ALU.add, ALU.add).then_inc(S["slot_pair_ready"], 1)
            vec.tensor_scalar(tile_used[0:1, 0:32], bank[4][0:1, 448:480], float(E), None, ALU.is_lt).then_inc(S["used_ready"], 1)
            dve.wait_ge(S["used_ready"], 1)
            vec.reduce_sum(tile_used[0:1, 0:1], tile_used[0:1, 0:32], AX.X).then_inc(S["used_ready"], 1)
            dve.wait_ge(S["used_ready"], 2)
            vec.tensor_copy(used_i[0:1, 0:1], tile_used[0:1, 0:1]).then_inc(S["expert_ready"], 1)

            def hidden_rows(t, p):
                dve.wait_ge(S["silu_ready"], t + 1)
                dve.wait_ge(S["up_done"], t + 1)
                if not (isinstance(t, int) and t < 2):
                    dve.wait_ge(S["hT_done"], t - 1)
                vec.tensor_tensor(hidden[:, p, :], silu[:, p, :], bank[2 + p][:, 0:FF], ALU.mult).then_inc(S["hidden_ready"], 1)

            def down_rows(t, p, half):
                dve.wait_ge(S["down_done"], t + 1)
                if not (isinstance(t, int) and t < 2):
                    dve.wait_ge(y_stored[p], 16 * half)
                vec.tensor_copy(y_out[:, p, :], bank[6][:, 0:C]).then_inc(S["y_out_ready"], 1)

            def expert(t):
                return dve.value_load(expert_i[0:1, bass.ds(t, 1)], min_val=0, max_val=E - 1)

            def gate_weights_low(t, p, e):
                dve.wait_ge(S["w_gate_high"], t + 1)
                vec.tensor_tensor(w_gate[1][0:CH, p], gate_or_up_e(e, 0), w_gate[0][0:CH, p].bitcast(F32), ALU.subtract).then_inc(S["w_gate_low"], 1)

            def up_weights_low(t, e):
                dve.wait_ge(S["w_up_high"], t + 1)
                vec.tensor_tensor(w_up[1][0:CH], gate_or_up_e(e, 1), w_up[0][0:CH].bitcast(F32), ALU.subtract).then_inc(S["w_up_low"], 1)

            def columns_low(t, p):
                dve.wait_ge(S["xgT_high"], t + 1)
                vec.tensor_tensor(xgT[1][0:CH, p], bank[5][0:CH, 0:256].rearrange("p (k n) -> p k n", k=2),
                                  xgT[0][0:CH, p].bitcast(F32), ALU.subtract).then_inc(S["xgT_low"], 1)

            def expert_step(t, p, half):
                ahead = not (isinstance(t, int) and t + 2 >= TILES)
                if ahead:
                    e = expert(t + 2)
                    gate_weights_low(t + 2, p, e)
                    columns_low(t + 2, p)
                if not (isinstance(t, int) and t + 1 >= TILES):
                    hidden_rows(t + 1, 1 - p)
                if ahead:
                    up_weights_low(t + 2, e)
                down_rows(t, p, half)

            dve.wait_ge(S["expert_ready"], 1)
            dve.wait_ge(S["ld_experts"], 16 * (2 * (E - LATE) + E))
            dve.wait_ge(S["ld_late"], 16 * 2 * LATE)
            e0, e1 = expert(0), expert(1)
            gate_weights_low(0, 0, e0)
            up_weights_low(0, e0)
            shared_rows(0)
            columns_low(0, 0)
            gate_weights_low(1, 1, e1)
            shared_rows(1)
            shared_hidden(FC)
            columns_low(1, 1)
            hidden_rows(0, 0)
            up_weights_low(1, e1)
            expert_step(0, 0, 0)
            expert_step(1, 1, 0)
            dve.wait_ge(S["expert_ready"], 2)
            loop_pairs(dve, expert_step)
            vec.memset(ended_dve, 0.0).then_inc(S["loop_dve"], 1)

            def mix(t):
                a, b = (tok, tok_b) if t < NT // 2 else (tok_b, tok)
                dve.wait_ge(back[t], 16)
                vec.scalar_tensor_tensor(a[:, t, :], y_back[:, t, 0, :], weight[:, t, 0:1], b[:, t, :], ALU.mult, ALU.add).then_inc(S["half_mixed"], 1)
                dve.wait_ge(S["half_mixed"], t + 1)
                vec.scalar_tensor_tensor(b[:, t, :], y_back[:, t, 1, :], weight[:, t, 1:2], a[:, t, :], ALU.mult, ALU.add).then_inc(S["mixed"], 1)

            dve.wait_ge(S["shared_ready"], 2)
            for u in range(FC + 1, 2 * FC):
                shared_hidden(u)
            for t in range(NT // 2):
                mix(t)
            for u in range(NT // 4, NT // 2):
                mix(2 * u)
                mix(2 * u + 1)
                dve.wait_ge(S["mixed"], 2 * u + 2)
                shared_rows(u)

        @block.tensor
        def _(pe):
            mm, tr = nc.tensor.matmul, nc.tensor.transpose
            pe.wait_ge(S["ld_fwd"], 16)
            pe.wait_ge(S["zeroed"], 4)
            for u in range(2 * B):
                b = u // 2
                if u % 2 == 0:
                    pe.wait_ge(ld_pix[b], 16)
                for q in range(2):
                    for k in range(2):
                        col = k * C + (2 * (u % 2) + q) * GC
                        for r in range(2):
                            last = mm(bank[u][IM * r:IM * r + IM, q * MODES:(q + 1) * MODES], pix[:, b, col:col + IM],
                                      fwd[:, k, r * MODES:(r + 1) * MODES], start=(k == 0), stop=(k == 1))
                last.then_inc(S["spec_done"], 1)
            pe.wait_ge(S["negated"], 1)
            for v in range(2 * GROUPS):
                bp, q = v // GROUPS, v % GROUPS
                pe.wait_ge(S["spec_act"], 2 * (bp + 1))
                pe.wait_ge(S["spec_dve"], 2 * (bp + 1))
                if v >= 4:
                    pe.wait_ge(S["hid_ready"], v - 3)
                else:
                    pe.wait_ge(S["spec_dve" if v % 2 else "spec_act"], B // 2 + v // 2 + 1)
                mm(bank[4 + v % 4][:, 0:2 * MODES], w1[:, q, :, :], spec[:, q, bp * 2 * MODES:(bp + 1) * 2 * MODES],
                   start=True, stop=True).then_inc(S["hid_done"], 1)
            pe.wait_ge(S["negated"], 2)
            pe.wait_ge(S["spec_act"], B)
            pe.wait_ge(S["spec_dve"], B)
            for u, (dst, _) in enumerate(spectrum_units()):
                pair, k = u // 3, u % 3
                pe.wait_ge(S["hid_ready"], GROUPS * (pair + 1))
                if u >= 4:
                    pe.wait_ge(S["y_ready"], u - 3)
                for q in range(GROUPS):
                    if k < 2:
                        m = (2 * pair + k) * MODES
                        last = mm(dst[:, 2 * q * GC:2 * (q + 1) * GC], hid[:, q, m:m + MA], w2[:, q, :, :], start=True, stop=True)
                    else:
                        for bb in range(2):
                            m = (2 * pair + bb) * MODES + MA
                            for r in range(2):
                                last = mm(dst[IM * r:IM * r + MB, bb * C + q * GC:bb * C + (q + 1) * GC], hid[:, q, m:m + MB],
                                          w2[:, q, r, :], start=True, stop=True)
                last.then_inc(S["y_done"], 1)
            pe.wait_ge(S["ld_const"], 2 * 16)
            def inverse(z):
                pair, jj = z // 2, z % 2
                pe.wait_ge(S["y_ready"], 3 * (pair + 1))
                if z == 0:
                    pe.wait_ge(S["hid_ready"], 8)
                for j in range(2):
                    for k in range(3):
                        for bb in range(2):
                            b, rows = 2 * pair + bb, slice(0, 128 if k == 1 else MA)
                            y = y_high[:, b, :] if k == 1 else y_low[0:MA, b, :, k // 2, :]
                            last = mm(bank[4 + z][64 * bb:64 * bb + 64, j * C:(j + 1) * C], inv[rows, k, (2 * jj + j) * 64:(2 * jj + j) * 64 + 64],
                                      y, start=(k == 0), stop=(k == 2))
                last.then_inc(S["img_done"], 1)
            def token_major(s):
                pair, h = s // 2, s % 2
                pe.wait_ge(S["img_ready"], 2 * (pair + 1))
                if s == 0:
                    pe.wait_ge(S["y_ready"], 6)
                for i in range(3):
                    last = tr(bank[s][:, 128 * i:128 * i + 128], img[:, pair, 256 * i + 128 * h:256 * i + 128 * h + 128], ident)
                last.then_inc(S["tok_done"], 1)

            def xhat_T(b):
                if b == 2:
                    pe.wait_ge(S["img_ready"], 4)
                pe.wait_ge(S["xhat_ready"], 2 * b + 2)
                for k in range(2):
                    for h in range(2):
                        last = tr(bank[4 + b][0:CH, 256 * k + 128 * h:256 * k + 128 * h + 128], xhat[:, 2 * b + h, k * CH:(k + 1) * CH], ident)
                last.then_inc(S["xT_done"], 1)

            def mm3(dst, w, x, first=True, last=True):
                mm(dst, w(0), x(0), start=first, stop=False)
                mm(dst, w(0), x(1), start=False, stop=False)
                return mm(dst, w(1), x(0), start=False, stop=last)

            def project_qk(b, parts=range(4)):
                if 0 in parts:
                    pe.wait_ge(S["xT_low"], b + 1)
                if 0 in parts and b == 0:
                    pe.wait_ge(S["tok_ready"], 4)
                    pe.wait_ge(S["bias_zeroed"], BIAS_SET)
                    pe.wait_ge(S["w_split"], 4)
                elif 0 in parts and b == 1:
                    pe.wait_ge(S["q_low"], 1)
                elif 0 in parts:
                    pe.wait_ge(S["smax_ready"], 12 * b)
                for part in parts:
                    m, t = 1 - part // 2, part % 2
                    for k in range(2):
                        last = mm3(bank[m][:, t * N:(t + 1) * N], lambda i: wqkv[i][:, k, m * 256 + t * 128:m * 256 + t * 128 + 128],
                                   lambda i: xT[i][:, b, k, :], k == 0, k == 1)
                if part == 3:
                    last.then_inc(S["qk_done"], 1)

            def project_v(b):
                if b == 0:
                    pe.wait_ge(S["xT_low"], 2)
                elif b == 1:
                    pe.wait_ge(S["v_ready"], 1)
                else:
                    pe.wait_ge(S["qmax_ready"], b)
                for h in range(2):
                    for k in range(2):
                        last = mm3(bank[5][:, h * C:(h + 1) * C], lambda i: xT[i][:, b, k, 128 * h:128 * h + 128],
                                   lambda i: wqkv[i][:, k, 512:WQ], k == 0, k == 1)
                last.then_inc(S["v_done"], 1)

            def scores_for_max(b, units):
                for u in units:
                    n, qh, g6 = 12 * b + u, u // 6, u % 6
                    if u == 0:
                        pe.wait_ge(S["q_high"], b + 1)
                        if b:
                            pe.wait_ge(S["q_low"], b + 1)
                        pe.wait_ge(S["k_masked_pool"], 3 * b + 1)
                    if u == 3:
                        pe.wait_ge(S["k_masked_dve"], b + 1)
                    if b or u >= 3:
                        pe.wait_ge(S["smax_ready"], n - (1 if b else 2))
                    t, h = g6 // 3, 2 * g6 % HPT
                    last = mm(max_bank(n), q_sb[0][:, b % 2, t, 128 * qh:128 * qh + 128],
                              k_sb[0][:, b % 2, t, h:h + 2, :], start=True, stop=True)
                    last.then_inc(S["smax_done"], 1)

            def maxima_rows(b):
                pe.wait_ge(S["smax_ready"], 12 * b + 12)
                if b == 0:
                    pe.wait_ge(S["v_ready"], 2)
                elif b == 1:
                    pe.wait_ge(S["qmax_ready"], 1)
                else:
                    pe.wait_ge(S["attn_ready"], b - 1)
                for t in range(2):
                    for qh in range(2):
                        last = tr(bank[5][0:CH + HPT, t * N + 128 * qh:t * N + 128 * qh + 128], negmax[:, t, qh, :], ident)
                last.then_inc(S["rT_done"], 1)

            def scores(b, u):
                n, kh, g6 = 12 * b + u, u // 2 % 2, 2 * (u // 4) + u % 2
                if u == 0:
                    pe.wait_ge(S["k_masked_pool"], 3 * b + 3)
                    pe.wait_ge(S["q_low"], b + 1)
                if n >= 3:
                    pe.wait_ge(S["exp_ready"], n - 2)
                if n == 0:
                    pe.wait_ge(S["xT_low"], B)
                for v in range(2):
                    t, h = g6 // 3, (2 * g6 + v) % HPT
                    last = mm3(bank[2 + n % 3][:, v * N:(v + 1) * N], lambda i: k_sb[i][:, b % 2, t, h, 128 * kh:128 * kh + 128],
                               lambda i: q_sb[i][:, b % 2, t, :])
                last.then_inc(S["st_done"], 1)

            def attend(quad):
                b, j, s = quad // 3, quad % 3, quad % 2
                pe.wait_ge(S["exp_ready"], 4 * quad + 4)
                if quad >= 2:
                    pe.wait_ge(S["norm_ready"], quad - 1)
                for kh in range(2):
                    for h in range(4):
                        last = mm(bank[6 + s][32 * h:32 * h + 32, 0:N], v_sb[:, b % 2, kh, 4 * j + h, :], probs[:, s, kh, h, :],
                                  start=(kh == 0), stop=(kh == 1))
                last.then_inc(S["pv_done"], 1)

            def project_out(b):
                pe.wait_ge(S["norm_ready"], 3 * b + 3)
                if b + 2 < B:
                    pe.wait_ge(S["v_ready"], b + 3)
                else:
                    pe.wait_ge(S["qmax_ready"], B)
                if b == B - 1:
                    pe.wait_ge(S["attn_ready"], b)
                for h in range(2):
                    for j in range(3):
                        last = mm(bank[5][:, h * C:(h + 1) * C], o_sb[:, b % 2, j, 128 * h:128 * h + 128], wproj[:, j, :],
                                  start=(j == 0), stop=(j == 2))
                last.then_inc(S["proj_done"], 1)

            for z in range(3):
                inverse(z)
            for s in range(2):
                token_major(s)
            inverse(3)
            for b in range(2):
                xhat_T(b)
            for s in range(2, 4):
                token_major(s)
            project_qk(0)
            project_v(0)
            for b in range(2, B):
                xhat_T(b)
            scores_for_max(0, range(3))
            for part in range(4):
                project_qk(1, [part])
                scores_for_max(0, range(3 + 2 * part, 5 + 2 * part))
            project_v(1)
            scores_for_max(0, range(11, 12))
            for b in range(B):
                if b:
                    attend(3 * b - 1)
                maxima_rows(b)
                if 0 < b < B - 1:
                    project_qk(b + 1)
                    project_v(b + 1)
                pe.wait_ge(S["qmax_ready"], b + 1)
                for u in range(12):
                    if b and u == 2:
                        project_out(b - 1)
                    scores(b, u)
                    scores_for_max(b + 1, max_units(b, u))
                    if u in (7, 11):
                        attend(3 * b + u // 4 - 1)
            def shared_gate_up(u):
                half, f = u // FC, u % FC
                for m in range(2):
                    for b in range(2):
                        for k in range(2):
                            last = mm(bank[shared_banks(u)[m]][:, b * N:(b + 1) * N],
                                      shared_gu[:, k * 2 * FF + m * FF + 128 * f:k * 2 * FF + m * FF + 128 * f + 128],
                                      x2T[:, 2 * half + b, k, :], start=(k == 0), stop=(k == 1))
                    last.then_inc(S["su_done" if m else "sg_done"], 1)

            def shared_down(u):
                for h in range(2):
                    t = 2 * u + h
                    for f in range(FC):
                        last = mm(bank[7 - u % 2][:, h * C:(h + 1) * C], hid_s[:, f, 128 * (t % 4):128 * (t % 4) + 128],
                                  shared_dn[:, f * C:(f + 1) * C], start=(f == 0), stop=(f == FC - 1))
                last.then_inc(S["shared_done"], 1)

            def rank_and_count():
                pe.wait_ge(S["route"], MEMBER_STEP)
                rank = bank[5][:, 0:NT * E].rearrange("p (t e) -> p t e", t=NT)
                for t in range(NT):
                    last = mm(bank[4][0:E, 256:384], member[:, t, :], ones, start=(t == 0), stop=(t == NT - 1))
                last.then_inc(S["count_done"], 1)
                mm(rank, before, member, start=True, stop=False, skip_group_check=True)
                for t in range(NT - 1):
                    mm(rank[:, t + 1:, :], ones, member[:, t:t + 1, :].broadcast_to([128, NT - 1 - t, E]),
                       start=False, stop=False, skip_group_check=True)

            def base():
                pe.wait_ge(S["padded_ready"], 1)
                rank = bank[5][:, 0:NT * E].rearrange("p (t e) -> p t e", t=NT)
                mm(rank, padded[0:E, :], before[0:E, 0:E].unsqueeze(1).broadcast_to([E, NT, E]), start=False, stop=True,
                   skip_group_check=True).then_inc(S["base_done"], 1)
                mm(bank[4][0:E, 384:416], upto, padded[0:E, 0:32], start=True, stop=True).then_inc(S["end_done"], 1)

            def slot_tokens():
                pe.wait_ge(S["ended_ready"], 1)
                mm(bank[4][0:1, 448:480], ones[0:E, 0:1], ended[0:E, :], start=True, stop=True)
                pe.wait_ge(S["is_part_ready"], 1)
                pe.wait_ge(S["id_tile_ready"], 1)
                for s in range(NT * TOPK):
                    last = mm(bank[5][:, 128:160], is_part[:, s, :], id_tile[:, s, :], start=(s == 0), stop=(s == NT * TOPK - 1))
                last.then_inc(S["inv_done"], 1)

            def tokens_for_experts(b):
                pe.wait_ge(S["xhat2_ready"], 2 * b + 2)
                if b >= 2:
                    pe.wait_ge(S["x2T_ready"], 1 if b == 2 else 3)
                for k in range(2):
                    for h in range(2):
                        last = tr(x2T_bank(b)[0:CH, 256 * k + 128 * h:256 * k + 128 * h + 128], xhat2[:, 2 * b + h, k * CH:(k + 1) * CH], ident)
                last.then_inc(S["x2T_done"], 1)

            def gate_logits(tiles):
                for t in tiles:
                    for k in range(2):
                        last = mm(bank[4][:, t * E:(t + 1) * E], x2T[:, t // 2, k, 128 * (t % 2):128 * (t % 2) + 128],
                                  wgate[:, k, :], start=(k == 0), stop=(k == 1))
                last.then_inc(S["logits_done"], 1)

            pe.wait_ge(S["w_zeroed"], 5)
            pe.wait_ge(S["ld_shared"], 3 * 16)
            pe.wait_ge(S["ld_attn"], 8 * 16)
            attend(3 * B - 1)
            for b in range(B - 1):
                tokens_for_experts(b)
            pe.wait_ge(S["exp_ready"], 48)
            pe.wait_ge(S["x2T_ready"], 2)
            pe.wait_ge(S["bias_zeroed"], BIAS_SET + 2)
            shared_gate_up(0)
            project_out(B - 1)
            pe.wait_ge(S["x2T_ready"], B - 1)
            gate_logits(NORM_PARTS[0])
            tokens_for_experts(B - 1)
            pe.wait_ge(S["x2T_ready"], B)
            gate_logits(NORM_PARTS[1])
            shared_gate_up(1)
            pe.wait_ge(S["attn_ready"], B)
            rank_and_count()
            pe.wait_ge(S["norm_ready"], 12)
            base()
            shared_gate_up(2)
            slot_tokens()
            pe.wait_ge(S["hid_s_ready"], 1)
            shared_gate_up(FC)
            pe.wait_ge(S["hid_s_ready"], FC)
            shared_down(0)

            pe.wait_ge(S["ld_experts"], 16 * (2 * (E - LATE) + E))
            pe.wait_ge(S["ld_late"], 16 * 2 * LATE)
            pe.wait_ge(S["expert_ready"], 1)
            pe.wait_ge(S["slot_pair_ready"], 1)

            def tokens_T(t, p, half):
                pe.wait_ge(gathered[p], 16 * half + 16)
                if not (isinstance(t, int) and t < 1):
                    pe.wait_ge(S["xgT_low"], t)
                for k in range(2):
                    last = tr(bank[5][0:CH, 128 * k:128 * k + 128], xg[:, p, k * CH:(k + 1) * CH], ident)
                last.then_inc(S["xg_done"], 1)

            def gate_up(t, p, m):
                if m == 0:
                    pe.wait_ge(S["xgT_low"], t + 1)
                pe.wait_ge(S["w_up_low" if m else "w_gate_low"], t + 1)
                if not (isinstance(t, int) and t < 2):
                    pe.wait_ge(S["hidden_ready" if m else "silu_ready"], t - 1)
                w = (lambda i, k: w_up[i][0:CH, k]) if m else (lambda i, k: w_gate[i][0:CH, p, k])
                for k in range(2):
                    last = mm3(bank[2 * m + p][:, 0:FF], lambda i: xgT[i][0:CH, p, k, :], lambda i: w(i, k), k == 0, k == 1)
                last.then_inc(S["up_done" if m else "gate_done"], 1)

            def hidden_T(t, p):
                pe.wait_ge(S["hidden_ready"], t + 1)
                if not (isinstance(t, int) and t < 1):
                    pe.wait_ge(S["hT_ready"], t)
                for f in range(FC):
                    last = tr(bank[4][:, 128 * f:128 * f + 128], hidden[:, p, 128 * f:128 * f + 128], ident)
                last.then_inc(S["hT_done"], 1)

            def down(t, e):
                pe.wait_ge(S["hT_ready"], t + 1)
                if isinstance(t, int) and t < 1:
                    pe.wait_ge(S["shared_ready"], 2)
                else:
                    pe.wait_ge(S["y_out_ready"], t)
                for f in range(FC):
                    last = mm(bank[6][:, 0:C], hiddenT[:, 128 * f:128 * f + 128], down_all[:, bass.ds(e * DN + f * C, C)],
                              start=(f == 0), stop=(f == FC - 1))
                last.then_inc(S["down_done"], 1)

            def expert(t):
                return pe.value_load(expert_i[0:1, bass.ds(t, 1)], min_val=0, max_val=E - 1)

            def step(t, p, half):
                more = not (isinstance(t, int) and t + 1 >= TILES)
                if more:
                    gate_up(t + 1, 1 - p, 0)
                hidden_T(t, p)
                if not (isinstance(t, int) and t + 2 >= TILES):
                    tokens_T(t + 2, p, half + 1)
                if more:
                    gate_up(t + 1, 1 - p, 1)
                down(t, expert(t))

            tokens_T(0, 0, 0)
            shared_down(1)
            tokens_T(1, 1, 0)
            gate_up(0, 0, 0)
            gate_up(0, 0, 1)
            pe.wait_ge(S["hid_s_ready"], FC + 1)
            step(0, 0, 0)
            step(1, 1, 0)
            pe.wait_ge(S["expert_ready"], 2)
            loop_pairs(pe, step)

            shared_gate_up(FC + 1)
            pe.wait_ge(S["loop_act"], 1)
            pe.wait_ge(S["loop_dve"], 1)
            shared_gate_up(FC + 2)

            def out_columns(b):
                for k in range(2):
                    for h in range(2):
                        last = tr(bank[b][0:CH, 256 * k + 128 * h:256 * k + 128 * h + 128], tok_b[:, 2 * b + h, k * CH:(k + 1) * CH], ident)
                last.then_inc(S["outT_done"], 1)

            pe.wait_ge(S["hid_s_ready"], 2 * FC)
            for u in range(NT // 4, NT // 2):
                shared_down(u)
            for b in range(B // 2):
                pe.wait_ge(S["mixed"], 2 * b + 2)
                out_columns(b)
            for b in range(B // 2, B):
                pe.wait_ge(S["shared_ready"], b + 1)
                out_columns(b)


_NAMES = {"x": "x", "w1": "L0_conv_w1", "b1": "L0_conv_b1", "w2": "L0_conv_w2", "b2": "L0_conv_b2",
          "w_qkv": "L1_attn_w_qkv", "b_qkv": "L1_attn_b_qkv", "w_proj": "L1_attn_w_proj", "b_proj": "L1_attn_b_proj",
          "w_gate": "L1_ffn_w_gate", "expert_bias": "L1_ffn_expert_bias", "wg": "L1_ffn_wg", "wu": "L1_ffn_wu",
          "wd": "L1_ffn_wd", "swg": "L1_ffn_swg", "swu": "L1_ffn_swu", "swd": "L1_ffn_swd"}


def kernel(**inputs):
    import concourse.bacc as bacc
    from concourse.bass_utils import run_bass_kernel_spmd

    nc = bacc.Bacc("TRN2", target_bir_lowering=False, num_devices=1)
    tables = constants()
    arrays = {k: np.ascontiguousarray(inputs[v]) for k, v in _NAMES.items()}
    arrays.update(tables_f32=tables[0], tables_bf16=tables[1])
    aps = {k: nc.dram_tensor(k, v.shape, mybir.dt.from_np(v.dtype), kind="ExternalInput").ap() for k, v in arrays.items()}
    out = nc.dram_tensor("out", [B, C, H, W], F32, kind="ExternalOutput").ap()
    program(nc, aps, out)
    return run_bass_kernel_spmd(nc, [arrays], core_ids=[0]).results[0]["out"]
```
